# Optimizing a Trainium2 kernel written in Bass

```python
import numpy as np
import jax
import jax.numpy as jnp

def _softmax(x, axis=-1):
    return jax.nn.softmax(x, axis=axis)

def _gelu(x):
    return jax.nn.gelu(x, approximate=True)

def _silu(x):
    return jax.nn.silu(x)

def _sigmoid(x):
    return jax.nn.sigmoid(x)

def _layernorm(x, axis=-1, eps=1e-05):
    m = jnp.mean(x, axis=axis, keepdims=True)
    v = jnp.var(x, axis=axis, keepdims=True)
    return (x - m) / jnp.sqrt(v + eps)

def _scatter_add(tgt, idx, src, axis=0):
    return tgt.at[idx].add(src)

def _segment_sum(src, seg, n):
    return jax.ops.segment_sum(src, seg, n)
kernel_name = 'mk_lm_tower_d2_tok_ids256_r4_498b8c'

def setup_inputs(seed: int=0):
    np.random.seed(seed)
    _w = jnp.asarray

    def _rec_inputs():
        import jax
        import jax.numpy as jnp
        _rk = jax.random.key(seed)
        x = jax.random.randint(jax.random.fold_in(_rk, 1), (8, 256), 0, 2000, jnp.int32)
        return x
    x = _rec_inputs()

    def _L0_tok_setup():
        import jax, jax.numpy as jnp
        import numpy as np
        D_MODEL = 64
        N_HEADS = 8
        D_HEAD = D_MODEL // N_HEADS
        N_LAYERS = 4
        VOCAB = 2000
        MAX_LEN = 256
        LN_EPS = 0.001

        def _positional_encoding(length, depth):
            positions = np.arange(length).reshape(-1, 1)
            depths = np.array([2 * (i // 2) for i in range(depth)]).reshape(1, -1)
            angle_rates = 1.0 / 10000.0 ** (depths / depth)
            angles = positions * angle_rates
            enc = np.cos(angles)
            enc[:, ::2] = np.sin(enc[:, ::2])
            return jnp.asarray(enc, dtype=jnp.float32)
        _POS_ENC = _positional_encoding(MAX_LEN, D_MODEL)

        def _layernorm(x, g, b):
            mu = jnp.mean(x, axis=-1, keepdims=True)
            var = jnp.mean(jnp.square(x - mu), axis=-1, keepdims=True)
            return (x - mu) * jax.lax.rsqrt(var + LN_EPS) * g + b
        key = jax.random.key(seed)
        ks = jax.random.split(key, 8)
        s = 0.02
        return {'x': jax.random.randint(ks[0], (16, 256), 0, VOCAB, dtype=jnp.int64 if jax.config.read('jax_enable_x64') else jnp.int32), 'emb': jax.random.normal(ks[1], (VOCAB, D_MODEL), jnp.float32) * s, 'wq': jax.random.normal(ks[2], (N_LAYERS, N_HEADS, D_MODEL, D_HEAD), jnp.float32) * s, 'wk': jax.random.normal(ks[3], (N_LAYERS, N_HEADS, D_MODEL, D_HEAD), jnp.float32) * s, 'wv': jax.random.normal(ks[4], (N_LAYERS, N_HEADS, D_MODEL, D_HEAD), jnp.float32) * s, 'wo': jax.random.normal(ks[5], (N_LAYERS, D_MODEL, D_MODEL), jnp.float32) * s, 'bo': jnp.zeros((N_LAYERS, D_MODEL), jnp.float32), 'gamma': jnp.ones((N_LAYERS, D_MODEL), jnp.float32), 'beta': jnp.zeros((N_LAYERS, D_MODEL), jnp.float32), 'w1': jax.random.normal(ks[6], (N_LAYERS, D_MODEL, 4 * D_MODEL), jnp.float32) * s, 'b1': jnp.zeros((N_LAYERS, 4 * D_MODEL), jnp.float32), 'w2': jax.random.normal(ks[7], (N_LAYERS, 4 * D_MODEL, D_MODEL), jnp.float32) * s, 'b2': jnp.zeros((N_LAYERS, D_MODEL), jnp.float32)}
    _L0_tok_all = _L0_tok_setup()
    _L0_tok_in = {k: v for k, v in _L0_tok_all.items() if k in ('emb', 'wq', 'wk', 'wv', 'wo', 'bo', 'gamma', 'beta', 'w1', 'b1', 'w2', 'b2')}
    del _L0_tok_all

    def _L0_attn_setup():
        import jax, jax.numpy as jnp
        import numpy as np
        N_HEADS, EMB, KQ = (8, 64, 64)
        BATCH, SEQ = (4, 512)
        key = jax.random.key(seed)
        ks = jax.random.split(key, 5)
        x = jax.random.normal(ks[0], (BATCH, SEQ, EMB), dtype=jnp.float32)
        key_matrices = 0.1 * jax.random.normal(ks[1], (N_HEADS, EMB, KQ), dtype=jnp.float32)
        query_matrices = 0.1 * jax.random.normal(ks[2], (N_HEADS, EMB, KQ), dtype=jnp.float32)
        value_in_matrices = 0.1 * jax.random.normal(ks[3], (N_HEADS, EMB, KQ), dtype=jnp.float32)
        value_out_matrices = 0.1 * jax.random.normal(ks[4], (N_HEADS, KQ, EMB), dtype=jnp.float32)
        return {'x': x, 'key_matrices': key_matrices, 'query_matrices': query_matrices, 'value_in_matrices': value_in_matrices, 'value_out_matrices': value_out_matrices}
    _L0_attn_all = _L0_attn_setup()
    _L0_attn_in = {k: v for k, v in _L0_attn_all.items() if k in ('key_matrices', 'query_matrices', 'value_in_matrices', 'value_out_matrices')}
    del _L0_attn_all

    def _L0_ffn_setup():
        import jax, jax.numpy as jnp
        import numpy as np
        B, T, C = (64, 96, 64)
        NH, NKV = (4, 2)
        HD = C // NH
        NREP = NH // NKV
        NE, TOPK = (8, 2)
        HID = int(8 / 3 * C)
        EPS_RMS = 1e-06

        def _rope_tables(t_len):
            inv_freq = 1.0 / 10000.0 ** (np.arange(0, HD, 2, dtype=np.float32) / HD)
            t = np.arange(t_len, dtype=np.float32)
            freqs = np.outer(t, inv_freq)
            emb = np.concatenate([freqs, freqs], axis=-1)
            return (jnp.asarray(np.cos(emb)), jnp.asarray(np.sin(emb)))

        def _rotate_half(x):
            h = x.shape[-1] // 2
            return jnp.concatenate([-x[..., h:], x[..., :h]], axis=-1)

        def _rmsnorm(v, w):
            return v * jax.lax.rsqrt(jnp.mean(v * v, axis=-1, keepdims=True) + EPS_RMS) * w
        key = jax.random.key(seed)
        ks = jax.random.split(key, 10)
        s = lambda k, shape: jax.random.normal(k, shape, jnp.float32) * 0.02
        return {'x': jax.random.normal(ks[0], (B, T, C), jnp.float32), 'ln1_w': jnp.ones((C,), jnp.float32), 'ln2_w': jnp.ones((C,), jnp.float32), 'wq': s(ks[1], (NH * HD, C)), 'wk': s(ks[2], (NKV * HD, C)), 'wv': s(ks[3], (NKV * HD, C)), 'wo': s(ks[4], (C, C)), 'router_w': s(ks[5], (NE, C)), 'w1': s(ks[6], (NE, HID, C)), 'w2': s(ks[7], (NE, C, HID)), 'w3': s(ks[8], (NE, HID, C))}
    _L0_ffn_all = _L0_ffn_setup()
    _L0_ffn_in = {k: v for k, v in _L0_ffn_all.items() if k in ('ln1_w', 'ln2_w', 'wq', 'wk', 'wv', 'wo', 'router_w', 'w1', 'w2', 'w3')}
    del _L0_ffn_all

    def _L1_attn_setup():
        import jax, jax.numpy as jnp
        import numpy as np
        key = jax.random.key(seed)
        ks = jax.random.split(key, 4)
        B, S, D = (4, 1024, 64)
        x = jax.random.normal(ks[0], (B, S, D), dtype=jnp.float32)
        Wq = jax.random.normal(ks[1], (D, D), dtype=jnp.float32) * 0.02
        Wk = jax.random.normal(ks[2], (D, D), dtype=jnp.float32) * 0.02
        Wv = jax.random.normal(ks[3], (D, D), dtype=jnp.float32) * 0.02
        bq = jnp.zeros((D,), dtype=jnp.float32)
        bk = jnp.zeros((D,), dtype=jnp.float32)
        bv = jnp.zeros((D,), dtype=jnp.float32)
        return {'x': x, 'Wq': Wq, 'bq': bq, 'Wk': Wk, 'bk': bk, 'Wv': Wv, 'bv': bv}
    _L1_attn_all = _L1_attn_setup()
    _L1_attn_in = {k: v for k, v in _L1_attn_all.items() if k in ('Wq', 'bq', 'Wk', 'bk', 'Wv', 'bv')}
    del _L1_attn_all

    def _L1_ffn_setup():
        import jax, jax.numpy as jnp
        import numpy as np
        E = 8
        K = 2
        D = 64
        H = 128
        DOUT = 64
        EPS = 1e-05
        key = jax.random.key(seed)
        ks = jax.random.split(key, 9)
        s = 0.02
        return {'x': jax.random.normal(ks[0], (4, 2048, D), jnp.float32), 'gamma': 1.0 + 0.05 * jax.random.normal(ks[1], (D,), jnp.float32), 'beta': 0.05 * jax.random.normal(ks[2], (D,), jnp.float32), 'Wr': 0.01 * jax.random.normal(ks[3], (D, E), jnp.float32), 'br': jnp.zeros((E,), jnp.float32), 'W1': s * jax.random.normal(ks[4], (E, D, H), jnp.float32), 'b1': s * jax.random.normal(ks[5], (E, H), jnp.float32), 'W2': s * jax.random.normal(ks[6], (E, H, DOUT), jnp.float32), 'b2': s * jax.random.normal(ks[7], (E, DOUT), jnp.float32)}
    _L1_ffn_all = _L1_ffn_setup()
    _L1_ffn_in = {k: v for k, v in _L1_ffn_all.items() if k in ('gamma', 'beta', 'Wr', 'br', 'W1', 'b1', 'W2', 'b2')}
    del _L1_ffn_all
    return {'x': x, 'L0_tok_emb': _L0_tok_in['emb'], 'L0_tok_wq': _L0_tok_in['wq'], 'L0_tok_wk': _L0_tok_in['wk'], 'L0_tok_wv': _L0_tok_in['wv'], 'L0_tok_wo': _L0_tok_in['wo'], 'L0_tok_bo': _L0_tok_in['bo'], 'L0_tok_gamma': _L0_tok_in['gamma'], 'L0_tok_beta': _L0_tok_in['beta'], 'L0_tok_w1': _L0_tok_in['w1'], 'L0_tok_b1': _L0_tok_in['b1'], 'L0_tok_w2': _L0_tok_in['w2'], 'L0_tok_b2': _L0_tok_in['b2'], 'L0_attn_key_matrices': _L0_attn_in['key_matrices'], 'L0_attn_query_matrices': _L0_attn_in['query_matrices'], 'L0_attn_value_in_matrices': _L0_attn_in['value_in_matrices'], 'L0_attn_value_out_matrices': _L0_attn_in['value_out_matrices'], 'L0_ffn_ln1_w': _L0_ffn_in['ln1_w'], 'L0_ffn_ln2_w': _L0_ffn_in['ln2_w'], 'L0_ffn_wq': _L0_ffn_in['wq'], 'L0_ffn_wk': _L0_ffn_in['wk'], 'L0_ffn_wv': _L0_ffn_in['wv'], 'L0_ffn_wo': _L0_ffn_in['wo'], 'L0_ffn_router_w': _L0_ffn_in['router_w'], 'L0_ffn_w1': _L0_ffn_in['w1'], 'L0_ffn_w2': _L0_ffn_in['w2'], 'L0_ffn_w3': _L0_ffn_in['w3'], 'L1_attn_Wq': _L1_attn_in['Wq'], 'L1_attn_bq': _L1_attn_in['bq'], 'L1_attn_Wk': _L1_attn_in['Wk'], 'L1_attn_bk': _L1_attn_in['bk'], 'L1_attn_Wv': _L1_attn_in['Wv'], 'L1_attn_bv': _L1_attn_in['bv'], 'L1_ffn_gamma': _L1_ffn_in['gamma'], 'L1_ffn_beta': _L1_ffn_in['beta'], 'L1_ffn_Wr': _L1_ffn_in['Wr'], 'L1_ffn_br': _L1_ffn_in['br'], 'L1_ffn_W1': _L1_ffn_in['W1'], 'L1_ffn_b1': _L1_ffn_in['b1'], 'L1_ffn_W2': _L1_ffn_in['W2'], 'L1_ffn_b2': _L1_ffn_in['b2']}

def reference(x, L0_tok_emb, L0_tok_wq, L0_tok_wk, L0_tok_wv, L0_tok_wo, L0_tok_bo, L0_tok_gamma, L0_tok_beta, L0_tok_w1, L0_tok_b1, L0_tok_w2, L0_tok_b2, L0_attn_key_matrices, L0_attn_query_matrices, L0_attn_value_in_matrices, L0_attn_value_out_matrices, L0_ffn_ln1_w, L0_ffn_ln2_w, L0_ffn_wq, L0_ffn_wk, L0_ffn_wv, L0_ffn_wo, L0_ffn_router_w, L0_ffn_w1, L0_ffn_w2, L0_ffn_w3, L1_attn_Wq, L1_attn_bq, L1_attn_Wk, L1_attn_bk, L1_attn_Wv, L1_attn_bv, L1_ffn_gamma, L1_ffn_beta, L1_ffn_Wr, L1_ffn_br, L1_ffn_W1, L1_ffn_b1, L1_ffn_W2, L1_ffn_b2):
    import jax
    import jax.numpy as jnp

    def _L0_tok_ref(x, emb, wq, wk, wv, wo, bo, gamma, beta, w1, b1, w2, b2):
        import jax, jax.numpy as jnp
        import numpy as np
        D_MODEL = 64
        N_HEADS = 8
        D_HEAD = D_MODEL // N_HEADS
        N_LAYERS = 4
        VOCAB = 2000
        MAX_LEN = 256
        LN_EPS = 0.001

        def _positional_encoding(length, depth):
            positions = np.arange(length).reshape(-1, 1)
            depths = np.array([2 * (i // 2) for i in range(depth)]).reshape(1, -1)
            angle_rates = 1.0 / 10000.0 ** (depths / depth)
            angles = positions * angle_rates
            enc = np.cos(angles)
            enc[:, ::2] = np.sin(enc[:, ::2])
            return jnp.asarray(enc, dtype=jnp.float32)
        _POS_ENC = _positional_encoding(MAX_LEN, D_MODEL)

        def _layernorm(x, g, b):
            mu = jnp.mean(x, axis=-1, keepdims=True)
            var = jnp.mean(jnp.square(x - mu), axis=-1, keepdims=True)
            return (x - mu) * jax.lax.rsqrt(var + LN_EPS) * g + b
        B, L = x.shape
        h = emb[x] + _POS_ENC[:L][None, :, :]
        scale = 1.0 / jnp.sqrt(jnp.float32(D_HEAD))
        for l in range(N_LAYERS):
            q = jnp.einsum('bsd,hdk->bhsk', h, wq[l])
            k = jnp.einsum('bsd,hdk->bhsk', h, wk[l])
            v = jnp.einsum('bsd,hdk->bhsk', h, wv[l])
            scores = jnp.einsum('bhsk,bhtk->bhst', q, k) * scale
            w = jax.nn.softmax(scores, axis=-1)
            att = jnp.einsum('bhst,bhtk->bhsk', w, v)
            att = att.transpose(0, 2, 1, 3).reshape(B, L, D_MODEL)
            att = att @ wo[l] + bo[l]
            h = _layernorm(h + att, gamma[l], beta[l])
            ffn = jax.nn.relu(h @ w1[l] + b1[l]) @ w2[l] + b2[l]
            h = _layernorm(h + ffn, gamma[l], beta[l])
        return h

    def _L0_attn_ref(x, key_matrices, query_matrices, value_in_matrices, value_out_matrices):
        import jax, jax.numpy as jnp
        import numpy as np
        N_HEADS, EMB, KQ = (8, 64, 64)
        BATCH, SEQ = (4, 512)
        seq_len = x.shape[1]
        queries = jnp.einsum('ned,bse->nbsd', query_matrices, x)
        keys = jnp.einsum('ned,bse->nbsd', key_matrices, x)
        kq = jnp.einsum('nbjd,nbkd->nbjk', keys, queries)
        mask = jnp.triu(jnp.ones((seq_len, seq_len), dtype=bool), k=1)
        kq = jnp.where(mask, -jnp.inf, kq)
        attention_pattern = jax.nn.softmax(kq, axis=3)
        v = jnp.einsum('bjp,npd->nbjd', x, value_in_matrices)
        ctx = jnp.einsum('nbsj,nbjd->nbsd', attention_pattern, v)
        return jnp.einsum('nbsd,nde->bse', ctx, value_out_matrices)

    def _L0_ffn_ref(x, ln1_w, ln2_w, wq, wk, wv, wo, router_w, w1, w2, w3):
        import jax, jax.numpy as jnp
        import numpy as np
        B, T, C = (64, 96, 64)
        NH, NKV = (4, 2)
        HD = C // NH
        NREP = NH // NKV
        NE, TOPK = (8, 2)
        HID = int(8 / 3 * C)
        EPS_RMS = 1e-06

        def _rope_tables(t_len):
            inv_freq = 1.0 / 10000.0 ** (np.arange(0, HD, 2, dtype=np.float32) / HD)
            t = np.arange(t_len, dtype=np.float32)
            freqs = np.outer(t, inv_freq)
            emb = np.concatenate([freqs, freqs], axis=-1)
            return (jnp.asarray(np.cos(emb)), jnp.asarray(np.sin(emb)))

        def _rotate_half(x):
            h = x.shape[-1] // 2
            return jnp.concatenate([-x[..., h:], x[..., :h]], axis=-1)

        def _rmsnorm(v, w):
            return v * jax.lax.rsqrt(jnp.mean(v * v, axis=-1, keepdims=True) + EPS_RMS) * w
        Bx, Tx, Cx = x.shape
        h = _rmsnorm(x, ln1_w)
        q = (h @ wq.T).reshape(Bx, Tx, NH, HD).transpose(0, 2, 1, 3)
        k = (h @ wk.T).reshape(Bx, Tx, NKV, HD).transpose(0, 2, 1, 3)
        v = (h @ wv.T).reshape(Bx, Tx, NKV, HD).transpose(0, 2, 1, 3)
        cos, sin = _rope_tables(Tx)
        cos, sin = (cos[None, None], sin[None, None])
        q = q * cos + _rotate_half(q) * sin
        k = k * cos + _rotate_half(k) * sin
        k = jnp.repeat(k, NREP, axis=1)
        v = jnp.repeat(v, NREP, axis=1)
        scores = jnp.einsum('bhtd,bhsd->bhts', q, k) / jnp.sqrt(jnp.float32(HD))
        causal = jnp.tril(jnp.ones((Tx, Tx), dtype=bool))
        scores = jnp.where(causal[None, None], scores, jnp.float32(-1e+30))
        att = jax.nn.softmax(scores, axis=-1)
        y = jnp.einsum('bhts,bhsd->bhtd', att, v).transpose(0, 2, 1, 3).reshape(Bx, Tx, Cx)
        x = x + y @ wo.T
        flat = _rmsnorm(x, ln2_w).reshape(-1, Cx)
        probs = jax.nn.softmax(flat @ router_w.T, axis=-1)
        tp, ti = jax.lax.top_k(probs, TOPK)
        tp = tp / (jnp.sum(tp, axis=-1, keepdims=True) + 1e-09)
        weights = jnp.sum(tp[..., None] * jax.nn.one_hot(ti, NE, dtype=flat.dtype), axis=1)
        out = jnp.zeros_like(flat)
        for e in range(NE):
            hh = jax.nn.silu(flat @ w1[e].T) * (flat @ w3[e].T)
            out = out + weights[:, e:e + 1] * (hh @ w2[e].T)
        return x + out.reshape(Bx, Tx, Cx)

    def _L1_attn_ref(x, Wq, bq, Wk, bk, Wv, bv):
        import jax, jax.numpy as jnp
        import numpy as np
        Q = jnp.einsum('bsd,de->bse', x, Wq) + bq
        K = jnp.einsum('bsd,de,->bse'.replace(',->', '->'), x, Wk) + bk
        V = jnp.einsum('bsd,de->bse', x, Wv) + bv
        scale = 1.0 / jnp.sqrt(jnp.asarray(Q.shape[-1], dtype=jnp.float32))
        scores = jnp.einsum('bqd,bkd->bqk', Q, K) * scale
        weights = jax.nn.softmax(scores, axis=-1)
        return jnp.einsum('bqk,bkd->bqd', weights, V)

    def _L1_ffn_ref(x, gamma, beta, Wr, br, W1, b1, W2, b2):
        import jax, jax.numpy as jnp
        import numpy as np
        E = 8
        K = 2
        D = 64
        H = 128
        DOUT = 64
        EPS = 1e-05
        mu = jnp.mean(x, axis=-1, keepdims=True)
        var = jnp.mean(jnp.square(x - mu), axis=-1, keepdims=True)
        xn = (x - mu) * jax.lax.rsqrt(var + EPS) * gamma + beta
        logits = jnp.einsum('bsd,de->bse', xn, Wr) + br
        top_vals, top_idx = jax.lax.top_k(logits, K)
        w = jax.nn.softmax(top_vals, axis=-1)
        w_full = jnp.einsum('bsk,bske->bse', w, jax.nn.one_hot(top_idx, E, dtype=w.dtype))
        y = jnp.zeros(x.shape[:-1] + (DOUT,), x.dtype)
        for e in range(E):
            h = jax.nn.gelu(jnp.einsum('bsd,dh->bsh', xn, W1[e]) + b1[e], approximate=False)
            y_e = jnp.einsum('bsh,hd->bsd', h, W2[e]) + b2[e]
            y = y + y_e * w_full[..., e, None]
        return y
    h = _L0_tok_ref(x, L0_tok_emb, L0_tok_wq, L0_tok_wk, L0_tok_wv, L0_tok_wo, L0_tok_bo, L0_tok_gamma, L0_tok_beta, L0_tok_w1, L0_tok_b1, L0_tok_w2, L0_tok_b2)
    h = h + _L0_attn_ref(_layernorm(h, axis=-1), L0_attn_key_matrices, L0_attn_query_matrices, L0_attn_value_in_matrices, L0_attn_value_out_matrices)
    h = h + _L0_ffn_ref(_layernorm(h, axis=-1), L0_ffn_ln1_w, L0_ffn_ln2_w, L0_ffn_wq, L0_ffn_wk, L0_ffn_wv, L0_ffn_wo, L0_ffn_router_w, L0_ffn_w1, L0_ffn_w2, L0_ffn_w3)
    h = h + _L1_attn_ref(_layernorm(h, axis=-1), L1_attn_Wq, L1_attn_bq, L1_attn_Wk, L1_attn_bk, L1_attn_Wv, L1_attn_bv)
    h = h + _L1_ffn_ref(_layernorm(h, axis=-1), L1_ffn_gamma, L1_ffn_beta, L1_ffn_Wr, L1_ffn_br, L1_ffn_W1, L1_ffn_b1, L1_ffn_W2, L1_ffn_b2)
    return h

_drawn_inputs = setup_inputs


def setup_inputs(seed=0):
    import zlib

    import numpy as np

    out = dict(_drawn_inputs(seed))
    spreads = {'L0_tok_bo': (0.0, 0.1),
     'L0_tok_gamma': (1.0, 0.2),
     'L0_tok_beta': (0.0, 0.1),
     'L0_tok_b1': (0.0, 0.1),
     'L0_tok_b2': (0.0, 0.1),
     'L0_ffn_ln1_w': (1.0, 0.6),
     'L0_ffn_ln2_w': (1.0, 0.6),
     'L1_attn_bq': (0.0, 2.0),
     'L1_attn_bk': (0.0, 2.0),
     'L1_attn_bv': (0.0, 0.1),
     'L1_ffn_br': (0.0, 0.8)}
    factors = {'L0_tok_wq': 8.0,
     'L0_tok_wk': 8.0,
     'L0_ffn_wq': 8.0,
     'L0_ffn_wk': 8.0,
     'L0_ffn_wv': 7.454,
     'L0_ffn_wo': 8.0,
     'L0_ffn_router_w': 8.0,
     'L0_ffn_w1': 8.0,
     'L0_ffn_w2': 8.0,
     'L0_ffn_w3': 8.0,
     'L1_attn_Wq': 34.498,
     'L1_attn_Wk': 37.181,
     'L1_ffn_gamma': 8.0,
     'L1_ffn_beta': 8.0,
     'L1_ffn_Wr': 8.0,
     'L1_ffn_W1': 8.0,
     'L1_ffn_b1': 28.165,
     'L1_ffn_W2': 8.0,
     'L1_ffn_b2': 45.587}
    for name, (base, spread) in spreads.items():
        noise = np.random.default_rng([zlib.crc32(name.encode()), seed]).standard_normal(out[name].shape)
        drawn = base * np.exp(spread * noise) if base else spread * noise
        out[name] = jnp.asarray(drawn.astype(out[name].dtype))
    for name, factor in factors.items():
        out[name] = (out[name] * factor).astype(out[name].dtype)
    return out
```

```python
from contextlib import ExitStack

import concourse.bass as bass
from concourse import mybir
import numpy as np

ALU = mybir.AluOpType
ACT = mybir.ActivationFunctionType
F32 = mybir.dt.float32
BF16 = mybir.dt.bfloat16
I32 = mybir.dt.int32
U32 = mybir.dt.uint32
X_AXIS = mybir.AxisListType.X

P = 128
D = 64
S = 256
TILES = S // P
BATCH = 8
CHAINS = 2
TOK_LAYERS, TOK_HEADS, TOK_HD = 4, 8, 8
FFN = 4 * D
PAIRS = TOK_HEADS // 2
SLOT = 64
Q_PARTS = [1, 1, 1, 2, 2, 3]
K_PARTS = [3, 1, 2, 1, 2, 1]
TERMS = len(Q_PARTS)
SPLIT_ROWS = TERMS * TOK_HD
ROWS = SPLIT_ROWS + 3
ATT_HEADS = 8
GQA_HEADS, GQA_KV, GQA_HD = 4, 2, 16
EXPERTS = 8
HID = 170
HID_TILES = -(-EXPERTS * HID // P)
VS = D + 1
CAUSAL = P + S
MASKED = -1e30



def constants():
    pos = np.arange(S).reshape(-1, 1)
    depth = np.array([2 * (i // 2) for i in range(D)]).reshape(1, -1)
    angle = pos * (1.0 / 10000.0 ** (depth / D))
    enc = np.cos(angle)
    enc[:, ::2] = np.sin(enc[:, ::2])
    enc = enc.astype(np.float32).reshape(TILES, P, D).transpose(1, 0, 2)
    inv = 1.0 / 10000.0 ** (np.arange(0, GQA_HD, 2, dtype=np.float32) / GQA_HD)
    freq = np.outer(np.arange(S, dtype=np.float32), inv)
    emb = np.concatenate([freq, freq], axis=-1)
    cos, sin = np.cos(emb).astype(np.float32), np.sin(emb).astype(np.float32)
    sin[:, :GQA_HD // 2] *= -1
    tile = lambda a: a.reshape(TILES, P, GQA_HD).transpose(1, 0, 2).reshape(P, -1)
    iota = np.tile(np.arange(EXPERTS, dtype=np.float32), (P, 1))
    later = np.triu(np.ones((P, P), np.float32), 1) * MASKED
    sel = np.zeros((EXPERTS, HID_TILES, P), np.float32)
    for j in range(EXPERTS * HID):
        sel[j // HID, j // P, j % P] = 1
    sel_e = np.zeros((EXPERTS, EXPERTS, P), np.float32)
    for e in range(EXPERTS):
        sel_e[e, e] = 1
    return {
        "eye": np.eye(P, dtype=np.float32), "enc": enc.reshape(P, -1), "cos": tile(cos), "sin": tile(sin),
        "iota": iota, "later": later, "later_t": np.ascontiguousarray(later.T),
        "sel": sel.reshape(EXPERTS, -1), "sel_e": sel_e.reshape(EXPERTS, -1),
    }


def rows(a):
    return np.broadcast_to(np.asarray(a).reshape(1, -1), (P, np.asarray(a).size))


def pack(i):
    a = {k: np.asarray(v) for k, v in i.items()}
    wq = a["L0_tok_wq"].transpose(2, 0, 1, 3).reshape(D, TOK_LAYERS, D)
    wk = a["L0_tok_wk"].transpose(2, 0, 1, 3).reshape(D, TOK_LAYERS, D)
    wv = a["L0_tok_wv"].transpose(2, 0, 1, 3).reshape(D, TOK_LAYERS, D)
    pad = HID_TILES * P - EXPERTS * HID
    flat = lambda w: np.pad(w.reshape(EXPERTS * HID, D), ((0, pad), (0, 0)))
    w2 = np.pad(a["L0_ffn_w2"].transpose(0, 2, 1).reshape(EXPERTS * HID, D), ((0, pad), (0, 0)))
    out = {
        "tok_qkv": np.concatenate([wq, wk, wv], axis=2).reshape(D, -1),
        "tok_wo": a["L0_tok_wo"].transpose(1, 0, 2).reshape(D, -1),
        "tok_w1": a["L0_tok_w1"].transpose(1, 0, 2).reshape(D, -1),
        "tok_w2": a["L0_tok_w2"].reshape(TOK_LAYERS, 2, P, D).transpose(2, 0, 1, 3).reshape(P, -1),
        "tok_b1": a["L0_tok_b1"].reshape(TOK_LAYERS * 2, P).T,
        "tok_bo": rows(a["L0_tok_bo"]), "tok_b2": rows(a["L0_tok_b2"]),
        "tok_gamma": rows(a["L0_tok_gamma"]), "tok_beta": rows(a["L0_tok_beta"]),
        "att_k": a["L0_attn_key_matrices"].transpose(2, 0, 1).reshape(D, -1),
        "att_q": a["L0_attn_query_matrices"].transpose(2, 0, 1).reshape(D, -1),
        "att_vi": a["L0_attn_value_in_matrices"].transpose(2, 0, 1).reshape(D, -1),
        "att_vo": a["L0_attn_value_out_matrices"].transpose(1, 0, 2).reshape(D, -1),
        "gqa_ln1": rows(a["L0_ffn_ln1_w"]), "gqa_ln2": rows(a["L0_ffn_ln2_w"]),
        "gqa_qkv": np.concatenate([a["L0_ffn_wq"], a["L0_ffn_wk"], a["L0_ffn_wv"]], axis=0).T,
        "gqa_wo": a["L0_ffn_wo"].T,
        "moe_router": a["L0_ffn_router_w"].T,
        "moe_w1": flat(a["L0_ffn_w1"]).T, "moe_w3": flat(a["L0_ffn_w3"]).T,
        "moe_w2": w2.reshape(HID_TILES, P, D).transpose(1, 0, 2).reshape(P, -1),
        "one_wq": a["L1_attn_Wq"], "one_wk": a["L1_attn_Wk"], "one_wv": a["L1_attn_Wv"],
        "one_bq": a["L1_attn_bq"].reshape(D, 1), "one_bk": a["L1_attn_bk"].reshape(D, 1),
        "one_bv": rows(a["L1_attn_bv"]),
        "gelu_gamma": rows(a["L1_ffn_gamma"]), "gelu_beta": rows(a["L1_ffn_beta"]),
        "gelu_router": a["L1_ffn_Wr"], "gelu_br": rows(a["L1_ffn_br"]),
        "gelu_w1": a["L1_ffn_W1"].transpose(1, 0, 2).reshape(D, -1), "gelu_b1": a["L1_ffn_b1"].T,
        "gelu_w2": a["L1_ffn_W2"].transpose(1, 0, 2).reshape(P, -1), "gelu_b2": a["L1_ffn_b2"],
    }
    out.update(constants())
    return out


def columns(shapes, parts):
    at, found = 0, {}
    for name, (p, n) in shapes.items():
        if p == parts:
            found[name] = (at, n)
            at += n
    return found, at


class Counts:

    def __init__(self):
        self.n = {}

    def __call__(self, name, k=1):
        self.n[name] = self.n.get(name, 0) + k
        return self.n[name]

    def now(self, name):
        return self.n.get(name, 0)


class Signals:

    def __init__(self, nc, ctx):
        self.nc, self.ctx, self.made, self.first, self.last = nc, ctx, {}, None, None

    def __getitem__(self, name):
        if name not in self.made:
            self.made[name] = [self.ctx.enter_context(self.nc.semaphore(f"{name}{c}")) for c in range(CHAINS)]
            self.first = self.first or self.made[name][0]
            self.last = self.made[name][-1]
        return self.made[name]


def in_turns(programs, lag):
    live, n = [True] * len(programs), 0
    while any(live):
        for c, program in enumerate(programs):
            if live[c] and n >= c * lag:
                live[c] = next(program, "end") != "end"
        n += 1


def tower(nc, x, table, packed, shapes, out, LAG=20):
    with ExitStack() as ctx:
        def sb(name, shape, dt=F32):
            return ctx.enter_context(nc.sbuf_tensor(name, shape, dt))

        def sem(name):
            return ctx.enter_context(nc.semaphore(name))

        W = {}
        for parts, dram in packed.items():
            at, n = columns(shapes, parts)
            t = sb(f"resident{parts}", [parts, n])
            W.update({k: (t, a, m) for k, (a, m) in at.items()})
            W[parts] = t

        def w(name, a=0, b=None):
            t, at, n = W[name]
            return t[:, at + a:at + (n if b is None else b)]

        eye = w("eye")
        eye_b = sb("eye_b", [P, P], BF16)
        later_b = sb("later_b", [P, 2, P], BF16)
        att_g = sb("att_g", [D, ATT_HEADS, D])
        att_v = sb("att_v", [D, ATT_HEADS, D])
        ids = sb("ids", [P, BATCH * TILES], I32)
        tokens = sb("tokens", [P, BATCH * TILES, D])
        minus_half = sb("minus_half", [P, TILES])

        def per(name, shape, dt=F32):
            return [sb(f"{name}{c}", shape, dt) for c in range(CHAINS)]

        h = per("h", [P, TILES, D])
        hb = per("hb", [P, TILES, D])
        s_ = per("s_", [P, TILES, D])
        xn = per("xn", [P, TILES, D])
        hc = per("hc", [P, TILES, D])
        stats = per("stats", [P, TILES, 6])
        mv = per("mv", [P, TILES, 2])
        var = per("var", [P, TILES])
        rstd = per("rstd", [P, TILES])
        hT = per("hT", [VS, S])
        qk1 = per("qk1", [P, 2, TILES * D], BF16)
        qk2 = per("qk2", [P, 2, TILES * D], BF16)
        rest = per("rest", [P, 2, TILES * D])
        qn = per("qn", [P, TILES * TOK_HEADS, SLOT], BF16)
        kn = per("kn", [P, TILES * TOK_HEADS, SLOT], BF16)
        qTa = per("qTa", [P, PAIRS, S], BF16)
        qTb = per("qTb", [P, PAIRS, S], BF16)
        kT = per("kT", [P, PAIRS, S], BF16)
        nm = per("nm", [P, TILES * TOK_HEADS])
        nr = per("nr", [P, TILES * TOK_HEADS])
        v8 = per("v8", [P, TILES, TOK_HEADS, 32])
        pr = per("pr", [P, 8, 2 * S])
        oT = per("oT", [P, 2, S])
        rden = per("rden", [P, TILES * TOK_HEADS])
        att = per("att", [P, TILES, D])
        aT = per("aT", [D, S])
        hid = per("hid", [P, 2, S])
        rT = per("rT", [VS, ATT_HEADS, S])
        nmT = per("nmT", [TILES * ATT_HEADS, P])
        vb = per("vb", [P, TILES, ATT_HEADS, VS])
        ob = per("ob", [P, TILES, ATT_HEADS, D])
        ss = per("ss", [P, TILES])
        q4 = per("q4", [P, TILES, GQA_HEADS, 32])
        k4 = per("k4", [P, TILES, GQA_HEADS, 32])
        q4T = per("q4T", [P, S])
        k4T = per("k4T", [P, S])
        v4 = per("v4", [P, TILES, GQA_KV, 32])
        ra = per("ra", [P, TILES, 6, GQA_HD])
        rb = per("rb", [P, TILES, 6, GQA_HD])
        lg = per("lg", [P, TILES, 10])
        lo = per("lo", [P, TILES, EXPERTS])
        top = per("top", [P, TILES, 8])
        idx = per("idx", [P, TILES, 8], U32)
        idf = per("idf", [P, TILES, 8])
        ex = per("ex", [P, TILES, 10])
        sw = per("sw", [P, TILES, 4])
        gates = per("gates", [P, TILES, EXPERTS])
        g2 = per("g2", [P, TILES, EXPERTS])
        gT = per("gT", [EXPERTS, S])
        act = per("act", [P, 2, S])
        t1 = per("t1", [P, 2, S])
        t2 = per("t2", [P, 2, S])

        bank = [[ctx.enter_context(nc.psum_tensor(f"bank{k}{c}", [P, 512], F32)) for k in "stxy"] for c in range(CHAINS)]

        sig = Signals(nc, ctx)
        loaded, gathered, setup_pe, setup_done = sem("loaded"), sem("gathered"), sem("setup_pe"), sem("setup_done")
        stored = sem("stored")

        with nc.Block() as block:
            n_loads = len(packed) + 1

            @block.sync
            def _(sp):
                sp.dma_start(ids[:], x).then_inc(loaded, 16)
                for parts, dram in packed.items():
                    sp.dma_start(W[parts][:], dram).then_inc(loaded, 16)
                sp.wait_ge(loaded, 16 * n_loads)

            @block.gpsimd
            def _(pool):
                for c in range(CHAINS):
                    pool.memset(qn[c][:], 0.0)
                    pool.memset(kn[c][:, :, ROWS:SLOT], 0.0)
                    pool.memset(kn[c][:, :, SPLIT_ROWS:ROWS], 1.0)
                    pool.memset(v8[c][:, :, :, TOK_HD + 1:32], 0.0)
                    pool.memset(v8[c][:, :, :, TOK_HD:TOK_HD + 1], 1.0)
                    pool.memset(vb[c][:, :, :, D:VS], 1.0)
                    pool.memset(q4[c][:], 0.0)
                    pool.memset(k4[c][:, :, :, GQA_HD + 1:32], 0.0)
                    pool.memset(k4[c][:, :, :, GQA_HD:GQA_HD + 1], 1.0)
                    pool.memset(v4[c][:, :, :, GQA_HD + 1:32], 0.0)
                    pool.memset(v4[c][:, :, :, GQA_HD:GQA_HD + 1], 1.0)
                pool.memset(minus_half[:], -0.5)
                pool.wait_ge(loaded, 16 * n_loads)
                for n in range(BATCH * TILES):
                    pool.indirect_dma_start(
                        out=tokens[:, n, :], out_offset=None, in_=table[:, :],
                        in_offset=bass.IndirectOffsetOnAxis(ap=ids[:, n:n + 1], axis=0)).then_inc(gathered, 16)
                pool.wait_ge(gathered, 16 * BATCH * TILES)

            @block.vector
            def _(dve):
                for c in range(CHAINS):
                    dve.memset(hT[c][D:VS, :], 1.0).then_inc(setup_done, 1)
                dve.wait_ge(loaded, 16 * n_loads)
                dve.tensor_copy(eye_b[:], eye).then_inc(setup_done, 1)
                dve.tensor_copy(later_b[:, 0, :], w("later")).then_inc(setup_done, 1)
                dve.tensor_copy(later_b[:, 1, :], w("later_t")).then_inc(setup_done, 1)
                for k, dst in enumerate((att_g, att_v)):
                    dve.wait_ge(setup_pe, k + 1)
                    dve.tensor_copy(dst[:], bank[0][k][0:D, :].rearrange("p (n e) -> p n e", n=ATT_HEADS)).then_inc(setup_done, 1)
                dve.wait_ge(setup_done, 5 + CHAINS)

            @block.tensor
            def _(pe):
                pe.wait_ge(loaded, 16 * n_loads)
                for k, (left, right) in enumerate((("att_k", "att_q"), ("att_vi", "att_vo"))):
                    for n in range(ATT_HEADS):
                        last = pe.matmul(bank[0][k][0:D, n * D:(n + 1) * D], w(left, n * D, (n + 1) * D),
                                         w(right, n * D, (n + 1) * D), start=True, stop=True)
                    last.then_inc(setup_pe, 1)

        out_v = out.rearrange("b (t p) d -> p (b t) d", p=P)

        def pe_chain(pe, c):
            cnt = Counts()
            bs, bt, bx, by = bank[c]

            def wait(name, k=1):
                pe.wait_ge(sig[name][c], cnt(name, k))

            def turn(src, dst, done):
                for t in range(TILES):
                    last = pe.transpose(dst[0:D, t * P:(t + 1) * P], src[:, t, :], eye)
                last.then_inc(sig[done][c], 1)

            def natural(dst, lhs, rhs, done, rows=D):
                n = rhs.shape[-1]
                for t in range(TILES):
                    last = pe.matmul(dst[:, t * n:(t + 1) * n], lhs[0:rows, t * P:(t + 1) * P], rhs, start=True, stop=True)
                last.then_inc(sig[done][c], 1)

            def turn_pairs(src, dst):
                d = dst[:].bitcast(BF16).rearrange("p (q s) -> p q s", q=PAIRS)
                for q in range(PAIRS):
                    for t in range(TILES):
                        h0 = t * TOK_HEADS + 2 * q
                        last = pe.transpose(d[:, q, t * P:(t + 1) * P],
                                            src[:, h0:h0 + 2, :].rearrange("p a b -> p (a b)"), eye_b[:])
                return last

            for l in range(TOK_LAYERS):
                wait("h")
                turn(h[c], bx, "turned")
                wait("hT")
                natural(by, hT[c], w("tok_qkv", l * 3 * D, (l + 1) * 3 * D), "qkv")
                yield
                wait("parts")
                wait("parts_p", 2)
                turn_pairs(kn[c], by).then_inc(sig["k_turned"][c], 1)
                turn_pairs(qn[c], bx).then_inc(sig["q_turned"][c], 1)
                yield
                wait("kT")
                wait("qTa")
                for n in range(TOK_HEADS):
                    if n >= 2:
                        pe.wait_ge(sig["max"][c], cnt.now("max") + n - 1)
                    r = slice(SLOT * (n % 2), SLOT * (n % 2) + SPLIT_ROWS)
                    for t in range(TILES):
                        last = pe.matmul((bs, bt)[n % 2][:, t * S:(t + 1) * S], qTa[c][r, n // 2, t * P:(t + 1) * P],
                                         kT[c][r, n // 2, :], start=True, stop=True)
                    last.then_inc(sig["scores"][c], 1)
                    yield
                cnt("max", TOK_HEADS)
                wait("max_split")
                turn_pairs(qn[c], bx).then_inc(sig["q_turned"][c], 1)
                yield
                wait("qTb")
                base = cnt.now("exp")

                def values(half):
                    pe.wait_ge(sig["exp"][c], base + 4 * half + 4)
                    for t in range(TILES):
                        for j in range(4):
                            last = pe.matmul((by, bx)[half][32 * j:32 * j + 32, 0:S], v8[c][:, t, 4 * half + j, :],
                                             pr[c][:, 4 * half + j, t * S:(t + 1) * S], start=(t == 0), stop=(t == 1),
                                             tile_position=(0, 32 * j), skip_group_check=True)
                    last.then_inc(sig["values"][c], 1)

                wait("v8")
                for n in range(TOK_HEADS):
                    if n >= 2:
                        pe.wait_ge(sig["exp"][c], base + n - 1)
                    r = slice(SLOT * (n % 2), SLOT * (n % 2) + ROWS)
                    for t in range(TILES):
                        last = pe.matmul((bs, bt)[n % 2][:, t * S:(t + 1) * S], kT[c][r, n // 2, t * P:(t + 1) * P],
                                         qTb[c][r, n // 2, :], start=True, stop=True)
                    last.then_inc(sig["scores"][c], 1)
                    if n == 5:
                        values(0)
                    yield
                values(1)
                cnt("exp", TOK_HEADS)
                yield
                wait("oT", 2)
                for half in range(2):
                    for t in range(TILES):
                        last = pe.transpose(bs[:, (t * 2 + half) * P:(t * 2 + half + 1) * P],
                                            oT[c][:, half, t * P:(t + 1) * P], eye)
                last.then_inc(sig["o_turned"][c], 1)
                yield
                wait("att")
                turn(att[c], bt, "turned")
                wait("aT")
                natural(bx, aT[c], w("tok_wo", l * D, (l + 1) * D), "proj")
                yield
                wait("h")
                turn(h[c], bx, "turned")
                yield
                wait("hT")
                for m in range(2):
                    pe.matmul((by, bs)[m][:, 0:S], w("tok_w1", l * FFN + m * P, l * FFN + (m + 1) * P), hT[c][0:D, :],
                              start=True, stop=True).then_inc(sig["ffn"][c], 1)
                yield
                wait("hid_a")
                wait("hid_v")
                for t in range(TILES):
                    for m in range(2):
                        last = pe.matmul(bt[:, t * D:(t + 1) * D], hid[c][:, m, t * P:(t + 1) * P],
                                         w("tok_w2", (l * 2 + m) * D, (l * 2 + m + 1) * D), start=(m == 0), stop=(m == 1))
                last.then_inc(sig["proj"][c], 1)
                yield

            wait("xn")
            turn(xn[c], bx, "turned")
            wait("hT")
            for i in range(4):
                if i >= 2:
                    pe.wait_ge(sig["rT"][c], i - 1)
                for j in range(2):
                    last = pe.matmul((by, bx)[i % 2][0:D, j * S:(j + 1) * S], att_g[:, 2 * i + j, :], hT[c][0:D, :],
                                     start=True, stop=True)
                last.then_inc(sig["row_side"][c], 1)
            for t in range(TILES):
                pe.matmul((bs, bt)[t][:], hT[c][0:D, t * P:(t + 1) * P], att_v[:].rearrange("p n e -> p (n e)"),
                          start=True, stop=True).then_inc(sig["v_side"][c], 1)
            yield
            pe.wait_ge(sig["rT"][c], 4)
            pe.wait_ge(sig["vb"][c], 2)

            def causal_natural(dst, lhs, rhs):
                pe.matmul(dst[:, 0:P], lhs(0), rhs(0, P), start=True, stop=False, skip_group_check=True)
                pe.matmul(dst[:, 0:P], eye_b[:], later_b[:, 0, :], start=False, stop=True, skip_group_check=True)
                pe.matmul(dst[:, P:P + S], lhs(1), rhs(0, S), start=True, stop=False, skip_group_check=True)
                return pe.matmul(dst[:, S:S + P], eye_b[:], later_b[:, 0, :], start=False, stop=True, skip_group_check=True)

            def causal_turned(dst, lhs, rhs):
                pe.matmul(dst[:, 0:S], lhs(0), rhs(0, S), start=True, stop=False, skip_group_check=True)
                pe.matmul(dst[:, 0:P], eye_b[:], later_b[:, 1, :], start=False, stop=True, skip_group_check=True)
                pe.matmul(dst[:, S:S + P], lhs(1), rhs(P, S), start=True, stop=False, skip_group_check=True)
                return pe.matmul(dst[:, S:S + P], eye_b[:], later_b[:, 1, :], start=False, stop=True, skip_group_check=True)

            for n in range(ATT_HEADS):
                if n >= 2:
                    pe.wait_ge(sig["max"][c], cnt.now("max") + n - 1)
                causal_natural((bs, bt)[n % 2], lambda t: rT[c][0:D, n, t * P:(t + 1) * P],
                               lambda a, b: hT[c][0:D, a:b]).then_inc(sig["scores"][c], 1)
                yield
            wait("max", ATT_HEADS)
            pe.transpose(bx[0:TILES * ATT_HEADS, 0:P], nm[c][:], eye).then_inc(sig["turned"][c], 1)
            yield
            wait("max_row", 16)
            base = cnt.now("exp")

            def values_natural(n):
                pe.wait_ge(sig["exp"][c], base + n + 1)
                if n == 4:
                    pe.wait_ge(sig["ob"][c], 2)
                k = n % 4
                pe.matmul(bx[:, k * VS:(k + 1) * VS], pr[c][:, n, 0:P], vb[c][:, 0, n, :], start=True, stop=True)
                pe.matmul(by[:, k * VS:(k + 1) * VS], pr[c][:, n, P:S], vb[c][:, 0, n, :], start=True, stop=False)
                last = pe.matmul(by[:, k * VS:(k + 1) * VS], pr[c][:, n, S:S + P], vb[c][:, 1, n, :], start=False, stop=True)
                if k == 3:
                    last.then_inc(sig["values"][c], 1)

            for n in range(ATT_HEADS):
                if n >= 2:
                    pe.wait_ge(sig["exp"][c], base + n - 1)
                causal_turned((bs, bt)[n % 2], lambda t: hT[c][0:VS, t * P:(t + 1) * P],
                              lambda a, b: rT[c][0:VS, n, a:b]).then_inc(sig["scores"][c], 1)
                if n >= 2:
                    values_natural(n - 2)
                yield
            values_natural(ATT_HEADS - 2)
            values_natural(ATT_HEADS - 1)
            cnt("exp", ATT_HEADS)
            yield

            wait("hc")
            turn(hc[c], bs, "turned")
            wait("hT")
            natural(bt, hT[c], w("gqa_qkv"), "qkv")
            yield
            wait("parts")
            for src, dst, done in ((k4, bx, "k_turned"), (q4, by, "q_turned")):
                for t in range(TILES):
                    last = pe.transpose(dst[:, t * P:(t + 1) * P], src[c][:, t].rearrange("p a b -> p (a b)"), eye)
                last.then_inc(sig[done][c], 1)
            yield
            wait("kT")
            wait("qTa")
            for n in range(GQA_HEADS):
                if n >= 2:
                    pe.wait_ge(sig["max"][c], cnt.now("max") + n - 1)
                r = slice(32 * n, 32 * n + GQA_HD)
                causal_natural((bs, bt)[n % 2], lambda t: q4T[c][r, t * P:(t + 1) * P],
                               lambda a, b: k4T[c][r, a:b]).then_inc(sig["scores"][c], 1)
                yield
            wait("max", GQA_HEADS)
            for t in range(TILES):
                last = pe.transpose(by[:, t * P:(t + 1) * P], q4[c][:, t].rearrange("p a b -> p (a b)"), eye)
            last.then_inc(sig["q_turned"][c], 1)
            yield
            wait("qTb")
            for n in range(GQA_HEADS):
                if n >= 2:
                    pe.wait_ge(sig["exp"][c], cnt.now("exp") + n - 1)
                r = slice(32 * n, 32 * n + GQA_HD + 1)
                causal_turned((bs, bt)[n % 2], lambda t: k4T[c][r, t * P:(t + 1) * P],
                              lambda a, b: q4T[c][r, a:b]).then_inc(sig["scores"][c], 1)
                yield
            wait("exp", GQA_HEADS)
            for t in range(TILES):
                for j in range(GQA_HEADS):
                    cols = (slice(0, S), slice(P, S))[t]
                    last = pe.matmul(by[32 * j:32 * j + 32, cols], v4[c][:, t, j // 2, :],
                                     pr[c][:, j, (0, S)[t]:(S, S + P)[t]], start=(t == 0), stop=(t == 1),
                                     tile_position=(0, 32 * j), skip_group_check=True)
            last.then_inc(sig["values"][c], 1)
            yield
            wait("oT")
            for t in range(TILES):
                last = pe.transpose(bs[:, t * P:(t + 1) * P], oT[c][:, 0, t * P:(t + 1) * P], eye)
            last.then_inc(sig["o_turned"][c], 1)
            yield
            wait("att")
            turn(att[c], bt, "turned")
            wait("aT")
            natural(bx, aT[c], w("gqa_wo"), "proj")
            yield

            def gates_turned():
                wait("gates")
                for t in range(TILES):
                    last = pe.transpose(bx[0:EXPERTS, t * P:(t + 1) * P], gates[c][:, t, :], eye)
                last.then_inc(sig["turned"][c], 1)
                wait("gT")

            def hidden_out(i, weights, tiles, bias=None):
                wait("t2")
                half = i % 2
                last = pe.matmul(by[D * half:D * half + D, 0:S], weights, t2[c][:, i % 2, :],
                                 start=(i < 2), stop=(i >= tiles - 2 and bias is None), tile_position=(0, D * half),
                                 skip_group_check=True)
                return last

            wait("hc")
            turn(hc[c], bs, "turned")
            wait("hT")
            natural(bt, hT[c], w("moe_router"), "logits")
            yield
            gates_turned()
            yield
            for i in range(HID_TILES + 1):
                if i < HID_TILES:
                    if i >= 2:
                        pe.wait_ge(sig["t1"][c], i - 1)
                    pe.matmul((bs, bt)[i % 2][:, 0:S], w("moe_w1", i * P, (i + 1) * P), hT[c][0:D, :], start=True, stop=True)
                    pe.matmul((bs, bt)[i % 2][:, S:2 * S], w("moe_w3", i * P, (i + 1) * P), hT[c][0:D, :],
                              start=True, stop=True).then_inc(sig["up"][c], 1)
                    if i >= 1:
                        pe.wait_ge(sig["t2"][c], cnt.now("t2") + 1)
                    pe.matmul(bx[:, 0:S], w("sel", i * P, (i + 1) * P), gT[c][:], start=True, stop=True
                              ).then_inc(sig["wide"][c], 1)
                if i >= 1:
                    last = hidden_out(i - 1, w("moe_w2", (i - 1) * D, i * D), HID_TILES)
                yield
            last.then_inc(sig["moe"][c], 1)
            wait("oT")
            for t in range(TILES):
                last = pe.transpose(bs[:, t * P:(t + 1) * P], oT[c][:, 0, t * P:(t + 1) * P], eye)
            last.then_inc(sig["o_turned"][c], 1)
            yield

            wait("xn", 2)
            turn(xn[c], bx, "turned")
            wait("hT")
            pe.matmul(by[0:D, 0:S], w("one_wq"), hT[c][0:D, :], start=True, stop=True).then_inc(sig["row_side"][c], 1)
            pe.matmul(bt[0:D, 0:S], w("one_wk"), hT[c][0:D, :], start=True, stop=True).then_inc(sig["row_side"][c], 1)
            natural(bx, hT[c], w("one_wv"), "v_side")
            yield
            pe.wait_ge(sig["rT"][c], 5)
            pe.wait_ge(sig["vb"][c], 3)
            wait("kT")
            for t in range(TILES):
                pe.matmul((bs, bt)[t][:, 0:S], rT[c][0:D, 0, t * P:(t + 1) * P], hT[c][0:D, :], start=True, stop=True
                          ).then_inc(sig["scores"][c], 1)
            wait("max", 2)
            pe.transpose(by[0:TILES, 0:P], nm[c][:, 0:TILES], eye).then_inc(sig["turned"][c], 1)
            yield
            wait("max_row", 16)
            for t in range(TILES):
                pe.matmul((bs, bt)[t][:, 0:S], hT[c][0:VS, t * P:(t + 1) * P], rT[c][0:VS, 0, :], start=True, stop=True
                          ).then_inc(sig["scores"][c], 1)
            wait("exp", 2)
            for t in range(TILES):
                for k in range(TILES):
                    last = pe.matmul(bx[:, t * VS:(t + 1) * VS], pr[c][:, k, t * P:(t + 1) * P], vb[c][:, k, 0, :],
                                     start=(k == 0), stop=(k == 1))
            last.then_inc(sig["values"][c], 1)
            yield

            wait("hc")
            turn(hc[c], bs, "turned")
            wait("hT")
            natural(bt, hT[c], w("gelu_router"), "logits")
            yield
            gates_turned()
            yield
            for i in range(EXPERTS + 1):
                if i < EXPERTS:
                    if i >= 2:
                        pe.wait_ge(sig["gelu"][c], i - 1)
                    pe.matmul((bs, bt)[i % 2][:, 0:S], w("gelu_w1", i * P, (i + 1) * P), hT[c][0:D, :], start=True, stop=True
                              ).then_inc(sig["up"][c], 1)
                    if i >= 1:
                        pe.wait_ge(sig["t2"][c], cnt.now("t2") + 1)
                    pe.matmul(bx[:, 0:S], w("sel_e", i * P, (i + 1) * P), gT[c][:], start=True, stop=True
                              ).then_inc(sig["wide"][c], 1)
                if i >= 1:
                    hidden_out(i - 1, w("gelu_w2", (i - 1) * D, i * D), EXPERTS, bias=True)
                yield
            pe.matmul(by[0:D, 0:S], w("gelu_b2"), gT[c][:], start=False, stop=True, skip_group_check=True
                      ).then_inc(sig["moe"][c], 1)
            wait("oT")
            for t in range(TILES):
                last = pe.transpose(bs[:, t * P:(t + 1) * P], oT[c][:, 0, t * P:(t + 1) * P], eye)
            last.then_inc(sig["o_turned"][c], 1)
            yield

        def act_chain(eng, c):
            cnt = Counts()
            bs, bt, bx, by = bank[c]

            def wait(name, k=1):
                eng.wait_ge(sig[name][c], cnt(name, k))

            def copy_turned(src, dst, name):
                wait("turned")
                eng.copy(dst[c][0:D, :], src[0:D, 0:S]).then_inc(sig[name][c], 1)

            for l in range(TOK_LAYERS):
                copy_turned(bx, hT, "hT")
                wait("qkv")
                y = by[:, 0:TILES * 3 * D].rearrange("p (t n) -> p t n", t=TILES)
                eng.copy(qk1[c][:].rearrange("p a (t n) -> p a t n", t=TILES),
                         y[:, :, 0:2 * D].rearrange("p t (a n) -> p a t n", a=2)).then_inc(sig["qk1"][c], 1)
                eng.copy(v8[c][:, :, :, 0:TOK_HD], y[:, :, 2 * D:3 * D].rearrange("p t (h k) -> p t h k", k=TOK_HD)
                         ).then_inc(sig["v8"][c], 1)
                yield
                wait("k_turned")
                eng.copy(kT[c][:].rearrange("p q s -> p (q s)"), by[:].bitcast(BF16)).then_inc(sig["kT"][c], 1)
                yield
                for n in range(TOK_HEADS):
                    yield
                wait("q_turned", 2)
                eng.copy(qTb[c][:].rearrange("p q s -> p (q s)"), bx[:].bitcast(BF16)).then_inc(sig["qTb"][c], 1)
                yield
                cnt("scores", TOK_HEADS)
                for n in range(TOK_HEADS):
                    wait("scores")
                    eng.activation(pr[c][:, n, :], (bs, bt)[n % 2][:], ACT.Exp, scale=TOK_HD ** -0.5).then_inc(sig["exp"][c], 1)
                    yield
                yield
                yield
                copy_turned(bt, aT, "aT")
                yield
                copy_turned(bx, hT, "hT")
                yield
                wait("ffn")
                eng.activation(hid[c][:, 0, :], by[:, 0:S], ACT.Relu, bias=w("tok_b1", 2 * l, 2 * l + 1)).then_inc(sig["hid_a"][c], 1)
                cnt("ffn")
                yield
                yield

            copy_turned(bx, hT, "hT")
            for i in range(4):
                wait("row_side")
                eng.copy(rT[c][0:D, 2 * i:2 * i + 2, :].rearrange("p a s -> p (a s)"), (by, bx)[i % 2][0:D, :]
                         ).then_inc(sig["rT"][c], 1)
            for t in range(TILES):
                wait("v_side")
                eng.copy(vb[c][:, t, :, 0:D], (bs, bt)[t][:].rearrange("p (n e) -> p n e", e=D)).then_inc(sig["vb"][c], 1)
            yield
            for n in range(ATT_HEADS):
                yield
            wait("turned")
            eng.copy(nmT[c][:], bx[0:TILES * ATT_HEADS, 0:P]).then_inc(sig["nmT"][c], 1)
            yield
            cnt("scores", ATT_HEADS)
            for n in range(ATT_HEADS):
                wait("scores")
                eng.activation(pr[c][:, n, 0:CAUSAL], (bs, bt)[n % 2][:, 0:CAUSAL], ACT.Exp).then_inc(sig["exp"][c], 1)
                yield
            yield

            copy_turned(bs, hT, "hT")
            wait("qkv")
            eng.copy(v4[c][:, :, :, 0:GQA_HD],
                     bt[:, 0:S].rearrange("p (t n) -> p t n", t=TILES)[:, :, 96:128].rearrange("p t (a k) -> p t a k", k=GQA_HD)
                     ).then_inc(sig["v8"][c], 1)
            yield
            wait("k_turned")
            eng.copy(k4T[c][:], bx[:, 0:S]).then_inc(sig["kT"][c], 1)
            yield
            for n in range(GQA_HEADS):
                yield
            wait("q_turned", 2)
            eng.copy(q4T[c][:], by[:, 0:S]).then_inc(sig["qTb"][c], 1)
            yield
            cnt("scores", GQA_HEADS)
            for n in range(GQA_HEADS):
                wait("scores")
                eng.activation(pr[c][:, n, 0:CAUSAL], (bs, bt)[n % 2][:, 0:CAUSAL], ACT.Exp, scale=GQA_HD ** -0.5
                               ).then_inc(sig["exp"][c], 1)
                yield
            yield
            yield
            copy_turned(bt, aT, "aT")
            yield

            def routed():
                copy_turned(bs, hT, "hT")
                wait("lg")
                eng.activation(ex[c][:], lg[c][:], ACT.Exp).then_inc(sig["ex"][c], 1)
                yield
                wait("turned")
                eng.copy(gT[c][:], bx[0:EXPERTS, 0:S]).then_inc(sig["gT"][c], 1)
                yield

            yield from routed()
            for i in range(HID_TILES + 1):
                if i < HID_TILES:
                    wait("up")
                    if i >= 2:
                        eng.wait_ge(sig["t1"][c], i - 1)
                    eng.activation(act[c][:, i % 2, :], (bs, bt)[i % 2][:, 0:S], ACT.Silu).then_inc(sig["silu"][c], 1)
                yield
            yield

            copy_turned(bx, hT, "hT")
            wait("row_side", 2)
            eng.activation(rT[c][0:D, 0, :], by[0:D, 0:S], ACT.Identity, bias=w("one_bq")).then_inc(sig["rT"][c], 1)
            wait("v_side")
            eng.activation(hT[c][0:D, :], bt[0:D, 0:S], ACT.Identity, bias=w("one_bk")).then_inc(sig["kT"][c], 1)
            eng.copy(vb[c][:, :, 0, 0:D], bx[:, 0:TILES * D].rearrange("p (t d) -> p t d", t=TILES)).then_inc(sig["vb"][c], 1)
            yield
            wait("turned")
            eng.copy(nmT[c][0:TILES, :], by[0:TILES, 0:P]).then_inc(sig["nmT"][c], 1)
            yield
            cnt("scores", TILES)
            for t in range(TILES):
                wait("scores")
                eng.activation(pr[c][:, t, 0:S], (bs, bt)[t][:, 0:S], ACT.Exp, scale=D ** -0.5).then_inc(sig["exp"][c], 1)
            yield

            yield from routed()
            for i in range(EXPERTS + 1):
                if i < EXPERTS:
                    wait("up")
                    if i >= 2:
                        eng.wait_ge(sig["t2"][c], HID_TILES + i - 1)
                    eng.activation(act[c][:, i % 2, :], (bs, bt)[i % 2][:, 0:S], ACT.Gelu, bias=w("gelu_b1", i, i + 1)
                                   ).then_inc(sig["gelu"][c], 1)
                yield
            yield

        def dve_chain(dve, c, g):
            cnt = Counts()
            bs, bt, bx, by = bank[c]

            def wait(name, k=1):
                dve.wait_ge(sig[name][c], cnt(name, k))

            def link(ins):
                ins.then_inc(sig["dve"][c], 1)
                dve.wait_ge(sig["dve"][c], cnt("dve"))

            def show(ins, name):
                ins.then_inc(sig[name][c], 1)
                dve.wait_ge(sig[name][c], cnt(name))

            def layer_norm(src, dst):
                for t in range(TILES):
                    last = dve.bn_stats(stats[c][:, t, :], src[:, t, :])
                    last.then_inc(sig["dve"][c], 1)
                dve.wait_ge(sig["dve"][c], cnt("dve", TILES))
                for t in range(TILES):
                    dve.bn_aggr(mv[c][:, t, :], stats[c][:, t, :]).then_inc(sig["mv"][c], 1)
                wait("mv", TILES)
                wait("rstd")
                for t in range(TILES):
                    ins = dve.tensor_scalar(dst[:, t, :], src[:, t, :], mv[c][:, t, 0:1], rstd[c][:, t:t + 1], ALU.subtract, ALU.mult)
                    if t < TILES - 1:
                        ins.then_inc(sig["dve"][c], 1)
                        cnt("dve")
                dve_last.append(ins)
                return ins

            dve_last = []

            def tile_bc(name, a=0, b=None):
                v = w(name, a, b)
                return v.rearrange("p (o d) -> p o d", o=1).to_broadcast([P, TILES, v.shape[-1]])

            def add_norm(src, l, final=False):
                wait("proj")
                wait("hb")
                link(dve.tensor_tensor(s_[c][:], src[:, 0:TILES * D].rearrange("p (t d) -> p t d", t=TILES), hb[c][:], ALU.add))
                link(layer_norm(s_[c], xn[c]))
                link(dve.tensor_tensor(s_[c][:], xn[c][:], tile_bc("tok_gamma", l * D, (l + 1) * D), ALU.mult))
                show(dve.tensor_tensor(h[c][:], s_[c][:], tile_bc("tok_beta", l * D, (l + 1) * D), ALU.add), "h")

            link(dve.tensor_tensor(h[c][:], tokens[:, bass.ds(g * (CHAINS * TILES) + c * TILES, TILES), :],
                                   w("enc").rearrange("p (t d) -> p t d", t=TILES), ALU.add))
            show(dve.tensor_copy(s_[c][:, 0, 0:1], h[c][:, 0, 0:1]), "h")

            for l in range(TOK_LAYERS):
                wait("qk1")
                wait("v8")
                y = by[:, 0:TILES * 3 * D].rearrange("p (t n) -> p t n", t=TILES)
                r4 = rest[c][:].rearrange("p a (t n) -> p a t n", t=TILES)
                for a in range(2):
                    ins = dve.tensor_tensor(r4[:, a], y[:, :, a * D:(a + 1) * D],
                                            qk1[c][:, a].rearrange("p (t n) -> p t n", t=TILES), ALU.subtract)
                    ins.then_inc(sig["dve"][c], 1)
                dve.wait_ge(sig["dve"][c], cnt("dve", 2))
                link(dve.tensor_copy(qk2[c][:], rest[c][:]))
                heads = lambda ap, o=1: ap.rearrange("p (h o k) -> p h o k", o=o, k=TOK_HD)
                n_heads = TILES * TOK_HEADS
                for a, dst, at in ((0, qn, 5), (1, kn, 0)):
                    dve.tensor_tensor(dst[c][:, :, at * TOK_HD:(at + 1) * TOK_HD],
                                      rest[c][:, a].rearrange("p (h k) -> p h k", k=TOK_HD),
                                      qk2[c][:, a].rearrange("p (h k) -> p h k", k=TOK_HD), ALU.subtract
                                      ).then_inc(sig["dve"][c], 1)
                q_slots = qn[c][:, :, 0:SPLIT_ROWS].rearrange("p h (i k) -> p h i k", k=TOK_HD)
                k_slots = kn[c][:, :, 0:SPLIT_ROWS].rearrange("p h (i k) -> p h i k", k=TOK_HD)
                dve.tensor_copy(q_slots[:, :, 3:5], heads(qk2[c][:, 0]).to_broadcast([P, n_heads, 2, TOK_HD])).then_inc(sig["dve"][c], 1)
                dve.wait_ge(sig["dve"][c], cnt("dve", 3))
                show(dve.tensor_copy(k_slots[:, :, 2:5:2], heads(qk2[c][:, 1]).to_broadcast([P, n_heads, 2, TOK_HD])), "parts")
                yield
                wait("q_turned")
                show(dve.tensor_copy(qTa[c][:].rearrange("p q s -> p (q s)"), bx[:].bitcast(BF16)), "qTa")
                yield
                for n in range(TOK_HEADS):
                    wait("scores")
                    dve.tensor_reduce(nm[c][:].rearrange("p (t h) -> p t h", t=TILES)[:, :, n],
                                      (bs, bt)[n % 2][:].rearrange("p (t s) -> p t s", t=TILES), X_AXIS, ALU.max, negate=True
                                      ).then_inc(sig["max"][c], 1)
                    yield
                wait("max", TOK_HEADS)
                link(dve.tensor_copy(qn[c][:, :, SPLIT_ROWS], nm[c][:]))
                link(dve.tensor_tensor(nr[c][:], nm[c][:], qn[c][:, :, SPLIT_ROWS], ALU.subtract))
                link(dve.tensor_copy(qn[c][:, :, SPLIT_ROWS + 1], nr[c][:]))
                show(dve.tensor_tensor(qn[c][:, :, SPLIT_ROWS + 2], nr[c][:], qn[c][:, :, SPLIT_ROWS + 1], ALU.subtract), "max_split")
                cnt("q_turned")
                yield
                cnt("scores", TOK_HEADS)
                for n in range(TOK_HEADS):
                    if n == 6:
                        wait("values")
                        dve.tensor_copy(oT[c][:, 0, :], by[:, 0:S]).then_inc(sig["oT"][c], 1)
                    yield
                wait("values")
                dve.tensor_copy(oT[c][:, 1, :], bx[:, 0:S]).then_inc(sig["oT"][c], 1)
                cnt("oT", 2)
                yield
                wait("o_turned")
                o = bs[:].rearrange("p (n k) -> p n k", k=32)
                link(dve.reciprocal(rden[c][:], o[:, :, TOK_HD]))
                show(dve.tensor_tensor(att[c][:].rearrange("p t (n k) -> p (t n) k", k=TOK_HD), o[:, :, 0:TOK_HD],
                                       rden[c][:].rearrange("p (n o) -> p n o", o=1).to_broadcast([P, n_heads, TOK_HD]),
                                       ALU.mult), "att")
                yield
                add_norm(bx, l)
                yield
                yield
                cnt("ffn")
                wait("ffn")
                dve.tensor_scalar(hid[c][:, 1, :], bs[:, 0:S], w("tok_b1", 2 * l + 1, 2 * l + 2), 0.0, ALU.add, ALU.max
                                  ).then_inc(sig["hid_v"][c], 1)
                yield
                add_norm(bt, l)
                yield

            show(layer_norm(h[c], xn[c]), "xn")
            yield
            for n in range(ATT_HEADS):
                wait("scores")
                b = (bs, bt)[n % 2]
                dve.tensor_reduce(nm[c][:, 2 * n:2 * n + 1], b[:, 0:P], X_AXIS, ALU.max, negate=True).then_inc(sig["dve"][c], 1)
                cnt("dve")
                dve.tensor_reduce(nm[c][:, 2 * n + 1:2 * n + 2], b[:, P:P + S], X_AXIS, ALU.max, negate=True
                                  ).then_inc(sig["max"][c], 1)
                yield
            cnt("max", ATT_HEADS)
            yield

            def take(half):
                wait("values")
                for t, b in enumerate((bx, by)):
                    o = b[:, 0:4 * VS].rearrange("p (n e) -> p n e", e=VS)
                    rd = rden[c][:, 4 * t:4 * t + 4]
                    link(dve.reciprocal(rd, o[:, :, D]))
                    dve.tensor_tensor(ob[c][:, t, 4 * half:4 * half + 4, :], o[:, :, 0:D],
                                      rd.rearrange("p (n o) -> p n o", o=1).to_broadcast([P, 4, D]), ALU.mult
                                      ).then_inc(sig["ob"][c], 1)
                cnt("ob", 2)

            cnt("scores", ATT_HEADS)
            for n in range(ATT_HEADS):
                if n == 5:
                    take(0)
                yield
            take(1)
            dve.wait_ge(sig["ob"][c], cnt.now("ob"))
            link(dve.tensor_reduce(s_[c][:], ob[c][:].rearrange("p t n d -> p t d n"), X_AXIS, ALU.add))
            link(dve.tensor_tensor(h[c][:], h[c][:], s_[c][:], ALU.add))
            yield

            def rms_scaled(src, name):
                for t in range(TILES):
                    dve.tensor_tensor_reduce(s_[c][:, t, :], src[:, t, :], src[:, t, :], 1.0, 0.0, ALU.mult, ALU.add,
                                             ss[c][:, t:t + 1]).then_inc(sig["ss"][c], 1)
                wait("ss", TILES)
                wait("rstd")
                for t in range(TILES):
                    ins = dve.scalar_tensor_tensor(hc[c][:, t, :], src[:, t, :], rstd[c][:, t:t + 1], w(name), ALU.mult, ALU.mult)
                    if t < TILES - 1:
                        ins.then_inc(sig["dve"][c], 1)
                        cnt("dve")
                show(ins, "hc")

            show(layer_norm(h[c], xn[c]), "dve")
            rms_scaled(xn[c], "gqa_ln1")
            wait("v8")
            y = bt[:, 0:S].rearrange("p (t n) -> p t n", t=TILES)[:, :, 0:96].rearrange("p t (n k) -> p t n k", k=GQA_HD)
            H = GQA_HD // 2
            tab = lambda name, a, b: w(name).rearrange("p (t o k) -> p t o k", t=TILES, o=1)[:, :, :, a:b].to_broadcast([P, TILES, 6, b - a])
            dve.tensor_tensor(ra[c][:], y, tab("cos", 0, GQA_HD), ALU.mult).then_inc(sig["dve"][c], 1)
            dve.tensor_tensor(rb[c][:, :, :, 0:H], y[:, :, :, H:2 * H], tab("sin", 0, H), ALU.mult).then_inc(sig["dve"][c], 1)
            dve.tensor_tensor(rb[c][:, :, :, H:2 * H], y[:, :, :, 0:H], tab("sin", H, 2 * H), ALU.mult).then_inc(sig["dve"][c], 1)
            dve.wait_ge(sig["dve"][c], cnt("dve", 3))
            dve.tensor_tensor(q4[c][:, :, :, 0:GQA_HD], ra[c][:, :, 0:4], rb[c][:, :, 0:4], ALU.add).then_inc(sig["dve"][c], 1)
            for t in range(TILES):
                src = lambda r: r[c][:, t, 4:6].rearrange("p a (o k) -> p a o k", o=1).to_broadcast([P, GQA_KV, 2, GQA_HD])
                ins = dve.tensor_tensor(k4[c][:, t, :, 0:GQA_HD].rearrange("p (a o) k -> p a o k", o=2), src(ra), src(rb), ALU.add)
                if t < TILES - 1:
                    ins.then_inc(sig["dve"][c], 1)
            dve.wait_ge(sig["dve"][c], cnt("dve", TILES))
            show(ins, "parts")
            yield
            wait("q_turned")
            show(dve.tensor_copy(q4T[c][:], by[:, 0:S]), "qTa")
            yield
            for n in range(GQA_HEADS):
                wait("scores")
                b = (bs, bt)[n % 2]
                dve.tensor_reduce(q4[c][:, 0, n, GQA_HD:GQA_HD + 1], b[:, 0:P], X_AXIS, ALU.max, negate=True).then_inc(sig["dve"][c], 1)
                dve.tensor_reduce(q4[c][:, 1, n, GQA_HD:GQA_HD + 1], b[:, P:P + S], X_AXIS, ALU.max, negate=True
                                  ).then_inc(sig["max"][c], 1)
                cnt("dve")
                yield
            cnt("q_turned")
            yield
            for n in range(GQA_HEADS):
                yield
            wait("values")
            show(dve.tensor_copy(oT[c][:, 0, :], by[:, 0:S]), "oT")
            yield
            wait("o_turned")
            o = bs[:, 0:S].rearrange("p (n k) -> p n k", k=32)
            n_heads = TILES * GQA_HEADS
            link(dve.reciprocal(rden[c][:, 0:n_heads], o[:, :, GQA_HD]))
            show(dve.tensor_tensor(att[c][:].rearrange("p t (n k) -> p (t n) k", k=GQA_HD), o[:, :, 0:GQA_HD],
                                   rden[c][:, 0:n_heads].rearrange("p (n o) -> p n o", o=1).to_broadcast([P, n_heads, GQA_HD]),
                                   ALU.mult), "att")
            yield

            def route(bias, eps):
                wait("logits")
                l3 = bt[:, 0:TILES * EXPERTS].rearrange("p (t e) -> p t e", t=TILES)
                if bias:
                    link(dve.tensor_tensor(lo[c][:], l3, tile_bc(bias), ALU.add))
                else:
                    link(dve.tensor_copy(lo[c][:], l3))
                for t in range(TILES):
                    link(dve.max(top[c][:, t, :], lo[c][:, t, :]))
                for t in range(TILES):
                    link(dve.max_index(idx[c][:, t, :], top[c][:, t, :], lo[c][:, t, :]))
                link(dve.tensor_copy(idf[c][:], idx[c][:]))
                first = top[c][:, :, 0:1]
                link(dve.tensor_tensor(lg[c][:, :, 0:EXPERTS], lo[c][:], first.to_broadcast([P, TILES, EXPERTS]), ALU.subtract))
                show(dve.tensor_tensor(lg[c][:, :, EXPERTS:EXPERTS + 2], top[c][:, :, 0:2], first.to_broadcast([P, TILES, 2]),
                                       ALU.subtract), "lg")
                wait("ex")
                link(dve.tensor_reduce(sw[c][:, :, 0:1], ex[c][:, :, 0:EXPERTS], X_AXIS, ALU.add))
                link(dve.tensor_reduce(sw[c][:, :, 1:2], ex[c][:, :, EXPERTS:EXPERTS + 2], X_AXIS, ALU.add))
                link(dve.scalar_tensor_tensor(sw[c][:, :, 2:3], sw[c][:, :, 0:1], eps, sw[c][:, :, 1:2], ALU.mult, ALU.add))
                link(dve.reciprocal(sw[c][:, :, 3:4], sw[c][:, :, 2:3]))
                link(dve.tensor_tensor(sw[c][:, :, 0:2], ex[c][:, :, EXPERTS:EXPERTS + 2], sw[c][:, :, 3:4].to_broadcast([P, TILES, 2]),
                                       ALU.mult))
                for t in range(TILES):
                    for k, dst in enumerate((gates, g2)):
                        link(dve.tensor_scalar(dst[c][:, t, :], w("iota"), idf[c][:, t, k:k + 1], sw[c][:, t, k:k + 1],
                                               ALU.is_equal, ALU.mult))
                show(dve.tensor_tensor(gates[c][:], gates[c][:], g2[c][:], ALU.add), "gates")

            def take_moe():
                wait("moe")
                show(dve.tensor_copy(oT[c][:, 0, :], by[:, 0:S]), "oT")
                wait("o_turned")
                o = bs[:, 0:TILES * P].rearrange("p (t n) -> p t n", t=TILES)
                link(dve.tensor_tensor(h[c][:], h[c][:], o[:, :, 0:D], ALU.add))
                link(dve.tensor_tensor(h[c][:], h[c][:], o[:, :, D:2 * D], ALU.add))

            wait("proj")
            link(dve.tensor_tensor(xn[c][:], xn[c][:], bx[:, 0:TILES * D].rearrange("p (t d) -> p t d", t=TILES), ALU.add))
            link(dve.tensor_tensor(h[c][:], h[c][:], xn[c][:], ALU.add))
            rms_scaled(xn[c], "gqa_ln2")
            yield
            route(None, 1e-9)
            yield
            yield
            base = cnt.now("t2")
            for i in range(HID_TILES + 1):
                if i < HID_TILES:
                    wait("silu")
                    show(dve.tensor_tensor(t1[c][:, i % 2, :], act[c][:, i % 2, :], (bs, bt)[i % 2][:, S:2 * S], ALU.mult), "t1")
                    wait("wide")
                    if i >= 2:
                        pass
                    dve.tensor_tensor(t2[c][:, i % 2, :], t1[c][:, i % 2, :], bx[:, 0:S], ALU.mult).then_inc(sig["t2"][c], 1)
                yield
            take_moe()
            yield

            show(layer_norm(h[c], xn[c]), "xn")
            show(dve.tensor_tensor(h[c][:], h[c][:], tile_bc("one_bv"), ALU.add), "xn")
            yield
            cnt("scores", ATT_HEADS * 0 + GQA_HEADS)
            for t in range(TILES):
                wait("scores")
                dve.tensor_reduce(nm[c][:, t:t + 1], (bs, bt)[t][:, 0:S], X_AXIS, ALU.max, negate=True).then_inc(sig["max"][c], 1)
            yield
            wait("values")
            o = bx[:, 0:TILES * VS].rearrange("p (t e) -> p t e", e=VS)
            link(dve.reciprocal(rden[c][:, 0:TILES], o[:, :, D]))
            for t in range(TILES):
                link(dve.scalar_tensor_tensor(h[c][:, t, :], o[:, t, 0:D], rden[c][:, t:t + 1], h[c][:, t, :], ALU.mult, ALU.add))
            yield

            show(layer_norm(h[c], xn[c]), "dve")
            link(layer_norm(xn[c], s_[c]))
            link(dve.tensor_tensor(s_[c][:], s_[c][:], tile_bc("gelu_gamma"), ALU.mult))
            show(dve.tensor_tensor(hc[c][:], s_[c][:], tile_bc("gelu_beta"), ALU.add), "hc")
            route("gelu_br", 0.0)
            yield
            yield
            for i in range(EXPERTS + 1):
                if i < EXPERTS:
                    wait("gelu")
                    wait("wide")
                    dve.tensor_tensor(t2[c][:, i % 2, :], act[c][:, i % 2, :], bx[:, 0:S], ALU.mult).then_inc(sig["t2"][c], 1)
                yield
            take_moe()
            show(dve.tensor_copy(s_[c][:], h[c][:]), "final")
            yield

        def pool_chain(pool, c):
            cnt = Counts()

            def wait(name, k=1):
                pool.wait_ge(sig[name][c], cnt(name, k))

            def link(ins):
                ins.then_inc(sig["pool"][c], 1)
                pool.wait_ge(sig["pool"][c], cnt("pool"))

            def inv_sqrt(src, scale, eps):
                link(pool.tensor_scalar(var[c][:], src, scale, eps, ALU.mult, ALU.add))
                pool.tensor_tensor(rstd[c][:], var[c][:], minus_half[:], ALU.pow).then_inc(sig["rstd"][c], 1)

            def norm(eps):
                wait("mv", TILES)
                inv_sqrt(mv[c][:, :, 1], 1.0, eps)

            def bias(name, l):
                wait("h")
                v = w(name, l * D, (l + 1) * D).rearrange("p (o d) -> p o d", o=1).to_broadcast([P, TILES, D])
                pool.tensor_tensor(hb[c][:], h[c][:], v, ALU.add).then_inc(sig["hb"][c], 1)

            n_heads = TILES * TOK_HEADS
            for l in range(TOK_LAYERS):
                bias("tok_bo", l)
                wait("qk1")
                for a, dst, sl in ((1, kn, slice(1, 6, 2)), (0, qn, slice(0, 3))):
                    slots = dst[c][:, :, 0:SPLIT_ROWS].rearrange("p h (i k) -> p h i k", k=TOK_HD)[:, :, sl]
                    src = qk1[c][:, a].rearrange("p (h o k) -> p h o k", o=1, k=TOK_HD).to_broadcast([P, n_heads, 3, TOK_HD])
                    pool.tensor_copy(slots, src).then_inc(sig["parts_p"][c], 1)
                yield
                yield
                for n in range(TOK_HEADS):
                    yield
                yield
                for n in range(TOK_HEADS):
                    yield
                yield
                yield
                norm(1e-3)
                bias("tok_b2", l)
                yield
                yield
                yield
                norm(1e-3)
                yield
            norm(1e-5)
            yield
            for n in range(ATT_HEADS):
                yield
            yield
            for n in range(ATT_HEADS):
                yield
            yield
            norm(1e-5)
            wait("ss", TILES)
            inv_sqrt(ss[c][:], 1.0 / D, 1e-6)
            yield
            yield
            for n in range(2 * GQA_HEADS + 1):
                yield
            yield
            yield
            wait("ss", TILES)
            inv_sqrt(ss[c][:], 1.0 / D, 1e-6)
            yield
            yield
            yield
            for i in range(HID_TILES + 1):
                yield
            yield
            norm(1e-5)
            yield
            yield
            yield
            norm(1e-5)
            norm(1e-5)
            yield

        def sp_chain(sp, c, g):
            cnt = Counts()
            for turn_ in range(2):
                sp.wait_ge(sig["nmT"][c], turn_ + 1)
                heads = (ATT_HEADS, 1)[turn_]
                sp.dma_start(rT[c][D:VS, 0:heads, :].rearrange("o n (t p) -> o (n t) p", p=P),
                             nmT[c][0:heads * TILES, :]).then_inc(sig["max_row"][c], 16)
                yield
            sp.wait_ge(sig["final"][c], 1)
            sp.dma_start(out_v[:, bass.ds(g * (CHAINS * TILES) + c * TILES, TILES), :], s_[c][:]).then_inc(sig["stored"][c], 16)
            sp.wait_ge(sig["stored"][c], 16)
            yield

        with nc.Fori(0, BATCH // CHAINS) as g:
            with nc.Block() as block:
                @block.tensor
                def _(pe):
                    in_turns([pe_chain(pe, c) for c in range(CHAINS)], LAG)

                @block.scalar
                def _(eng):
                    in_turns([act_chain(eng, c) for c in range(CHAINS)], LAG)

                @block.vector
                def _(dve):
                    in_turns([dve_chain(dve, c, g) for c in range(CHAINS)], LAG)

                @block.gpsimd
                def _(pool):
                    in_turns([pool_chain(pool, c) for c in range(CHAINS)], LAG)

                @block.sync
                def _(sp):
                    in_turns([sp_chain(sp, c, g) for c in range(CHAINS)], 0)

            with nc.Block() as block:
                @block.sync
                def _(sp):
                    sp.sem_clear(range(sig.first.num, sig.last.num + 1))


def kernel(**inputs):
    import concourse.bacc as _bacc
    from concourse.bass_utils import run_bass_kernel_spmd as _run

    nc = _bacc.Bacc("TRN2", target_bir_lowering=False, num_devices=1)
    laid = {k: np.ascontiguousarray(v) for k, v in pack(inputs).items()}
    shapes = {k: v.shape for k, v in laid.items()}
    arrays, packed = {}, {}
    for parts in sorted({p for p, _ in shapes.values()}):
        a = np.concatenate([v for v in laid.values() if v.shape[0] == parts], axis=1)
        arrays[f"packed{parts}"] = a
        packed[parts] = nc.dram_tensor(f"packed{parts}", a.shape, F32, kind="ExternalInput").ap()
    arrays["x"] = np.ascontiguousarray(np.asarray(inputs["x"]).reshape(BATCH * TILES, P).T)
    arrays["table"] = np.ascontiguousarray(inputs["L0_tok_emb"])
    x = nc.dram_tensor("x", arrays["x"].shape, I32, kind="ExternalInput").ap()
    table = nc.dram_tensor("table", arrays["table"].shape, F32, kind="ExternalInput").ap()
    out = nc.dram_tensor("out", (BATCH, S, D), F32, kind="ExternalOutput").ap()
    tower(nc, x, table, packed, shapes, out)
    r = _run(nc, [arrays], core_ids=[0])
    return r.results[0]["out"]
```

```python
from contextlib import ExitStack

import concourse.bass as bass
from concourse import mybir
import numpy as np

ALU = mybir.AluOpType
ACT = mybir.ActivationFunctionType
F32 = mybir.dt.float32
BF16 = mybir.dt.bfloat16
I32 = mybir.dt.int32
U32 = mybir.dt.uint32
X_AXIS = mybir.AxisListType.X

P = 128
D = 64
S = 256
TILES = S // P
BATCH = 8
CHAINS = 2
TOK_LAYERS, TOK_HEADS, TOK_HD = 4, 8, 8
FFN = 4 * D
PAIRS = TOK_HEADS // 2
SLOT = 64
Q_PARTS = [1, 1, 1, 2, 2, 3]
K_PARTS = [3, 1, 2, 1, 2, 1]
TERMS = len(Q_PARTS)
SPLIT_ROWS = TERMS * TOK_HD
ROWS = SPLIT_ROWS + 3
ATT_HEADS = 8
GQA_HEADS, GQA_KV, GQA_HD = 4, 2, 16
EXPERTS = 8
GATE_ROWS = 3 * EXPERTS
HID = 170
HID_TILES = -(-EXPERTS * HID // P)
VS = D + 1
CAUSAL = P + S
MASKED = -1e30



def constants():
    pos = np.arange(S).reshape(-1, 1)
    depth = np.array([2 * (i // 2) for i in range(D)]).reshape(1, -1)
    angle = pos * (1.0 / 10000.0 ** (depth / D))
    enc = np.cos(angle)
    enc[:, ::2] = np.sin(enc[:, ::2])
    enc = enc.astype(np.float32).reshape(TILES, P, D).transpose(1, 0, 2)
    inv = 1.0 / 10000.0 ** (np.arange(0, GQA_HD, 2, dtype=np.float32) / GQA_HD)
    freq = np.outer(np.arange(S, dtype=np.float32), inv)
    emb = np.concatenate([freq, freq], axis=-1)
    cos, sin = np.cos(emb).astype(np.float32), np.sin(emb).astype(np.float32)
    sin[:, :GQA_HD // 2] *= -1
    tile = lambda a: a.reshape(TILES, P, GQA_HD).transpose(1, 0, 2).reshape(P, -1)
    iota = np.tile(np.arange(EXPERTS, dtype=np.float32), (P, 1))
    later = np.triu(np.ones((P, P), np.float32), 1) * MASKED
    sel = np.zeros((EXPERTS, HID_TILES, P), np.float32)
    for j in range(EXPERTS * HID):
        sel[j // HID, j // P, j % P] = 1
    sel_e = np.zeros((EXPERTS, EXPERTS, P), np.float32)
    for e in range(EXPERTS):
        sel_e[e, e] = 1
    return {
        "eye": np.eye(P, dtype=np.float32), "enc": enc.reshape(P, -1), "cos": tile(cos), "sin": tile(sin),
        "iota": iota, "later": later, "later_t": np.ascontiguousarray(later.T),
        "sel": np.tile(np.concatenate([sel.reshape(EXPERTS, -1), sel_e.reshape(EXPERTS, -1)], axis=1), (3, 1)),
    }


def rows(a):
    return np.broadcast_to(np.asarray(a).reshape(1, -1), (P, np.asarray(a).size))


def pack(i):
    a = {k: np.asarray(v) for k, v in i.items()}
    wq = a["L0_tok_wq"].transpose(2, 0, 1, 3).reshape(D, TOK_LAYERS, D)
    wk = a["L0_tok_wk"].transpose(2, 0, 1, 3).reshape(D, TOK_LAYERS, D)
    wv = a["L0_tok_wv"].transpose(2, 0, 1, 3).reshape(D, TOK_LAYERS, D)
    pad = HID_TILES * P - EXPERTS * HID
    flat = lambda w: np.pad(w.reshape(EXPERTS * HID, D), ((0, pad), (0, 0)))
    w2 = np.pad(a["L0_ffn_w2"].transpose(0, 2, 1).reshape(EXPERTS * HID, D), ((0, pad), (0, 0)))
    row = lambda w, b=None: np.concatenate([w, np.zeros((1, w.shape[1]), w.dtype) if b is None else b.reshape(1, -1)], axis=0)
    out = {
        "tok_qkv": row(np.concatenate([wq, wk, wv], axis=2).reshape(D, -1)),
        "tok_wo": row(a["L0_tok_wo"].transpose(1, 0, 2).reshape(D, -1), a["L0_tok_bo"]),
        "tok_w1": row(a["L0_tok_w1"].transpose(1, 0, 2).reshape(D, -1), a["L0_tok_b1"]),
        "gqa_qkv": row(np.concatenate([a["L0_ffn_wq"], a["L0_ffn_wk"], a["L0_ffn_wv"]], axis=0).T),
        "gqa_wo": row(a["L0_ffn_wo"].T),
        "moe_router": row(a["L0_ffn_router_w"].T),
        "moe_w1": row(flat(a["L0_ffn_w1"]).T), "moe_w3": row(flat(a["L0_ffn_w3"]).T),
        "one_wq": row(a["L1_attn_Wq"], a["L1_attn_bq"]), "one_wk": row(a["L1_attn_Wk"], a["L1_attn_bk"]),
        "one_wv": row(a["L1_attn_Wv"], a["L1_attn_bv"]),
        "gelu_router": row(a["L1_ffn_Wr"], a["L1_ffn_br"]),
        "gelu_w1": row(a["L1_ffn_W1"].transpose(1, 0, 2).reshape(D, -1), a["L1_ffn_b1"]),
        "tok_w2": a["L0_tok_w2"].reshape(TOK_LAYERS, 2, P, D).transpose(2, 0, 1, 3).reshape(P, -1),
        "tok_b2": rows(a["L0_tok_b2"]),
        "tok_gamma": rows(a["L0_tok_gamma"]), "tok_beta": rows(a["L0_tok_beta"]),
        "att_k": a["L0_attn_key_matrices"].transpose(2, 0, 1).reshape(D, -1),
        "att_q": a["L0_attn_query_matrices"].transpose(2, 0, 1).reshape(D, -1),
        "att_vi": a["L0_attn_value_in_matrices"].transpose(2, 0, 1).reshape(D, -1),
        "att_vo": a["L0_attn_value_out_matrices"].transpose(1, 0, 2).reshape(D, -1),
        "gqa_ln1": rows(a["L0_ffn_ln1_w"]), "gqa_ln2": rows(a["L0_ffn_ln2_w"]),
        "moe_w2": w2.reshape(HID_TILES, P, D).transpose(1, 0, 2).reshape(P, -1),
        "gelu_gamma": rows(a["L1_ffn_gamma"]), "gelu_beta": rows(a["L1_ffn_beta"]),
        "gelu_w2": a["L1_ffn_W2"].transpose(1, 0, 2).reshape(P, -1),
        "gelu_b2": np.tile(a["L1_ffn_b2"], (3, 1)),
    }
    out.update(constants())
    return out


def columns(shapes, parts):
    at, found = 0, {}
    for name, (p, n) in shapes.items():
        if p == parts:
            found[name] = (at, n)
            at += n
    return found, at


class Counts:

    def __init__(self):
        self.n = {}

    def __call__(self, name, k=1):
        self.n[name] = self.n.get(name, 0) + k
        return self.n[name]

    def now(self, name):
        return self.n.get(name, 0)


class Signals:

    def __init__(self, nc, ctx):
        self.nc, self.ctx, self.made, self.first, self.last = nc, ctx, {}, None, None

    def __getitem__(self, name):
        if name not in self.made:
            self.made[name] = [self.ctx.enter_context(self.nc.semaphore(f"{name}{c}")) for c in range(CHAINS)]
            self.first = self.first or self.made[name][0]
            self.last = self.made[name][-1]
        return self.made[name]


TOK_STEPS = ([1.6, 1.6, 3.0, 2.5] + [0.7] * TOK_HEADS + [1.2, 1.5] + [0.7] * TOK_HEADS
             + [1.5, 1.5, 0.8, 0.8, 2.5, 1.0, 0.8, 1.5, 1.0, 2.5, 1.0])
CAUSAL_STEPS = [2.0, 1.0, 6.0] + [1.0] * ATT_HEADS + [3.0] + [1.6] * ATT_HEADS + [3.0]
GQA_STEPS = [2.0, 2.0, 1.0, 2.0, 3.0, 2.0] + [1.0] * GQA_HEADS + [1.5] + [1.0] * GQA_HEADS + [1.5, 1.5, 1.0, 2.0]
SILU_STEPS = [1.0, 1.5, 5.0, 1.5] + [1.4] * (HID_TILES + 2) + [2.5]
ONE_STEPS = [1.5, 3.0, 3.0, 2.0, 3.0]
GELU_STEPS = [2.0, 1.0, 1.0, 1.5, 5.0, 1.5] + [1.0] * (EXPERTS + 2) + [2.5]
STEPS = TOK_LAYERS * TOK_STEPS + CAUSAL_STEPS + GQA_STEPS + SILU_STEPS + ONE_STEPS + GELU_STEPS


def in_turns(programs, lag, steps):
    at = [c * lag for c in range(len(programs))]
    taken = [0] * len(programs)
    while min(taken) < len(steps):
        c = min((c for c in range(len(programs)) if taken[c] < len(steps)), key=lambda c: (at[c], c))
        next(programs[c])
        at[c] += steps[taken[c]]
        taken[c] += 1
    assert all(next(p, "end") == "end" for p in programs)


def tower(nc, x, table, packed, shapes, out, LAG=0):
    with ExitStack() as ctx:
        def sb(name, shape, dt=F32):
            return ctx.enter_context(nc.sbuf_tensor(name, shape, dt))

        def sem(name):
            return ctx.enter_context(nc.semaphore(name))

        pr = [sb(f"pr{c}", [P, 8, 2 * S]) for c in range(CHAINS)]

        W = {}
        early = {D: pr[0], GATE_ROWS: pr[1]}
        for parts, dram in packed.items():
            at, n = columns(shapes, parts)
            if parts in early:
                t = early[parts][:].rearrange("p a b -> p (a b)")[0:parts, 0:n]
            else:
                t = sb(f"resident{parts}", [P if parts == VS else parts, n])
            W.update({k: (t, a, m) for k, (a, m) in at.items()})
            W[parts] = t

        def w(name, a=0, b=None):
            t, at, n = W[name]
            return t[:, at + a:at + (n if b is None else b)]

        eye = w("eye")
        eye_b = sb("eye_b", [P, P], BF16)
        later_b = sb("later_b", [P, 2, P], BF16)
        n_sel = W["sel"][2]
        sel_b = sb("sel_b", [P, n_sel], BF16)
        b2_b = sb("b2_b", [P, 3, D], BF16)
        b2_rest = sb("b2_rest", [GATE_ROWS, 2, D])
        att_g = sb("att_g", [P, ATT_HEADS, D])
        att_v = sb("att_v", [P, ATT_HEADS, D])
        ids = sb("ids", [P, BATCH * TILES], I32)
        tokens = sb("tokens", [P, BATCH * TILES, D])
        minus_half = sb("minus_half", [P, TILES])

        def per(name, shape, dt=F32):
            return [sb(f"{name}{c}", shape, dt) for c in range(CHAINS)]

        h = per("h", [P, TILES, D])
        hb = per("hb", [P, TILES, D])
        s_ = per("s_", [P, TILES, D])
        xn = per("xn", [P, TILES, D])
        hc = per("hc", [P, TILES, D])
        stats = per("stats", [P, TILES, 6])
        mv = per("mv", [P, TILES, 2])
        var = per("var", [P, TILES])
        rstd = per("rstd", [P, TILES])
        hT = per("hT", [P, S])
        qk1 = per("qk1", [P, 2, TILES * D], BF16)
        qk2 = per("qk2", [P, 2, TILES * D], BF16)
        rest = per("rest", [P, 2, TILES * D])
        qn = per("qn", [P, TILES * TOK_HEADS, SLOT], BF16)
        kn = per("kn", [P, TILES * TOK_HEADS, SLOT], BF16)
        qTa = per("qTa", [P, PAIRS, S], BF16)
        qTb = per("qTb", [P, PAIRS, S], BF16)
        kT = per("kT", [P, PAIRS, 2, S], BF16)
        nm = per("nm", [P, TILES * TOK_HEADS])
        nr = per("nr", [P, TILES * TOK_HEADS])
        v8 = per("v8", [P, TILES, TOK_HEADS, 32])
        oT = per("oT", [P, 2, S])
        rden = per("rden", [P, TILES * TOK_HEADS])
        att = per("att", [P, TILES, D])
        aT = per("aT", [P, S])
        hid = per("hid", [P, 2, S])
        rT = per("rT", [P, ATT_HEADS, S])
        nmT = per("nmT", [TILES * ATT_HEADS, P])
        vb = per("vb", [P, TILES, ATT_HEADS, VS])
        ob = per("ob", [P, TILES, ATT_HEADS, D])
        ss = per("ss", [P, TILES])
        q4 = per("q4", [P, TILES, GQA_HEADS, 32])
        k4 = per("k4", [P, TILES, GQA_HEADS, 32])
        q4T = per("q4T", [P, S])
        k4T = per("k4T", [P, GQA_HEADS, S])
        v4 = per("v4", [P, TILES, GQA_KV, 32])
        ra = per("ra", [P, TILES, 6, GQA_HD])
        rb = per("rb", [P, TILES, 6, GQA_HD])
        lg = per("lg", [P, TILES, EXPERTS + 2])
        lo = per("lo", [P, TILES, EXPERTS])
        top = per("top", [P, TILES, 8])
        idx = per("idx", [P, TILES, 8], U32)
        idf = per("idf", [P, TILES, 8])
        ex = per("ex", [P, TILES, EXPERTS + 2])
        sw = per("sw", [P, TILES, 4])
        gates = per("gates", [P, TILES, EXPERTS])
        g2 = per("g2", [P, TILES, EXPERTS])
        gp = per("gp", [P, TILES, GATE_ROWS], BF16)
        gT = per("gT", [P, S], BF16)
        act = per("act", [P, 2, S])
        t1 = per("t1", [P, 2, S])
        t2 = per("t2", [P, 2, S])

        bank = [[ctx.enter_context(nc.psum_tensor(f"bank{k}{c}", [P, 512], F32)) for k in "stxy"] for c in range(CHAINS)]

        sig = Signals(nc, ctx)
        loaded, cleared, gathered = sem("loaded"), sem("cleared"), sem("gathered")
        folded_pe, folded, constant, b2_split = sem("folded_pe"), sem("folded"), sem("constant"), sem("b2_split")

        with nc.Block() as block:
            n_loads = len(packed) + 1

            @block.sync
            def _(sp):
                sp.dma_start(ids[:], x).then_inc(loaded, 16)
                for parts, dram in sorted(packed.items(), key=lambda kv: kv[0] == VS):
                    if parts == VS:
                        sp.wait_ge(cleared, 1)
                    sp.dma_start(W[parts][0:parts], dram).then_inc(loaded, 16)
                sp.wait_ge(loaded, 16 * n_loads)

            @block.gpsimd
            def _(pool):
                pool.wait_ge(loaded, 16 * n_loads)
                for n in range(BATCH * TILES):
                    pool.indirect_dma_start(
                        out=tokens[:, n, :], out_offset=None, in_=table[:, :],
                        in_offset=bass.IndirectOffsetOnAxis(ap=ids[:, n:n + 1], axis=0)).then_inc(gathered, 16)
                for c in range(CHAINS):
                    pool.memset(qn[c][:], 0.0)
                    pool.memset(kn[c][:, :, ROWS:SLOT], 0.0)
                    pool.memset(kn[c][:, :, SPLIT_ROWS:ROWS], 1.0)
                    pool.memset(kT[c][:], 0.0)
                    pool.memset(v8[c][:, :, :, TOK_HD + 1:32], 0.0)
                    pool.memset(v8[c][:, :, :, TOK_HD:TOK_HD + 1], 1.0)
                    pool.memset(vb[c][:, :, :, D:VS], 1.0)
                    pool.memset(q4[c][:], 0.0)
                    pool.memset(k4[c][:, :, :, GQA_HD + 1:32], 0.0)
                    pool.memset(k4[c][:, :, :, GQA_HD:GQA_HD + 1], 1.0)
                    pool.memset(v4[c][:, :, :, GQA_HD + 1:32], 0.0)
                    pool.memset(v4[c][:, :, :, GQA_HD:GQA_HD + 1], 1.0)
                pool.memset(minus_half[:], -0.5)
                pool.wait_ge(gathered, 16 * BATCH * TILES)

            @block.vector
            def _(dve):
                dve.memset(W[VS][D:P, :], 0.0).then_inc(cleared, 1)
                n = 0
                for c in range(CHAINS):
                    for b in (hT, aT, rT, gT, k4T):
                        rows_ = slice(0, P) if b in (gT, k4T) else slice(D, P)
                        dve.memset(b[c][rows_], 0.0).then_inc(constant, 1)
                        n += 1
                for b in (att_g, att_v):
                    dve.memset(b[D:P], 0.0).then_inc(constant, 1)
                dve.memset(sel_b[:], 0.0).then_inc(constant, 1)
                dve.memset(b2_b[:], 0.0).then_inc(constant, 1)
                dve.wait_ge(constant, n + 4)
                for c in range(CHAINS):
                    dve.memset(hT[c][D:VS, :], 1.0)
                    dve.memset(aT[c][D:VS, :], 1.0)
                dve.wait_ge(loaded, 16 * n_loads)
                dve.tensor_copy(eye_b[:], eye)
                dve.tensor_copy(later_b[:, 0, :], w("later"))
                dve.tensor_copy(later_b[:, 1, :], w("later_t"))
                dve.tensor_copy(sel_b[0:GATE_ROWS, :], w("sel"))
                src = w("gelu_b2")
                for k in range(3):
                    dve.tensor_copy(b2_b[0:GATE_ROWS, k, :], src).then_inc(b2_split, 1)
                    dve.wait_ge(b2_split, 2 * k + 1)
                    if k < 2:
                        dve.tensor_tensor(b2_rest[:, k, :], src, b2_b[0:GATE_ROWS, k, :], ALU.subtract).then_inc(b2_split, 1)
                        dve.wait_ge(b2_split, 2 * k + 2)
                        src = b2_rest[:, k, :]
                for k, dst in enumerate((att_g, att_v)):
                    dve.wait_ge(folded_pe, k + 1)
                    dve.tensor_copy(dst[0:D], bank[0][k][0:D, :].rearrange("p (n e) -> p n e", n=ATT_HEADS)).then_inc(folded, 1)
                dve.wait_ge(folded, 2)

            @block.tensor
            def _(pe):
                pe.wait_ge(loaded, 16 * n_loads)
                for k, (left, right) in enumerate((("att_k", "att_q"), ("att_vi", "att_vo"))):
                    for n in range(ATT_HEADS):
                        last = pe.matmul(bank[0][k][0:D, n * D:(n + 1) * D], w(left, n * D, (n + 1) * D),
                                         w(right, n * D, (n + 1) * D), start=True, stop=True)
                    last.then_inc(folded_pe, 1)

        out_v = out.rearrange("b (t p) d -> p (b t) d", p=P)

        def pe_chain(pe, c):
            cnt = Counts()
            bs, bt, bx, by = bank[c]

            def wait(name, k=1):
                pe.wait_ge(sig[name][c], cnt(name, k))

            def turn(src, dst):
                for t in range(TILES):
                    last = pe.transpose(dst[0:D, t * P:(t + 1) * P], src[:, t, :], eye)
                last.then_inc(sig["turned"][c], 1)

            def natural(dst, lhs, rhs, done):
                n = rhs.shape[-1]
                for t in range(TILES):
                    last = pe.matmul(dst[:, t * n:(t + 1) * n], lhs[:, t * P:(t + 1) * P], rhs, start=True, stop=True)
                last.then_inc(sig[done][c], 1)

            def turn_pairs(src, dst, done):
                d = dst[:].bitcast(BF16).rearrange("p (q s) -> p q s", q=PAIRS)
                for q in range(PAIRS):
                    for t in range(TILES):
                        h0 = t * TOK_HEADS + 2 * q
                        last = pe.transpose(d[:, q, t * P:(t + 1) * P],
                                            src[:, h0:h0 + 2, :].rearrange("p a b -> p (a b)"), eye_b[:])
                last.then_inc(sig[done][c], 1)

            for l in range(TOK_LAYERS):
                wait("h", TILES)
                turn(h[c], bx)
                yield
                wait("hT")
                natural(by, hT[c], w("tok_qkv", l * 3 * D, (l + 1) * 3 * D), "qkv")
                yield
                yield
                wait("parts")
                wait("parts_p", 2)
                turn_pairs(kn[c], by, "k_turned")
                if l > 0:
                    wait("max_clear")
                turn_pairs(qn[c], bx, "q_turned")
                yield
                wait("kT", 2)
                wait("qTa")
                for n in range(TOK_HEADS):
                    if n >= 2:
                        pe.wait_ge(sig["max"][c], cnt.now("max") + n - 1)
                    for t in range(TILES):
                        last = pe.matmul((bs, bt)[n % 2][:, t * S:(t + 1) * S], qTa[c][:, n // 2, t * P:(t + 1) * P],
                                         kT[c][:, n // 2, n % 2, :], start=True, stop=True)
                    last.then_inc(sig["scores"][c], 1)
                    yield
                cnt("max", TOK_HEADS)
                yield
                wait("max_split")
                turn_pairs(qn[c], bx, "q_turned")
                yield
                wait("qTb")
                base = cnt.now("exp")

                def values(half):
                    pe.wait_ge(sig["exp"][c], base + 4 * half + 4)
                    for t in range(TILES):
                        for j in range(4):
                            last = pe.matmul((by, bx)[half][32 * j:32 * j + 32, 0:S], v8[c][:, t, 4 * half + j, :],
                                             pr[c][:, 4 * half + j, t * S:(t + 1) * S], start=(t == 0), stop=(t == 1),
                                             tile_position=(0, 32 * j), skip_group_check=True)
                    last.then_inc(sig["values"][c], 1)

                wait("v8")
                for n in range(TOK_HEADS):
                    if n >= 2:
                        pe.wait_ge(sig["exp"][c], base + n - 1)
                    for t in range(TILES):
                        last = pe.matmul((bs, bt)[n % 2][:, t * S:(t + 1) * S], kT[c][:, n // 2, n % 2, t * P:(t + 1) * P],
                                         qTb[c][:, n // 2, :], start=True, stop=True)
                    last.then_inc(sig["scores"][c], 1)
                    if n == 5:
                        values(0)
                    yield
                values(1)
                cnt("exp", TOK_HEADS)
                yield
                wait("oT", 2)
                for half in range(2):
                    for t in range(TILES):
                        last = pe.transpose(bs[:, (t * 2 + half) * P:(t * 2 + half + 1) * P],
                                            oT[c][:, half, t * P:(t + 1) * P], eye)
                last.then_inc(sig["o_turned"][c], 1)
                yield
                wait("att")
                turn(att[c], bt)
                yield
                wait("aT")
                natural(bx, aT[c], w("tok_wo", l * D, (l + 1) * D), "proj")
                yield
                yield
                yield
                wait("h", TILES)
                turn(h[c], bx)
                yield
                wait("hT")
                for m in range(2):
                    pe.matmul((by, bs)[m][:, 0:S], w("tok_w1", l * FFN + m * P, l * FFN + (m + 1) * P), hT[c][:],
                              start=True, stop=True).then_inc(sig["ffn"][c], 1)
                yield
                wait("hid_a")
                wait("hid_v")
                for t in range(TILES):
                    for m in range(2):
                        last = pe.matmul(bt[:, t * D:(t + 1) * D], hid[c][:, m, t * P:(t + 1) * P],
                                         w("tok_w2", (l * 2 + m) * D, (l * 2 + m + 1) * D), start=(m == 0), stop=(m == 1))
                last.then_inc(sig["proj"][c], 1)
                yield
                yield
                yield

            yield
            yield
            wait("xn", TILES)
            turn(xn[c], bx)
            wait("hT")
            for i in range(4):
                if i >= 2:
                    pe.wait_ge(sig["rT"][c], i - 1)
                for j in range(2):
                    last = pe.matmul((by, bx)[i % 2][0:D, j * S:(j + 1) * S], att_g[:, 2 * i + j, :], hT[c][:],
                                     start=True, stop=True)
                last.then_inc(sig["row_side"][c], 1)
                if i < TILES:
                    pe.matmul((bs, bt)[i][:], hT[c][:, i * P:(i + 1) * P], att_v[:].rearrange("p n e -> p (n e)"),
                              start=True, stop=True).then_inc(sig["v_side"][c], 1)
            yield
            pe.wait_ge(sig["rT"][c], 4)
            pe.wait_ge(sig["vb"][c], 2)

            def causal_natural(dst, lhs, rhs):
                pe.matmul(dst[:, 0:P], lhs(0), rhs(0, P), start=True, stop=False, skip_group_check=True)
                pe.matmul(dst[:, 0:P], eye_b[:], later_b[:, 0, :], start=False, stop=True, skip_group_check=True)
                pe.matmul(dst[:, P:P + S], lhs(1), rhs(0, S), start=True, stop=False, skip_group_check=True)
                return pe.matmul(dst[:, S:S + P], eye_b[:], later_b[:, 0, :], start=False, stop=True, skip_group_check=True)

            def causal_turned(dst, lhs, rhs):
                pe.matmul(dst[:, 0:S], lhs(0), rhs(0, S), start=True, stop=False, skip_group_check=True)
                pe.matmul(dst[:, 0:P], eye_b[:], later_b[:, 1, :], start=False, stop=True, skip_group_check=True)
                pe.matmul(dst[:, S:S + P], lhs(1), rhs(P, S), start=True, stop=False, skip_group_check=True)
                return pe.matmul(dst[:, S:S + P], eye_b[:], later_b[:, 1, :], start=False, stop=True, skip_group_check=True)

            for n in range(ATT_HEADS):
                if n >= 2:
                    pe.wait_ge(sig["max"][c], cnt.now("max") + n - 1)
                causal_natural((bs, bt)[n % 2], lambda t: rT[c][0:D, n, t * P:(t + 1) * P],
                               lambda a, b: hT[c][0:D, a:b]).then_inc(sig["scores"][c], 1)
                yield
            wait("max", ATT_HEADS)
            pe.transpose(bx[0:TILES * ATT_HEADS, 0:P], nm[c][:], eye).then_inc(sig["turned"][c], 1)
            yield
            wait("max_row", 16)
            base = cnt.now("exp")

            def values_natural(n):
                pe.wait_ge(sig["exp"][c], base + n + 1)
                if n == 4:
                    pe.wait_ge(sig["ob"][c], 2)
                k = n % 4
                pe.matmul(bx[:, k * VS:(k + 1) * VS], pr[c][:, n, 0:P], vb[c][:, 0, n, :], start=True, stop=True)
                pe.matmul(by[:, k * VS:(k + 1) * VS], pr[c][:, n, P:S], vb[c][:, 0, n, :], start=True, stop=False)
                last = pe.matmul(by[:, k * VS:(k + 1) * VS], pr[c][:, n, S:S + P], vb[c][:, 1, n, :], start=False, stop=True)
                if k == 3:
                    last.then_inc(sig["values"][c], 1)

            for n in range(ATT_HEADS):
                if n >= 2:
                    pe.wait_ge(sig["exp"][c], base + n - 1)
                causal_turned((bs, bt)[n % 2], lambda t: hT[c][:, t * P:(t + 1) * P],
                              lambda a, b: rT[c][:, n, a:b]).then_inc(sig["scores"][c], 1)
                if n >= 2:
                    values_natural(n - 2)
                yield
            values_natural(ATT_HEADS - 2)
            values_natural(ATT_HEADS - 1)
            cnt("exp", ATT_HEADS)
            yield

            yield
            yield
            yield
            wait("hc", TILES)
            turn(hc[c], bs)
            wait("hT")
            natural(bt, hT[c], w("gqa_qkv"), "qkv")
            yield
            yield
            wait("parts")
            wait("max_clear", 2)
            for src, dst, done in ((k4, bx, "k_turned"), (q4, by, "q_turned")):
                for t in range(TILES):
                    last = pe.transpose(dst[:, t * P:(t + 1) * P], src[c][:, t].rearrange("p a b -> p (a b)"), eye)
                last.then_inc(sig[done][c], 1)
            yield
            wait("kT", GQA_HEADS)
            wait("qTa")
            for n in range(GQA_HEADS):
                if n >= 2:
                    pe.wait_ge(sig["max"][c], cnt.now("max") + n - 1)
                causal_natural((bs, bt)[n % 2], lambda t: q4T[c][:, t * P:(t + 1) * P],
                               lambda a, b: k4T[c][:, n, a:b]).then_inc(sig["scores"][c], 1)
                yield
            wait("max", GQA_HEADS)
            for t in range(TILES):
                last = pe.transpose(by[:, t * P:(t + 1) * P], q4[c][:, t].rearrange("p a b -> p (a b)"), eye)
            last.then_inc(sig["q_turned"][c], 1)
            yield
            wait("qTb")
            for n in range(GQA_HEADS):
                if n >= 2:
                    pe.wait_ge(sig["exp"][c], cnt.now("exp") + n - 1)
                causal_turned((bs, bt)[n % 2], lambda t: k4T[c][:, n, t * P:(t + 1) * P],
                              lambda a, b: q4T[c][:, a:b]).then_inc(sig["scores"][c], 1)
                yield
            wait("exp", GQA_HEADS)
            for t in range(TILES):
                for j in range(GQA_HEADS):
                    cols = (slice(0, S), slice(P, S))[t]
                    last = pe.matmul(by[32 * j:32 * j + 32, cols], v4[c][:, t, j // 2, :],
                                     pr[c][:, j, (0, S)[t]:(S, S + P)[t]], start=(t == 0), stop=(t == 1),
                                     tile_position=(0, 32 * j), skip_group_check=True)
            last.then_inc(sig["values"][c], 1)
            yield
            wait("oT")
            for t in range(TILES):
                last = pe.transpose(bs[:, t * P:(t + 1) * P], oT[c][:, 0, t * P:(t + 1) * P], eye)
            last.then_inc(sig["o_turned"][c], 1)
            yield
            wait("att")
            turn(att[c], bt)
            yield
            wait("aT")
            natural(bx, aT[c], w("gqa_wo"), "proj")
            yield

            def mixture(router, up, down, tiles, sel_at, bank_free, bias=None):
                yield
                wait("hc", TILES)
                turn(hc[c], bs)
                wait("hT")
                natural(bt, hT[c], w(router), "logits")
                yield
                yield
                wait("gates")
                for t in range(TILES):
                    last = pe.transpose(bx[:].bitcast(BF16)[0:GATE_ROWS, t * P:(t + 1) * P], gp[c][:, t, :], eye_b[:])
                last.then_inc(sig["turned"][c], 1)
                wait("gT")
                yield
                free = cnt.now(bank_free)
                done = cnt.now("t2")
                for i in range(tiles + 2):
                    if i < tiles:
                        if i >= 2:
                            pe.wait_ge(sig[bank_free][c], free + i - 1)
                        for k, name in enumerate(up):
                            last = pe.matmul((bs, bt)[i % 2][:, k * S:(k + 1) * S], w(name, i * P, (i + 1) * P), hT[c][:],
                                             start=True, stop=True)
                        last.then_inc(sig["up"][c], 1)
                    if i >= 2:
                        k = i - 2
                        wait("t2")
                        half = k % 2
                        last = pe.matmul(by[D * half:D * half + D, 0:S], w(down, k * D, (k + 1) * D), t2[c][:, half, :],
                                         start=(k < 2), stop=(k >= tiles - 2 and bias is None),
                                         tile_position=(0, D * half), skip_group_check=True)
                    if 1 <= i <= tiles:
                        k = i - 1
                        pe.matmul(bx[:, 0:S], sel_b[:, sel_at + k * P:sel_at + (k + 1) * P], gT[c][:], start=True, stop=True
                                  ).then_inc(sig["wide"][c], 1)
                    if i < tiles + 1:
                        yield
                if bias is not None:
                    for k in range(3):
                        last = pe.matmul(by[0:D, 0:S], bias[:, k, :], gT[c][:], start=False, stop=(k == 2), skip_group_check=True)
                last.then_inc(sig["moe"][c], 1)
                yield
                wait("oT")
                for t in range(TILES):
                    last = pe.transpose(bs[:, t * P:(t + 1) * P], oT[c][:, 0, t * P:(t + 1) * P], eye)
                last.then_inc(sig["o_turned"][c], 1)

            yield from mixture("moe_router", ("moe_w1", "moe_w3"), "moe_w2", HID_TILES, 0, "t1")
            yield

            yield
            wait("xn", TILES)
            turn(xn[c], bx)
            wait("hT")
            for dst, name in ((by, "one_wq"), (bt, "one_wk")):
                pe.matmul(dst[0:D, 0:S], w(name), hT[c][:], start=True, stop=True).then_inc(sig["row_side"][c], 1)
            natural(bx, hT[c], w("one_wv"), "v_side")
            yield
            pe.wait_ge(sig["rT"][c], 5)
            pe.wait_ge(sig["vb"][c], 3)
            wait("kT")
            for t in range(TILES):
                pe.matmul((bs, bt)[t][:, 0:S], rT[c][0:D, 0, t * P:(t + 1) * P], hT[c][0:D, :], start=True, stop=True
                          ).then_inc(sig["scores"][c], 1)
            wait("max", TILES)
            pe.transpose(by[0:TILES, 0:P], nm[c][:, 0:TILES], eye).then_inc(sig["turned"][c], 1)
            yield
            wait("max_row", 16)
            for t in range(TILES):
                pe.matmul((bs, bt)[t][:, 0:S], hT[c][:, t * P:(t + 1) * P], rT[c][:, 0, :], start=True, stop=True
                          ).then_inc(sig["scores"][c], 1)
            yield
            wait("exp", TILES)
            for t in range(TILES):
                for k in range(TILES):
                    last = pe.matmul(bx[:, t * VS:(t + 1) * VS], pr[c][:, k, t * P:(t + 1) * P], vb[c][:, k, 0, :],
                                     start=(k == 0), stop=(k == 1))
            last.then_inc(sig["values"][c], 1)
            yield

            yield
            yield
            yield from mixture("gelu_router", ("gelu_w1",), "gelu_w2", EXPERTS, HID_TILES * P, "gelu", bias=b2_b)
            yield

        def act_chain(eng, c):
            cnt = Counts()
            bs, bt, bx, by = bank[c]

            def wait(name, k=1):
                eng.wait_ge(sig[name][c], cnt(name, k))

            def copy_turned(src, dst, name):
                wait("turned")
                eng.copy(dst[c][0:D, :], src[0:D, 0:S]).then_inc(sig[name][c], 1)

            for l in range(TOK_LAYERS):
                copy_turned(bx, hT, "hT")
                yield
                wait("qkv")
                y = by[:, 0:TILES * 3 * D].rearrange("p (t n) -> p t n", t=TILES)
                eng.copy(qk1[c][:].rearrange("p a (t n) -> p a t n", t=TILES),
                         y[:, :, 0:2 * D].rearrange("p t (a n) -> p a t n", a=2)).then_inc(sig["qk1"][c], 1)
                eng.copy(v8[c][:, :, :, 0:TOK_HD], y[:, :, 2 * D:3 * D].rearrange("p t (h k) -> p t h k", k=TOK_HD)
                         ).then_inc(sig["v8"][c], 1)
                yield
                yield
                wait("k_turned")
                for a in range(2):
                    eng.copy(kT[c][SLOT * a:SLOT * (a + 1), :, a, :],
                             by[:].bitcast(BF16)[SLOT * a:SLOT * (a + 1), :].rearrange("p (q s) -> p q s", q=PAIRS)
                             ).then_inc(sig["kT"][c], 1)
                yield
                for n in range(TOK_HEADS):
                    yield
                yield
                wait("q_turned", 2)
                eng.copy(qTb[c][:].rearrange("p q s -> p (q s)"), bx[:].bitcast(BF16)).then_inc(sig["qTb"][c], 1)
                yield
                cnt("scores", TOK_HEADS)
                for n in range(TOK_HEADS):
                    wait("scores")
                    eng.activation(pr[c][:, n, :], (bs, bt)[n % 2][:], ACT.Exp, scale=TOK_HD ** -0.5).then_inc(sig["exp"][c], 1)
                    yield
                yield
                yield
                copy_turned(bt, aT, "aT")
                yield
                yield
                yield
                yield
                copy_turned(bx, hT, "hT")
                yield
                wait("ffn")
                eng.activation(hid[c][:, 0, :], by[:, 0:S], ACT.Relu).then_inc(sig["hid_a"][c], 1)
                cnt("ffn")
                yield
                yield
                yield
                yield

            yield
            yield
            copy_turned(bx, hT, "hT")
            for i in range(4):
                wait("row_side")
                eng.copy(rT[c][0:D, 2 * i:2 * i + 2, :].rearrange("p a s -> p (a s)"), (by, bx)[i % 2][0:D, :]
                         ).then_inc(sig["rT"][c], 1)
            yield
            for n in range(ATT_HEADS):
                yield
            wait("turned")
            eng.copy(nmT[c][:], bx[0:TILES * ATT_HEADS, 0:P]).then_inc(sig["nmT"][c], 1)
            yield
            cnt("scores", ATT_HEADS)
            for n in range(ATT_HEADS):
                wait("scores")
                eng.activation(pr[c][:, n, 0:CAUSAL], (bs, bt)[n % 2][:, 0:CAUSAL], ACT.Exp).then_inc(sig["exp"][c], 1)
                yield
            yield

            yield
            yield
            yield
            copy_turned(bs, hT, "hT")
            wait("qkv")
            eng.copy(v4[c][:, :, :, 0:GQA_HD],
                     bt[:, 0:S].rearrange("p (t n) -> p t n", t=TILES)[:, :, 96:128].rearrange("p t (a k) -> p t a k", k=GQA_HD)
                     ).then_inc(sig["v8"][c], 1)
            yield
            yield
            wait("k_turned")
            for n in range(GQA_HEADS):
                eng.copy(k4T[c][32 * n:32 * n + 32, n, :], bx[32 * n:32 * n + 32, 0:S]).then_inc(sig["kT"][c], 1)
            yield
            for n in range(GQA_HEADS):
                yield
            wait("q_turned", 2)
            eng.copy(q4T[c][:], by[:, 0:S]).then_inc(sig["qTb"][c], 1)
            yield
            cnt("scores", GQA_HEADS)
            for n in range(GQA_HEADS):
                wait("scores")
                eng.activation(pr[c][:, n, 0:CAUSAL], (bs, bt)[n % 2][:, 0:CAUSAL], ACT.Exp, scale=GQA_HD ** -0.5
                               ).then_inc(sig["exp"][c], 1)
                yield
            yield
            yield
            copy_turned(bt, aT, "aT")
            yield
            yield

            def mixture(func, name, buffer_free, tiles):
                yield
                copy_turned(bs, hT, "hT")
                yield
                wait("lg", 2)
                eng.activation(ex[c][:], lg[c][:], ACT.Exp).then_inc(sig["ex"][c], 1)
                yield
                wait("turned")
                eng.copy(gT[c][0:GATE_ROWS, :], bx[:].bitcast(BF16)[0:GATE_ROWS, 0:S]).then_inc(sig["gT"][c], 1)
                yield
                free, at = buffer_free
                for i in range(tiles + 2):
                    if i < tiles:
                        wait("up")
                        if i >= 2:
                            eng.wait_ge(sig[free][c], at + i - 1)
                        eng.activation(act[c][:, i % 2, :], (bs, bt)[i % 2][:, 0:S], func).then_inc(sig[name][c], 1)
                    yield

            yield from mixture(ACT.Silu, "silu", ("t1", 0), HID_TILES)
            yield

            yield
            copy_turned(bx, hT, "hT")
            wait("row_side", 2)
            eng.copy(rT[c][0:D, 0, :], by[0:D, 0:S]).then_inc(sig["rT"][c], 1)
            cnt("v_side", TILES)
            wait("v_side")
            eng.copy(hT[c][0:D, :], bt[0:D, 0:S]).then_inc(sig["kT"][c], 1)
            eng.copy(vb[c][:, :, 0, 0:D], bx[:, 0:TILES * D].rearrange("p (t d) -> p t d", t=TILES)).then_inc(sig["vb"][c], 1)
            yield
            wait("turned")
            eng.copy(nmT[c][0:TILES, :], by[0:TILES, 0:P]).then_inc(sig["nmT"][c], 1)
            yield
            cnt("scores", TILES)
            for t in range(TILES):
                wait("scores")
                eng.activation(pr[c][:, t, 0:S], (bs, bt)[t][:, 0:S], ACT.Exp, scale=D ** -0.5).then_inc(sig["exp"][c], 1)
            yield
            yield

            yield
            yield
            yield from mixture(ACT.Gelu, "gelu", ("t2", HID_TILES), EXPERTS)
            yield

        def dve_chain(dve, c, g):
            cnt = Counts()
            bs, bt, bx, by = bank[c]

            def wait(name, k=1):
                dve.wait_ge(sig[name][c], cnt(name, k))

            def link(ins):
                ins.then_inc(sig["dve"][c], 1)
                dve.wait_ge(sig["dve"][c], cnt("dve"))

            def show(ins, name):
                ins.then_inc(sig[name][c], 1)
                dve.wait_ge(sig[name][c], cnt(name))

            def moments(src):
                for t in range(TILES):
                    dve.bn_stats(stats[c][:, t, :], src[:, t, :]).then_inc(sig["dve"][c], 1)
                dve.wait_ge(sig["dve"][c], cnt("dve", TILES))
                for t in range(TILES):
                    dve.bn_aggr(mv[c][:, t, :], stats[c][:, t, :]).then_inc(sig["mv"][c], 1)
                wait("mv", TILES)

            def normalise(src, dst, name):
                wait("rstd")
                for t in range(TILES):
                    dve.tensor_scalar(dst[:, t, :], src[:, t, :], mv[c][:, t, 0:1], rstd[c][:, t:t + 1], ALU.subtract, ALU.mult
                                      ).then_inc(sig[name][c], 1)
                wait(name, TILES)

            def moments_scaled(src, dst, gamma, a, b):
                moments(src)
                for t in range(TILES):
                    dve.scalar_tensor_tensor(dst[:, t, :], src[:, t, :], mv[c][:, t, 0:1], w(gamma, a, b), ALU.subtract, ALU.mult
                                             ).then_inc(sig["dve"][c], 1)
                cnt("dve", TILES)

            def normalise_scaled(src, dst, beta, a, b, name):
                dve.wait_ge(sig["dve"][c], cnt.now("dve"))
                wait("rstd")
                for t in range(TILES):
                    dve.scalar_tensor_tensor(dst[:, t, :], src[:, t, :], rstd[c][:, t:t + 1], w(beta, a, b), ALU.mult, ALU.add
                                             ).then_inc(sig[name][c], 1)
                wait(name, TILES)

            def squares(src):
                for t in range(TILES):
                    dve.tensor_tensor_reduce(s_[c][:, t, :], src[:, t, :], src[:, t, :], 1.0, 0.0, ALU.mult, ALU.add,
                                             ss[c][:, t:t + 1]).then_inc(sig["ss"][c], 1)
                wait("ss", TILES)

            def rms_scaled(src, name):
                wait("rstd")
                for t in range(TILES):
                    dve.scalar_tensor_tensor(hc[c][:, t, :], src[:, t, :], rstd[c][:, t:t + 1], w(name), ALU.mult, ALU.mult
                                             ).then_inc(sig["hc"][c], 1)
                wait("hc", TILES)

            for t in range(TILES):
                dve.tensor_tensor(h[c][:, t:t + 1, :], tokens[:, bass.ds(g * (CHAINS * TILES) + (c * TILES + t), 1), :],
                                  w("enc", t * D, (t + 1) * D).rearrange("p (t d) -> p t d", t=1), ALU.add
                                  ).then_inc(sig["h"][c], 1)
            wait("h", TILES)

            n_heads = TILES * TOK_HEADS
            for l in range(TOK_LAYERS):
                yield
                yield
                wait("qk1")
                wait("v8")
                y = by[:, 0:TILES * 3 * D].rearrange("p (t n) -> p t n", t=TILES)
                r4 = rest[c][:].rearrange("p a (t n) -> p a t n", t=TILES)
                for a in range(2):
                    dve.tensor_tensor(r4[:, a], y[:, :, a * D:(a + 1) * D], qk1[c][:, a].rearrange("p (t n) -> p t n", t=TILES),
                                      ALU.subtract).then_inc(sig["dve"][c], 1)
                dve.wait_ge(sig["dve"][c], cnt("dve", 2))
                link(dve.tensor_copy(qk2[c][:], rest[c][:]))
                heads = lambda ap, o=1: ap.rearrange("p (h o k) -> p h o k", o=o, k=TOK_HD)
                for a, dst, at in ((0, qn, 5), (1, kn, 0)):
                    dve.tensor_tensor(dst[c][:, :, at * TOK_HD:(at + 1) * TOK_HD],
                                      rest[c][:, a].rearrange("p (h k) -> p h k", k=TOK_HD),
                                      qk2[c][:, a].rearrange("p (h k) -> p h k", k=TOK_HD), ALU.subtract
                                      ).then_inc(sig["dve"][c], 1)
                q_slots = qn[c][:, :, 0:SPLIT_ROWS].rearrange("p h (i k) -> p h i k", k=TOK_HD)
                k_slots = kn[c][:, :, 0:SPLIT_ROWS].rearrange("p h (i k) -> p h i k", k=TOK_HD)
                dve.tensor_copy(q_slots[:, :, 3:5], heads(qk2[c][:, 0]).to_broadcast([P, n_heads, 2, TOK_HD])).then_inc(sig["dve"][c], 1)
                dve.wait_ge(sig["dve"][c], cnt("dve", 3))
                show(dve.tensor_copy(k_slots[:, :, 2:5:2], heads(qk2[c][:, 1]).to_broadcast([P, n_heads, 2, TOK_HD])), "parts")
                yield
                wait("q_turned")
                dve.tensor_copy(qTa[c][:].rearrange("p q s -> p (q s)"), bx[:].bitcast(BF16)).then_inc(sig["qTa"][c], 1)
                yield
                for n in range(TOK_HEADS):
                    wait("scores")
                    dve.tensor_reduce(nm[c][:].rearrange("p (t h) -> p t h", t=TILES)[:, :, n],
                                      (bs, bt)[n % 2][:].rearrange("p (t s) -> p t s", t=TILES), X_AXIS, ALU.max, negate=True
                                      ).then_inc(sig["max"][c], 1)
                    yield
                wait("max", TOK_HEADS)
                link(dve.tensor_copy(qn[c][:, :, SPLIT_ROWS], nm[c][:]))
                link(dve.tensor_tensor(nr[c][:], nm[c][:], qn[c][:, :, SPLIT_ROWS], ALU.subtract))
                link(dve.tensor_copy(qn[c][:, :, SPLIT_ROWS + 1], nr[c][:]))
                show(dve.tensor_tensor(qn[c][:, :, SPLIT_ROWS + 2], nr[c][:], qn[c][:, :, SPLIT_ROWS + 1], ALU.subtract), "max_split")
                cnt("q_turned")
                yield
                yield
                cnt("scores", TOK_HEADS)
                for n in range(TOK_HEADS):
                    if n == 6:
                        wait("values")
                        dve.tensor_copy(oT[c][:, 0, :], by[:, 0:S]).then_inc(sig["oT"][c], 1)
                    yield
                wait("values")
                dve.tensor_copy(oT[c][:, 1, :], bx[:, 0:S]).then_inc(sig["oT"][c], 1)
                cnt("oT", 2)
                yield
                wait("o_turned")
                o = bs[:].rearrange("p (n k) -> p n k", k=32)
                link(dve.reciprocal(rden[c][:], o[:, :, TOK_HD]))
                show(dve.tensor_tensor(att[c][:].rearrange("p t (n k) -> p (t n) k", k=TOK_HD), o[:, :, 0:TOK_HD],
                                       rden[c][:].rearrange("p (n o) -> p n o", o=1).to_broadcast([P, n_heads, TOK_HD]),
                                       ALU.mult), "att")
                yield
                yield
                yield
                lay = (l * D, (l + 1) * D)
                wait("proj")
                link(dve.tensor_tensor(s_[c][:], bx[:, 0:TILES * D].rearrange("p (t d) -> p t d", t=TILES), h[c][:], ALU.add))
                moments_scaled(s_[c], xn[c], "tok_gamma", *lay)
                yield
                normalise_scaled(xn[c], h[c], "tok_beta", *lay, "h")
                yield
                yield
                cnt("ffn")
                wait("ffn")
                dve.tensor_scalar_max(hid[c][:, 1, :], bs[:, 0:S], 0.0).then_inc(sig["hid_v"][c], 1)
                yield
                yield
                wait("proj")
                wait("hb")
                link(dve.tensor_tensor(s_[c][:], bt[:, 0:TILES * D].rearrange("p (t d) -> p t d", t=TILES), hb[c][:], ALU.add))
                moments_scaled(s_[c], xn[c], "tok_gamma", *lay)
                yield
                normalise_scaled(xn[c], h[c], "tok_beta", *lay, "h")
                yield

            moments(h[c])
            yield
            normalise(h[c], xn[c], "xn")
            yield
            for t in range(TILES):
                wait("v_side")
                dve.tensor_copy(vb[c][:, t, :, 0:D], (bs, bt)[t][:].rearrange("p (n e) -> p n e", e=D)).then_inc(sig["vb"][c], 1)
            yield
            for n in range(ATT_HEADS):
                wait("scores")
                b = (bs, bt)[n % 2]
                dve.tensor_reduce(nm[c][:, 2 * n:2 * n + 1], b[:, 0:P], X_AXIS, ALU.max, negate=True).then_inc(sig["dve"][c], 1)
                cnt("dve")
                dve.tensor_reduce(nm[c][:, 2 * n + 1:2 * n + 2], b[:, P:P + S], X_AXIS, ALU.max, negate=True
                                  ).then_inc(sig["max"][c], 1)
                yield
            cnt("max", ATT_HEADS)
            yield

            def take(half):
                wait("values")
                for t, b in enumerate((bx, by)):
                    o = b[:, 0:4 * VS].rearrange("p (n e) -> p n e", e=VS)
                    rd = rden[c][:, 4 * t:4 * t + 4]
                    link(dve.reciprocal(rd, o[:, :, D]))
                    dve.tensor_tensor(ob[c][:, t, 4 * half:4 * half + 4, :], o[:, :, 0:D],
                                      rd.rearrange("p (n o) -> p n o", o=1).to_broadcast([P, 4, D]), ALU.mult
                                      ).then_inc(sig["ob"][c], 1)
                cnt("ob", 2)

            cnt("scores", ATT_HEADS)
            for n in range(ATT_HEADS):
                if n == 5:
                    take(0)
                yield
            dve.wait_ge(sig["ob"][c], cnt.now("ob"))
            take(1)
            dve.wait_ge(sig["ob"][c], cnt.now("ob"))
            link(dve.tensor_reduce(s_[c][:], ob[c][:].rearrange("p t n d -> p t d n"), X_AXIS, ALU.add))
            link(dve.tensor_tensor(h[c][:], h[c][:], s_[c][:], ALU.add))
            yield

            moments(h[c])
            yield
            normalise(h[c], xn[c], "dve")
            squares(xn[c])
            yield
            rms_scaled(xn[c], "gqa_ln1")
            yield
            yield
            wait("v8")
            y = bt[:, 0:S].rearrange("p (t n) -> p t n", t=TILES)[:, :, 0:96].rearrange("p t (n k) -> p t n k", k=GQA_HD)
            H = GQA_HD // 2
            tab = lambda name, a, b: w(name).rearrange("p (t o k) -> p t o k", t=TILES, o=1)[:, :, :, a:b].to_broadcast([P, TILES, 6, b - a])
            dve.tensor_tensor(ra[c][:], y, tab("cos", 0, GQA_HD), ALU.mult).then_inc(sig["dve"][c], 1)
            dve.tensor_tensor(rb[c][:, :, :, 0:H], y[:, :, :, H:2 * H], tab("sin", 0, H), ALU.mult).then_inc(sig["dve"][c], 1)
            dve.tensor_tensor(rb[c][:, :, :, H:2 * H], y[:, :, :, 0:H], tab("sin", H, 2 * H), ALU.mult).then_inc(sig["dve"][c], 1)
            dve.wait_ge(sig["dve"][c], cnt("dve", 3))
            dve.tensor_tensor(q4[c][:, :, :, 0:GQA_HD], ra[c][:, :, 0:4], rb[c][:, :, 0:4], ALU.add).then_inc(sig["dve"][c], 1)
            for t in range(TILES):
                src = lambda r: r[c][:, t, 4:6].rearrange("p a (o k) -> p a o k", o=1).to_broadcast([P, GQA_KV, 2, GQA_HD])
                ins = dve.tensor_tensor(k4[c][:, t, :, 0:GQA_HD].rearrange("p (a o) k -> p a o k", o=2), src(ra), src(rb), ALU.add)
                if t < TILES - 1:
                    ins.then_inc(sig["dve"][c], 1)
            dve.wait_ge(sig["dve"][c], cnt("dve", TILES))
            show(ins, "parts")
            yield
            wait("q_turned")
            show(dve.tensor_copy(q4T[c][:], by[:, 0:S]), "qTa")
            yield
            for n in range(GQA_HEADS):
                wait("scores")
                b = (bs, bt)[n % 2]
                dve.tensor_reduce(q4[c][:, 0, n, GQA_HD:GQA_HD + 1], b[:, 0:P], X_AXIS, ALU.max, negate=True).then_inc(sig["dve"][c], 1)
                dve.tensor_reduce(q4[c][:, 1, n, GQA_HD:GQA_HD + 1], b[:, P:P + S], X_AXIS, ALU.max, negate=True
                                  ).then_inc(sig["max"][c], 1)
                cnt("dve")
                yield
            cnt("q_turned")
            yield
            for n in range(GQA_HEADS):
                yield
            wait("values")
            show(dve.tensor_copy(oT[c][:, 0, :], by[:, 0:S]), "oT")
            yield
            wait("o_turned")
            o = bs[:, 0:S].rearrange("p (n k) -> p n k", k=32)
            n_heads = TILES * GQA_HEADS
            link(dve.reciprocal(rden[c][:, 0:n_heads], o[:, :, GQA_HD]))
            show(dve.tensor_tensor(att[c][:].rearrange("p t (n k) -> p (t n) k", k=GQA_HD), o[:, :, 0:GQA_HD],
                                   rden[c][:, 0:n_heads].rearrange("p (n o) -> p n o", o=1).to_broadcast([P, n_heads, GQA_HD]),
                                   ALU.mult), "att")
            yield
            yield
            wait("proj")
            link(dve.tensor_tensor(xn[c][:], xn[c][:], bx[:, 0:TILES * D].rearrange("p (t d) -> p t d", t=TILES), ALU.add))
            squares(xn[c])
            yield

            def mixture(eps, tiles, gated):
                yield
                wait("logits")
                l3 = bt[:, 0:TILES * EXPERTS].rearrange("p (t e) -> p t e", t=TILES)
                link(dve.tensor_copy(lo[c][:], l3))
                for t in range(TILES):
                    dve.max(top[c][:, t, :], lo[c][:, t, :]).then_inc(sig["dve"][c], 1)
                dve.wait_ge(sig["dve"][c], cnt("dve", TILES))
                first = top[c][:, :, 0:1]
                dve.tensor_tensor(lg[c][:, :, 0:EXPERTS], lo[c][:], first.to_broadcast([P, TILES, EXPERTS]), ALU.subtract
                                  ).then_inc(sig["lg"][c], 1)
                dve.tensor_tensor(lg[c][:, :, EXPERTS:EXPERTS + 2], top[c][:, :, 0:2], first.to_broadcast([P, TILES, 2]),
                                  ALU.subtract).then_inc(sig["lg"][c], 1)
                for t in range(TILES):
                    dve.max_index(idx[c][:, t, :], top[c][:, t, :], lo[c][:, t, :]).then_inc(sig["dve"][c], 1)
                dve.wait_ge(sig["dve"][c], cnt("dve", TILES))
                link(dve.tensor_copy(idf[c][:], idx[c][:]))
                yield
                wait("ex")
                dve.tensor_reduce(sw[c][:, :, 0:1], ex[c][:, :, 0:EXPERTS], X_AXIS, ALU.add).then_inc(sig["dve"][c], 1)
                dve.tensor_reduce(sw[c][:, :, 1:2], ex[c][:, :, EXPERTS:EXPERTS + 2], X_AXIS, ALU.add).then_inc(sig["dve"][c], 1)
                dve.wait_ge(sig["dve"][c], cnt("dve", 2))
                link(dve.scalar_tensor_tensor(sw[c][:, :, 2:3], sw[c][:, :, 0:1], eps, sw[c][:, :, 1:2], ALU.mult, ALU.add))
                link(dve.reciprocal(sw[c][:, :, 3:4], sw[c][:, :, 2:3]))
                link(dve.tensor_tensor(sw[c][:, :, 0:2], ex[c][:, :, EXPERTS:EXPERTS + 2], sw[c][:, :, 3:4].to_broadcast([P, TILES, 2]),
                                       ALU.mult))
                for t in range(TILES):
                    for k, dst in enumerate((gates, g2)):
                        dve.tensor_scalar(dst[c][:, t, :], w("iota"), idf[c][:, t, k:k + 1], sw[c][:, t, k:k + 1],
                                          ALU.is_equal, ALU.mult).then_inc(sig["dve"][c], 1)
                dve.wait_ge(sig["dve"][c], cnt("dve", 2 * TILES))
                link(dve.tensor_tensor(gates[c][:], gates[c][:], g2[c][:], ALU.add))
                part = [gp[c][:, :, k * EXPERTS:(k + 1) * EXPERTS] for k in range(3)]
                link(dve.tensor_copy(part[0], gates[c][:]))
                link(dve.tensor_tensor(gates[c][:], gates[c][:], part[0], ALU.subtract))
                link(dve.tensor_copy(part[1], gates[c][:]))
                show(dve.tensor_tensor(part[2], gates[c][:], part[1], ALU.subtract), "gates")
                yield
                yield
                for i in range(tiles + 2):
                    if gated and i < tiles:
                        if i >= 2:
                            dve.wait_ge(sig["t2"][c], i - 1)
                        wait("silu")
                        dve.tensor_tensor(t1[c][:, i % 2, :], act[c][:, i % 2, :], (bs, bt)[i % 2][:, S:2 * S], ALU.mult
                                          ).then_inc(sig["t1"][c], 1)
                    if 1 <= i <= tiles:
                        k = i - 1
                        wait("t1" if gated else "gelu")
                        wait("wide")
                        dve.tensor_tensor(t2[c][:, k % 2, :], (t1 if gated else act)[c][:, k % 2, :], bx[:, 0:S], ALU.mult
                                          ).then_inc(sig["t2"][c], 1)
                    yield
                wait("moe")
                show(dve.tensor_copy(oT[c][:, 0, :], by[:, 0:S]), "oT")
                wait("o_turned")
                o = bs[:, 0:TILES * P].rearrange("p (t n) -> p t n", t=TILES)
                link(dve.tensor_tensor(h[c][:], h[c][:], o[:, :, 0:D], ALU.add))
                show(dve.tensor_tensor(h[c][:], h[c][:], o[:, :, D:2 * D], ALU.add), "stream")

            rms_scaled(xn[c], "gqa_ln2")
            link(dve.tensor_tensor(h[c][:], h[c][:], xn[c][:], ALU.add))
            yield from mixture(1e-9, HID_TILES, gated=True)
            moments(h[c])
            yield

            normalise(h[c], xn[c], "xn")
            yield
            yield
            cnt("scores", GQA_HEADS)
            for t in range(TILES):
                wait("scores")
                dve.tensor_reduce(nm[c][:, t:t + 1], (bs, bt)[t][:, 0:S], X_AXIS, ALU.max, negate=True).then_inc(sig["max"][c], 1)
            yield
            yield
            wait("values")
            o = bx[:, 0:TILES * VS].rearrange("p (t e) -> p t e", e=VS)
            link(dve.reciprocal(rden[c][:, 0:TILES], o[:, :, D]))
            for t in range(TILES):
                dve.scalar_tensor_tensor(h[c][:, t, :], o[:, t, 0:D], rden[c][:, t:t + 1], h[c][:, t, :], ALU.mult, ALU.add
                                         ).then_inc(sig["dve"][c], 1)
            dve.wait_ge(sig["dve"][c], cnt("dve", TILES))
            moments(h[c])
            yield

            normalise(h[c], xn[c], "dve")
            moments_scaled(xn[c], s_[c], "gelu_gamma", 0, D)
            yield
            normalise_scaled(s_[c], hc[c], "gelu_beta", 0, D, "hc")
            yield
            yield from mixture(0.0, EXPERTS, gated=False)
            yield

        def pool_chain(pool, c):
            cnt = Counts()

            def wait(name, k=1):
                pool.wait_ge(sig[name][c], cnt(name, k))

            def link(ins):
                ins.then_inc(sig["pool"][c], 1)
                pool.wait_ge(sig["pool"][c], cnt("pool"))

            def inv_sqrt(src, scale, eps):
                link(pool.tensor_scalar(var[c][:], src, scale, eps, ALU.mult, ALU.add))
                pool.tensor_tensor(rstd[c][:], var[c][:], minus_half[:], ALU.pow).then_inc(sig["rstd"][c], 1)

            def norm(eps):
                wait("mv", TILES)
                inv_sqrt(mv[c][:, :, 1], 1.0, eps)

            def rms():
                wait("ss", TILES)
                inv_sqrt(ss[c][:], 1.0 / D, 1e-6)

            n_heads = TILES * TOK_HEADS
            cnt("h", TILES)
            for l in range(TOK_LAYERS):
                yield
                yield
                wait("qk1")
                for a, dst, sl in ((1, kn, slice(1, 6, 2)), (0, qn, slice(0, 3))):
                    slots = dst[c][:, :, 0:SPLIT_ROWS].rearrange("p h (i k) -> p h i k", k=TOK_HD)[:, :, sl]
                    src = qk1[c][:, a].rearrange("p (h o k) -> p h o k", o=1, k=TOK_HD).to_broadcast([P, n_heads, 3, TOK_HD])
                    pool.tensor_copy(slots, src).then_inc(sig["parts_p"][c], 1)
                yield
                yield
                for n in range(TOK_HEADS):
                    yield
                yield
                yield
                for n in range(TOK_HEADS):
                    yield
                yield
                yield
                wait("q_turned", 2)
                pool.memset(qn[c][:, :, SPLIT_ROWS:ROWS], 0.0).then_inc(sig["max_clear"][c], 1)
                yield
                yield
                norm(1e-3)
                yield
                wait("h", TILES)
                v = w("tok_b2", l * D, (l + 1) * D).rearrange("p (o d) -> p o d", o=1).to_broadcast([P, TILES, D])
                pool.tensor_tensor(hb[c][:], h[c][:], v, ALU.add).then_inc(sig["hb"][c], 1)
                cnt("h", TILES)
                yield
                yield
                yield
                yield
                norm(1e-3)
                yield
                yield
            norm(1e-5)
            yield
            yield
            yield
            for n in range(ATT_HEADS):
                yield
            yield
            for n in range(ATT_HEADS):
                yield
            yield
            norm(1e-5)
            yield
            pool.memset(q4[c][:, :, :, GQA_HD:GQA_HD + 1], 0.0).then_inc(sig["max_clear"][c], 1)
            rms()
            yield
            yield
            yield
            yield
            yield
            for n in range(2 * GQA_HEADS + 1):
                yield
            yield
            yield
            yield
            rms()
            yield
            for i in range(4 + HID_TILES + 2):
                yield
            norm(1e-5)
            yield
            for i in range(4):
                yield
            norm(1e-5)
            yield
            norm(1e-5)
            yield
            yield
            for i in range(4 + EXPERTS + 2):
                yield
            yield

        def sp_chain(sp, c, g):
            for turn_ in range(2):
                sp.wait_ge(sig["nmT"][c], turn_ + 1)
                heads = (ATT_HEADS, 1)[turn_]
                sp.dma_start(rT[c][D:VS, 0:heads, :].rearrange("o n (t p) -> o (n t) p", p=P),
                             nmT[c][0:heads * TILES, :]).then_inc(sig["max_row"][c], 16)
                yield
            sp.wait_ge(sig["stream"][c], 2)
            sp.dma_start(out_v[:, bass.ds(g * (CHAINS * TILES) + c * TILES, TILES), :], h[c][:]).then_inc(sig["stored"][c], 16)
            yield
            sp.wait_ge(sig["stored"][c], 16)
            yield

        with nc.Fori(0, BATCH // CHAINS) as g:
            with nc.Block() as block:
                @block.tensor
                def _(pe):
                    in_turns([pe_chain(pe, c) for c in range(CHAINS)], LAG, STEPS)

                @block.scalar
                def _(eng):
                    in_turns([act_chain(eng, c) for c in range(CHAINS)], LAG, STEPS)

                @block.vector
                def _(dve):
                    in_turns([dve_chain(dve, c, g) for c in range(CHAINS)], LAG, STEPS)

                @block.gpsimd
                def _(pool):
                    in_turns([pool_chain(pool, c) for c in range(CHAINS)], LAG, STEPS)

                @block.sync
                def _(sp):
                    in_turns([sp_chain(sp, c, g) for c in range(CHAINS)], 0.5, [1] * 4)

            with nc.Block() as block:
                @block.sync
                def _(sp):
                    sp.sem_clear(range(sig.first.num, sig.last.num + 1))


def kernel(**inputs):
    import concourse.bacc as _bacc
    from concourse.bass_utils import run_bass_kernel_spmd as _run

    nc = _bacc.Bacc("TRN2", target_bir_lowering=False, num_devices=1)
    laid = {k: np.ascontiguousarray(v) for k, v in pack(inputs).items()}
    shapes = {k: v.shape for k, v in laid.items()}
    arrays, packed = {}, {}
    for parts in sorted({p for p, _ in shapes.values()}):
        a = np.concatenate([v for v in laid.values() if v.shape[0] == parts], axis=1)
        arrays[f"packed{parts}"] = a
        packed[parts] = nc.dram_tensor(f"packed{parts}", a.shape, F32, kind="ExternalInput").ap()
    arrays["x"] = np.ascontiguousarray(np.asarray(inputs["x"]).reshape(BATCH * TILES, P).T)
    arrays["table"] = np.ascontiguousarray(inputs["L0_tok_emb"])
    x = nc.dram_tensor("x", arrays["x"].shape, I32, kind="ExternalInput").ap()
    table = nc.dram_tensor("table", arrays["table"].shape, F32, kind="ExternalInput").ap()
    out = nc.dram_tensor("out", (BATCH, S, D), F32, kind="ExternalOutput").ap()
    tower(nc, x, table, packed, shapes, out)
    r = _run(nc, [arrays], core_ids=[0])
    return r.results[0]["out"]
```

```python
from contextlib import ExitStack

import concourse.bass as bass
from concourse import mybir
import numpy as np

ALU = mybir.AluOpType
ACT = mybir.ActivationFunctionType
F32 = mybir.dt.float32
BF16 = mybir.dt.bfloat16
I32 = mybir.dt.int32
U32 = mybir.dt.uint32
X_AXIS = mybir.AxisListType.X

P = 128
D = 64
S = 256
TILES = S // P
BATCH = 8
CHAINS = 4
TOK_LAYERS, TOK_HEADS, TOK_HD = 4, 8, 8
FFN = 4 * D
PAIRS = TOK_HEADS // 2
SLOT = 64
Q_PARTS = [1, 1, 1, 2, 2, 3]
K_PARTS = [3, 1, 2, 1, 2, 1]
TERMS = len(Q_PARTS)
SPLIT_ROWS = TERMS * TOK_HD
ROWS = SPLIT_ROWS + 3
ATT_HEADS = 8
GQA_HEADS, GQA_KV, GQA_HD = 4, 2, 16
EXPERTS = 8
GATE_ROWS = 3 * EXPERTS
HID = 170
HID_TILES = -(-EXPERTS * HID // P)
VS = D + 1
CAUSAL = P + S
MASKED = -1e30



def constants():
    pos = np.arange(S).reshape(-1, 1)
    depth = np.array([2 * (i // 2) for i in range(D)]).reshape(1, -1)
    angle = pos * (1.0 / 10000.0 ** (depth / D))
    enc = np.cos(angle)
    enc[:, ::2] = np.sin(enc[:, ::2])
    enc = enc.astype(np.float32).reshape(TILES, P, D).transpose(1, 0, 2)
    inv = 1.0 / 10000.0 ** (np.arange(0, GQA_HD, 2, dtype=np.float32) / GQA_HD)
    freq = np.outer(np.arange(S, dtype=np.float32), inv)
    emb = np.concatenate([freq, freq], axis=-1)
    cos, sin = np.cos(emb).astype(np.float32), np.sin(emb).astype(np.float32)
    sin[:, :GQA_HD // 2] *= -1
    tile = lambda a: a.reshape(TILES, P, GQA_HD).transpose(1, 0, 2).reshape(P, -1)
    iota = np.tile(np.arange(EXPERTS, dtype=np.float32), (P, 1))
    later = np.triu(np.ones((P, P), np.float32), 1) * MASKED
    sel = np.zeros((EXPERTS, HID_TILES, P), np.float32)
    for j in range(EXPERTS * HID):
        sel[j // HID, j // P, j % P] = 1
    sel_e = np.zeros((EXPERTS, EXPERTS, P), np.float32)
    for e in range(EXPERTS):
        sel_e[e, e] = 1
    return {
        "eye": np.eye(P, dtype=np.float32), "enc": enc.reshape(P, -1), "cos": tile(cos), "sin": tile(sin),
        "iota": iota, "later": later, "later_t": np.ascontiguousarray(later.T),
        "sel": np.tile(np.concatenate([sel.reshape(EXPERTS, -1), sel_e.reshape(EXPERTS, -1)], axis=1), (3, 1)),
    }


def rows(a):
    return np.broadcast_to(np.asarray(a).reshape(1, -1), (P, np.asarray(a).size))


def pack(i):
    a = {k: np.asarray(v) for k, v in i.items()}
    wq = a["L0_tok_wq"].transpose(2, 0, 1, 3).reshape(D, TOK_LAYERS, D)
    wk = a["L0_tok_wk"].transpose(2, 0, 1, 3).reshape(D, TOK_LAYERS, D)
    wv = a["L0_tok_wv"].transpose(2, 0, 1, 3).reshape(D, TOK_LAYERS, D)
    pad = HID_TILES * P - EXPERTS * HID
    flat = lambda w: np.pad(w.reshape(EXPERTS * HID, D), ((0, pad), (0, 0)))
    w2 = np.pad(a["L0_ffn_w2"].transpose(0, 2, 1).reshape(EXPERTS * HID, D), ((0, pad), (0, 0)))
    row = lambda w, b=None: np.concatenate([w, np.zeros((1, w.shape[1]), w.dtype) if b is None else b.reshape(1, -1)], axis=0)
    out = {
        "tok_qkv": row(np.concatenate([wq, wk, wv], axis=2).reshape(D, -1)),
        "tok_wo": row(a["L0_tok_wo"].transpose(1, 0, 2).reshape(D, -1), a["L0_tok_bo"]),
        "tok_w1": row(a["L0_tok_w1"].transpose(1, 0, 2).reshape(D, -1), a["L0_tok_b1"]),
        "gqa_qkv": row(np.concatenate([a["L0_ffn_wq"], a["L0_ffn_wk"], a["L0_ffn_wv"]], axis=0).T),
        "gqa_wo": row(a["L0_ffn_wo"].T),
        "moe_router": row(a["L0_ffn_router_w"].T),
        "moe_w1": row(flat(a["L0_ffn_w1"]).T), "moe_w3": row(flat(a["L0_ffn_w3"]).T),
        "one_wq": row(a["L1_attn_Wq"], a["L1_attn_bq"]), "one_wk": row(a["L1_attn_Wk"], a["L1_attn_bk"]),
        "one_wv": row(a["L1_attn_Wv"], a["L1_attn_bv"]),
        "gelu_router": row(a["L1_ffn_Wr"], a["L1_ffn_br"]),
        "gelu_w1": row(a["L1_ffn_W1"].transpose(1, 0, 2).reshape(D, -1), a["L1_ffn_b1"]),
        "tok_w2": a["L0_tok_w2"].reshape(TOK_LAYERS, 2, P, D).transpose(2, 0, 1, 3).reshape(P, -1),
        "tok_b2": rows(a["L0_tok_b2"]),
        "tok_gamma": rows(a["L0_tok_gamma"]), "tok_beta": rows(a["L0_tok_beta"]),
        "att_k": a["L0_attn_key_matrices"].transpose(2, 0, 1).reshape(D, -1),
        "att_q": a["L0_attn_query_matrices"].transpose(2, 0, 1).reshape(D, -1),
        "att_vi": a["L0_attn_value_in_matrices"].transpose(2, 0, 1).reshape(D, -1),
        "att_vo": a["L0_attn_value_out_matrices"].transpose(1, 0, 2).reshape(D, -1),
        "gqa_ln1": rows(a["L0_ffn_ln1_w"]), "gqa_ln2": rows(a["L0_ffn_ln2_w"]),
        "moe_w2": w2.reshape(HID_TILES, P, D).transpose(1, 0, 2).reshape(P, -1),
        "gelu_gamma": rows(a["L1_ffn_gamma"]), "gelu_beta": rows(a["L1_ffn_beta"]),
        "gelu_w2": a["L1_ffn_W2"].transpose(1, 0, 2).reshape(P, -1),
        "gelu_b2": np.tile(a["L1_ffn_b2"], (3, 1)),
    }
    out.update(constants())
    return out


def columns(shapes, parts):
    at, found = 0, {}
    for name, (p, n) in shapes.items():
        if p == parts:
            found[name] = (at, n)
            at += n
    return found, at


CLEAR_B = 7
SHARED = [
    [("rest_q", TILES * TOK_LAYERS), ("row_side", 5)],
    [("rest_k", TILES * TOK_LAYERS), ("rT", 5)],
    [("q_parts", TOK_LAYERS), ("vb", 3)],
    [("k_parts", 2 * TOK_LAYERS), ("nmT", 2)],
    [("max_split", TOK_LAYERS), ("max_row", 32), ("stored", 16)],
    [("hid", TOK_LAYERS), ("xn", 2 * TILES)],
    [("v_side", 3), ("gelu", EXPERTS)],
    [("ffn", TOK_LAYERS), ("up", HID_TILES + EXPERTS)],
    [("hb", TOK_LAYERS), ("ss", 2 * TILES), ("wide", HID_TILES + EXPERTS)],
    [("part1", 2 * TILES * TOK_LAYERS), ("parts", 1), ("t1", HID_TILES)],
    [("clear_a", 3), ("clear_b", CLEAR_B), ("clear_c", 1), ("silu", HID_TILES)],
    [("clear_k", 1), ("hc", 3 * TILES)],
    [("ob", 2 * TILES), ("t2", HID_TILES + EXPERTS)],
    [("v8", TOK_LAYERS + 1), ("logits", 2)],
    [("k_turned", TOK_LAYERS + 1), ("gT", 2)],
    [("qTa", TOK_LAYERS + 1), ("lg", 4)],
    [("qTb", 2 * TOK_LAYERS + 1), ("gates", 2)],
    [("max_clear", TOK_LAYERS - 1), ("ex", 2)],
    [("q_turned", 2 * TOK_LAYERS + 2), ("moe", 2)],
    [("att", TOK_LAYERS + 1), ("stream", 2)],
]
FIRST, HOLDER = {}, {}
for group in SHARED:
    at = 0
    for name, times in group:
        FIRST[name], HOLDER[name] = at, group[0][0]
        at += times


class Counts:

    def __init__(self):
        self.n = dict(FIRST)

    def __call__(self, name, k=1):
        self.n[name] = self.n.get(name, 0) + k
        return self.n[name]

    def now(self, name):
        return self.n.get(name, 0)


class Signals:

    def __init__(self, nc, ctx):
        self.nc, self.ctx, self.made = nc, ctx, {}

    def __getitem__(self, name):
        name = HOLDER.get(name, name)
        if name not in self.made:
            self.made[name] = [self.ctx.enter_context(self.nc.semaphore(f"{name}{c}")) for c in range(CHAINS)]
        return self.made[name]

    def numbers(self):
        n = sorted(s.num for group in self.made.values() for s in group)
        assert n == list(range(n[0], n[0] + len(n)))
        return range(n[0], n[-1] + 1)


NORM_STEPS = 5
ROUTE_STEPS = 9
TOK_STEPS = ([1.6, 1.6, 1.5, 0.5, 0.5, 0.8] + [0.6] * TOK_HEADS + [0.38, 0.38, 0.38, 0.38, 1.3] + [0.6] * TOK_HEADS
             + [1.3, 0.85, 0.4, 0.7, 0.7] + [0.45, 0.4, 0.4, 0.8, 1.2] + [0.7, 0.91, 0.89] + [0.5, 0.4, 0.4, 0.8, 1.2])
CAUSAL_STEPS = [2.0, 1.0, 6.0] + [1.0] * ATT_HEADS + [3.0] + [0.55] * ATT_HEADS + [2.4, 5.0]
GQA_STEPS = [2.0, 2.0, 1.0, 2.4, 3.0, 2.0] + [3.0] * GQA_HEADS + [1.5] + [1.27] * GQA_HEADS + [1.5, 1.5, 0.5, 2.0]
SILU_STEPS = ([1.2, 5.4] + [0.6, 0.8, 0.4, 0.6, 0.6, 0.25, 0.4, 0.8, 1.2] + [1.8, 2.88, 1.2] + [2.4, 1.2] * (HID_TILES - 1)
              + [1.2, 3.0])
ONE_STEPS = [0.91, 2.5, 2.5, 1.7, 2.5]
GELU_STEPS = [1.7, 1.4, 1.4, 0.45] + [0.6, 0.8, 1.2, 0.6, 0.6, 0.5, 0.4, 0.8, 1.8] + [0.5] + [4.8] * EXPERTS + [1.0, 2.5]
STEPS = TOK_LAYERS * TOK_STEPS + CAUSAL_STEPS + GQA_STEPS + SILU_STEPS + ONE_STEPS + GELU_STEPS


def in_turns(programs, lag, steps):
    at = list(lag)
    taken = [0] * len(programs)
    while min(taken) < len(steps):
        c = min((c for c in range(len(programs)) if taken[c] < len(steps)), key=lambda c: (at[c], c))
        next(programs[c])
        at[c] += steps[taken[c]]
        taken[c] += 1
    assert all(next(p, "end") == "end" for p in programs)


def tower(nc, x, table, packed, shapes, out, LAG=(0.0, 3.0, 6.0, 9.0)):
    with ExitStack() as ctx:
        def sb(name, shape, dt=F32):
            return ctx.enter_context(nc.sbuf_tensor(name, shape, dt))

        def sem(name):
            return ctx.enter_context(nc.semaphore(name))

        pr = [sb(f"pr{c}", [P, 8, 2 * S]) for c in range(CHAINS)]

        W = {}
        early = {D: pr[0], GATE_ROWS: pr[1]}
        for parts, dram in packed.items():
            at, n = columns(shapes, parts)
            if parts in early:
                t = early[parts][:].rearrange("p a b -> p (a b)")[0:parts, 0:n]
            else:
                t = sb(f"resident{parts}", [P if parts == VS else parts, n])
            W.update({k: (t, a, m) for k, (a, m) in at.items()})
            W[parts] = t

        def w(name, a=0, b=None):
            t, at, n = W[name]
            return t[:, at + a:at + (n if b is None else b)]

        eye = w("eye")
        eye_b = sb("eye_b", [P, P], BF16)
        later_b = sb("later_b", [P, 2, 2, P], BF16)
        n_sel = W["sel"][2]
        sel_b = sb("sel_b", [P, n_sel], BF16)
        b2_b = sb("b2_b", [P, 3, D], BF16)
        b2_rest = sb("b2_rest", [GATE_ROWS, 2, D])
        att_g = sb("att_g", [P, ATT_HEADS, D])
        att_v = sb("att_v", [P, ATT_HEADS, D])
        ids = sb("ids", [P, BATCH * TILES], I32)
        tokens = sb("tokens", [P, BATCH * TILES, D])
        minus_half = sb("minus_half", [P, TILES])

        def per(name, shape, dt=F32):
            return [sb(f"{name}{c}", shape, dt) for c in range(CHAINS)]

        h = per("h", [P, TILES, D])
        s_ = per("s_", [P, TILES, D])
        xn = per("xn", [P, TILES, D])
        hc = per("hc", [P, TILES, D])
        att = hc
        stats = per("stats", [P, TILES, 6])
        mv = per("mv", [P, TILES, 2])
        ss = per("ss", [P, TILES])
        var = per("var", [P, TILES])
        rstd = per("rstd", [P, TILES])
        hT = per("hT", [P, S])
        rest = per("rest", [P, 2, TILES * D])
        nm = per("nm", [P, TILES * TOK_HEADS])
        nr = per("nr", [P, TILES * TOK_HEADS])
        nmT = per("nmT", [TILES * ATT_HEADS, P])
        rden = per("rden", [P, TILES * TOK_HEADS])
        v8 = per("v8", [P, TILES, TOK_HEADS, 32])
        q4 = per("q4", [P, TILES, GQA_HEADS, 32])
        k4 = per("k4", [P, TILES, GQA_HEADS, 32])
        v4 = per("v4", [P, TILES, GQA_KV, 32])
        lg = per("lg", [P, TILES, EXPERTS + 2])
        top = per("top", [P, TILES, 8])
        idx = per("idx", [P, TILES, 8], U32)
        idf = per("idf", [P, TILES, 8])
        ex = per("ex", [P, TILES, EXPERTS + 2])
        sw = per("sw", [P, TILES, 4])
        pick = per("pick", [P, TILES, 2, EXPERTS])
        gates = per("gates", [P, TILES, EXPERTS])
        gp = per("gp", [P, TILES, GATE_ROWS], BF16)
        gT = per("gT", [P, S], BF16)

        rT = per("rT", [P, ATT_HEADS, S])
        half_rT = [t[:].rearrange("p n s -> p (n s)").bitcast(BF16) for t in rT]
        n_kT, n_qT = PAIRS * 2 * S, PAIRS * S
        kT = [t[:, 0:n_kT].rearrange("p (q a s) -> p q a s", q=PAIRS, a=2) for t in half_rT]
        qTa, qTb = ([t[:, a:a + n_qT].rearrange("p (q s) -> p q s", q=PAIRS) for t in half_rT]
                    for a in (n_kT, n_kT + n_qT))
        vb = per("vb", [P, TILES, ATT_HEADS, VS])
        half_vb = [t[:].rearrange("p t n e -> p (t n e)").bitcast(BF16) for t in vb]
        n_qn = TILES * TOK_HEADS * SLOT
        qn, kn = ([t[:, a:a + n_qn].rearrange("p (h k) -> p h k", k=SLOT) for t in half_vb] for a in (0, n_qn))
        slot = lambda a, n: [t[:].rearrange("p a b -> p (a b)")[:, a * 2 * S:a * 2 * S + n] for t in pr]
        oT = [t.rearrange("p (a b) -> p a b", a=2) for t in slot(0, 2 * S)]
        ob = [t.rearrange("p (t n d) -> p t n d", t=TILES, n=ATT_HEADS) for t in slot(0, TILES * ATT_HEADS * D)]
        hid = [t.rearrange("p (a b) -> p a b", a=2) for t in slot(1, 2 * S)]
        act, t1, t2 = ([t.rearrange("p (a b) -> p a b", a=2) for t in slot(k, 2 * S)] for k in (2, 3, 4))
        k4T = [t.rearrange("p (n s) -> p n s", n=GQA_HEADS) for t in slot(4, GQA_HEADS * S)]
        ra = [t.rearrange("p (t n k) -> p t n k", t=TILES, k=GQA_HD) for t in slot(6, TILES * 6 * GQA_HD)]
        rb = [t.rearrange("p (t n k) -> p t n k", t=TILES, k=GQA_HD) for t in slot(7, TILES * 6 * GQA_HD)]
        q4T = [t[:, S:2 * S] for t in slot(7, 2 * S)]

        bank = [[ctx.enter_context(nc.psum_tensor(f"bank{k}{c}", [P, 512], F32)) for k in "st"] for c in range(CHAINS)]

        sig = Signals(nc, ctx)
        ids_loaded, loaded, cleared, gathered = sem("ids_loaded"), sem("loaded"), sem("cleared"), sem("gathered")
        folded_pe, folded, constant, b2_split = sem("folded_pe"), sem("folded"), sem("constant"), sem("b2_split")

        with nc.Block() as block:
            n_loads = len(packed)

            @block.sync
            def _(sp):
                sp.dma_start(ids[:], x).then_inc(ids_loaded, 16)
                for parts, dram in sorted(packed.items(), key=lambda kv: kv[0] == VS):
                    if parts == VS:
                        sp.wait_ge(cleared, 1)
                    sp.dma_start(W[parts][0:parts], dram).then_inc(loaded, 16)
                sp.wait_ge(loaded, 16 * n_loads)

            @block.gpsimd
            def _(pool):
                pool.wait_ge(ids_loaded, 16)
                for n in range(BATCH * TILES):
                    pool.indirect_dma_start(
                        out=tokens[:, n, :], out_offset=None, in_=table[:, :],
                        in_offset=bass.IndirectOffsetOnAxis(ap=ids[:, n:n + 1], axis=0)).then_inc(gathered, 16)
                pool.memset(minus_half[:], -0.5)
                pool.wait_ge(gathered, 16 * BATCH * TILES)

            @block.vector
            def _(dve):
                dve.memset(W[VS][D:P, :], 0.0).then_inc(cleared, 1)
                n = 0
                for c in range(CHAINS):
                    dve.memset(hT[c][D:P], 0.0).then_inc(constant, 1)
                    dve.memset(gT[c][:], 0.0).then_inc(constant, 1)
                    dve.memset(v8[c][:, :, :, TOK_HD + 1:32], 0.0)
                    dve.memset(v8[c][:, :, :, TOK_HD:TOK_HD + 1], 1.0)
                    n += 2
                for b in (att_g, att_v):
                    dve.memset(b[D:P], 0.0).then_inc(constant, 1)
                dve.memset(sel_b[:], 0.0).then_inc(constant, 1)
                dve.memset(b2_b[:], 0.0).then_inc(constant, 1)
                dve.wait_ge(constant, n + 4)
                for c in range(CHAINS):
                    dve.memset(hT[c][D:VS, :], 1.0)
                dve.wait_ge(loaded, 16 * n_loads)
                dve.tensor_copy(eye_b[:], eye)
                for a in range(2):
                    dve.tensor_copy(later_b[:, 0, a, :], w("later"))
                    dve.tensor_copy(later_b[:, 1, a, :], w("later_t"))
                dve.tensor_copy(sel_b[0:GATE_ROWS, :], w("sel"))
                src = w("gelu_b2")
                for k in range(3):
                    dve.tensor_copy(b2_b[0:GATE_ROWS, k, :], src).then_inc(b2_split, 1)
                    dve.wait_ge(b2_split, 2 * k + 1)
                    if k < 2:
                        dve.tensor_tensor(b2_rest[:, k, :], src, b2_b[0:GATE_ROWS, k, :], ALU.subtract).then_inc(b2_split, 1)
                        dve.wait_ge(b2_split, 2 * k + 2)
                        src = b2_rest[:, k, :]
                for k, dst in enumerate((att_g, att_v)):
                    dve.wait_ge(folded_pe, k + 1)
                    dve.tensor_copy(dst[0:D], bank[0][k][0:D, :].rearrange("p (n e) -> p n e", n=ATT_HEADS)).then_inc(folded, 1)
                dve.wait_ge(folded, 2)

            @block.tensor
            def _(pe):
                pe.wait_ge(loaded, 16 * n_loads)
                for k, (left, right) in enumerate((("att_k", "att_q"), ("att_vi", "att_vo"))):
                    for n in range(ATT_HEADS):
                        last = pe.matmul(bank[0][k][0:D, n * D:(n + 1) * D], w(left, n * D, (n + 1) * D),
                                         w(right, n * D, (n + 1) * D), start=True, stop=True)
                    last.then_inc(folded_pe, 1)

        out_v = out.rearrange("b (t p) d -> p (b t) d", p=P)

        def pe_chain(pe, c):
            cnt = Counts()
            bs, bt = bank[c]
            by_turns = (bt, bs)

            def wait(name, k=1):
                pe.wait_ge(sig[name][c], cnt(name, k))

            def turn(src, dst):
                for t in range(TILES):
                    last = pe.transpose(dst[0:D, t * P:(t + 1) * P], src[:, t, :], eye)
                last.then_inc(sig["turned"][c], 1)

            def natural(dst, lhs, rhs, done):
                n = rhs.shape[-1]
                for t in range(TILES):
                    last = pe.matmul(dst[:, t * n:(t + 1) * n], lhs[:, t * P:(t + 1) * P], rhs, start=True, stop=True)
                last.then_inc(sig[done][c], 1)

            def turn_pairs(src, dst, done):
                d = dst[:].bitcast(BF16).rearrange("p (q s) -> p q s", q=PAIRS)
                for q in range(PAIRS):
                    for t in range(TILES):
                        h0 = t * TOK_HEADS + 2 * q
                        last = pe.transpose(d[:, q, t * P:(t + 1) * P],
                                            src[:, h0:h0 + 2, :].rearrange("p a b -> p (a b)"), eye_b[:])
                last.then_inc(sig[done][c], 1)

            for l in range(TOK_LAYERS):
                wait("h", TILES)
                turn(h[c], bs)
                yield
                wait("hT")
                natural(bt, hT[c], w("tok_qkv", l * 3 * D, (l + 1) * 3 * D), "qkv")
                yield
                yield
                yield
                yield
                wait("k_parts", 2)
                turn_pairs(kn[c], bs, "k_turned")
                wait("q_parts")
                if l > 0:
                    wait("max_clear")
                turn_pairs(qn[c], bt, "q_turned")
                yield
                wait("qTa")
                for n in range(TOK_HEADS):
                    if n < 2:
                        wait("kT")
                    else:
                        pe.wait_ge(sig["max"][c], cnt.now("max") + n - 1)
                    for t in range(TILES):
                        last = pe.matmul(by_turns[n % 2][:, t * S:(t + 1) * S], qTa[c][:, n // 2, t * P:(t + 1) * P],
                                         kT[c][:, n // 2, n % 2, :], start=True, stop=True)
                    last.then_inc(sig["scores"][c], 1)
                    yield
                cnt("max", TOK_HEADS)
                for part in range(4):
                    yield
                wait("max_split")
                turn_pairs(qn[c], bs, "q_turned")
                yield
                for n in range(TOK_HEADS):
                    if n < 2:
                        wait("qTb")
                    else:
                        pe.wait_ge(sig["exp"][c], cnt.now("exp") + n - 1)
                    for t in range(TILES):
                        last = pe.matmul(by_turns[n % 2][:, t * S:(t + 1) * S], kT[c][:, n // 2, n % 2, t * P:(t + 1) * P],
                                         qTb[c][:, n // 2, :], start=True, stop=True)
                    last.then_inc(sig["scores"][c], 1)
                    yield
                wait("v8")
                for half in range(2):
                    pe.wait_ge(sig["exp"][c], cnt.now("exp") + TOK_HEADS - 1 + half)
                    for t in range(TILES):
                        for j in range(4):
                            last = pe.matmul(by_turns[half][32 * j:32 * j + 32, 0:S], v8[c][:, t, 4 * half + j, :],
                                             pr[c][:, 4 * half + j, t * S:(t + 1) * S], start=(t == 0), stop=(t == 1),
                                             tile_position=(0, 32 * j), skip_group_check=True)
                    last.then_inc(sig["values"][c], 1)
                cnt("exp", TOK_HEADS)
                yield
                wait("oT", 2)
                for half in range(2):
                    for t in range(TILES):
                        last = pe.transpose(bt[:, (t * 2 + half) * P:(t * 2 + half + 1) * P],
                                            oT[c][:, half, t * P:(t + 1) * P], eye)
                last.then_inc(sig["o_turned"][c], 1)
                yield
                yield
                wait("att")
                turn(att[c], bs)
                yield
                wait("hT")
                natural(bt, hT[c], w("tok_wo", l * D, (l + 1) * D), "proj")
                yield
                for part in range(NORM_STEPS):
                    yield
                wait("h", TILES)
                turn(h[c], bs)
                yield
                wait("hT")
                for m in range(2):
                    last = pe.matmul(bt[:, m * S:(m + 1) * S], w("tok_w1", l * FFN + m * P, l * FFN + (m + 1) * P), hT[c][:],
                                     start=True, stop=True)
                last.then_inc(sig["ffn"][c], 1)
                yield
                wait("hid")
                for t in range(TILES):
                    for m in range(2):
                        last = pe.matmul(bs[:, t * D:(t + 1) * D], hid[c][:, m, t * P:(t + 1) * P],
                                         w("tok_w2", (l * 2 + m) * D, (l * 2 + m + 1) * D), start=(m == 0), stop=(m == 1))
                last.then_inc(sig["proj"][c], 1)
                yield
                for part in range(NORM_STEPS):
                    yield

            yield
            yield
            wait("xn", TILES)
            turn(xn[c], bs)
            wait("hT")

            def row_side(i, dst):
                for j in range(2):
                    last = pe.matmul(dst[0:D, j * S:(j + 1) * S], att_g[:, 2 * i + j, :], hT[c][:], start=True, stop=True)
                last.then_inc(sig["row_side"][c], 1)

            def v_side(t, dst):
                pe.matmul(dst[:], hT[c][:, t * P:(t + 1) * P], att_v[:].rearrange("p n e -> p (n e)"),
                          start=True, stop=True).then_inc(sig["v_side"][c], 1)

            row_side(0, bt)
            v_side(0, bs)
            wait("rT")
            row_side(1, bt)
            wait("vb")
            v_side(1, bs)
            wait("rT")
            row_side(2, bt)
            wait("vb")
            row_side(3, bs)
            yield
            wait("rT", 2)

            def masked(dst, turned):
                blocks = dst[:].rearrange("p (a b) -> p a b", a=2)[:, :, 0:P]
                return pe.matmul(blocks, eye_b[:], later_b[:, turned], start=False, stop=True, skip_group_check=True)

            def causal_natural(dst, lhs, rhs):
                pe.matmul(dst[:, 0:P], lhs(0), rhs(0, P), start=True, stop=False, skip_group_check=True)
                pe.matmul(dst[:, P:P + S], lhs(1), rhs(0, S), start=False, stop=False, skip_group_check=True)
                return masked(dst, 0)

            def causal_turned(dst, lhs, rhs):
                pe.matmul(dst[:, 0:S], lhs(0), rhs(0, S), start=True, stop=False, skip_group_check=True)
                pe.matmul(dst[:, S:S + P], lhs(1), rhs(P, S), start=False, stop=False, skip_group_check=True)
                return masked(dst, 1)

            for n in range(ATT_HEADS):
                if n >= 2:
                    pe.wait_ge(sig["max"][c], cnt.now("max") + n - 1)
                causal_natural(by_turns[n % 2], lambda t: rT[c][0:D, n, t * P:(t + 1) * P],
                               lambda a, b: hT[c][0:D, a:b]).then_inc(sig["scores"][c], 1)
                yield
            wait("max", ATT_HEADS)
            pe.transpose(bt[0:TILES * ATT_HEADS, 0:P], nm[c][:], eye).then_inc(sig["turned"][c], 1)
            yield
            wait("max_row", 16)
            for n in range(ATT_HEADS):
                if n >= 2:
                    pe.wait_ge(sig["exp"][c], cnt.now("exp") + n - 1)
                causal_turned(by_turns[n % 2], lambda t: hT[c][:, t * P:(t + 1) * P],
                              lambda a, b: rT[c][:, n, a:b]).then_inc(sig["scores"][c], 1)
                yield
            wait("exp", ATT_HEADS)
            for half in range(2):
                if half:
                    wait("ob", 2)
                for k in range(4):
                    n, cols = 4 * half + k, slice(k * VS, (k + 1) * VS)
                    pe.matmul(bt[:, cols], pr[c][:, n, 0:P], vb[c][:, 0, n, :], start=True, stop=True)
                    pe.matmul(bs[:, cols], pr[c][:, n, P:S], vb[c][:, 0, n, :], start=True, stop=False)
                    last = pe.matmul(bs[:, cols], pr[c][:, n, S:S + P], vb[c][:, 1, n, :], start=False, stop=True)
                last.then_inc(sig["values"][c], 1)
                yield

            yield
            yield
            yield
            wait("hc", TILES)
            turn(hc[c], bs)
            wait("hT")
            natural(bt, hT[c], w("gqa_qkv"), "qkv")
            yield
            yield
            wait("parts")
            for src, dst, done in ((k4, bs, "k_turned"), (q4, bt, "q_turned")):
                for t in range(TILES):
                    last = pe.transpose(dst[:, t * P:(t + 1) * P], src[c][:, t].rearrange("p a b -> p (a b)"), eye)
                last.then_inc(sig[done][c], 1)
            yield
            wait("kT", GQA_HEADS)
            wait("qTa")
            for n in range(GQA_HEADS):
                if n >= 2:
                    pe.wait_ge(sig["max"][c], cnt.now("max") + n - 1)
                causal_natural(by_turns[n % 2], lambda t: q4T[c][:, t * P:(t + 1) * P],
                               lambda a, b: k4T[c][:, n, a:b]).then_inc(sig["scores"][c], 1)
                yield
            wait("max", GQA_HEADS)
            for t in range(TILES):
                last = pe.transpose(bt[:, t * P:(t + 1) * P], q4[c][:, t].rearrange("p a b -> p (a b)"), eye)
            last.then_inc(sig["q_turned"][c], 1)
            yield
            wait("qTb")
            for n in range(GQA_HEADS):
                if n >= 2:
                    pe.wait_ge(sig["exp"][c], cnt.now("exp") + n - 1)
                causal_turned((bs, bt)[n % 2], lambda t: k4T[c][:, n, t * P:(t + 1) * P],
                              lambda a, b: q4T[c][:, a:b]).then_inc(sig["scores"][c], 1)
                yield
            wait("exp", GQA_HEADS)
            for t in range(TILES):
                for j in range(GQA_HEADS):
                    cols = (slice(0, S), slice(P, S))[t]
                    last = pe.matmul(bs[32 * j:32 * j + 32, cols], v4[c][:, t, j // 2, :],
                                     pr[c][:, j, (0, S)[t]:(S, S + P)[t]], start=(t == 0), stop=(t == 1),
                                     tile_position=(0, 32 * j), skip_group_check=True)
            last.then_inc(sig["values"][c], 1)
            yield
            wait("oT")
            for t in range(TILES):
                last = pe.transpose(bt[:, t * P:(t + 1) * P], oT[c][:, 0, t * P:(t + 1) * P], eye)
            last.then_inc(sig["o_turned"][c], 1)
            yield
            wait("att")
            turn(att[c], bs)
            yield
            wait("hT")
            natural(bt, hT[c], w("gqa_wo"), "proj")
            yield

            def mixture(router, up, down, tiles, sel_at, bias=None):
                yield
                wait("hc", TILES)
                turn(hc[c], bs)
                wait("hT")
                natural(bt, hT[c], w(router), "logits")
                yield
                for part in range(ROUTE_STEPS):
                    yield
                wait("gates")
                for t in range(TILES):
                    last = pe.transpose(bs[:].bitcast(BF16)[0:GATE_ROWS, t * P:(t + 1) * P], gp[c][:, t, :], eye_b[:])
                last.then_inc(sig["turned"][c], 1)
                wait("gT")
                yield
                gated = len(up) == 2

                def gates_wide(i, dst):
                    pe.matmul(dst, sel_b[:, sel_at + i * P:sel_at + (i + 1) * P], gT[c][:], start=True, stop=True
                              ).then_inc(sig["wide"][c], 1)

                for i in range(tiles + 1):
                    if i > 0:
                        wait("t2")
                    if i < tiles:
                        for k, name in enumerate(up):
                            last = pe.matmul(bs[:, k * S:(k + 1) * S], w(name, i * P, (i + 1) * P), hT[c][:], start=True, stop=True)
                        last.then_inc(sig["up"][c], 1)
                        if not gated:
                            gates_wide(i, bs[:, S:2 * S])
                    if i > 0:
                        k = i - 1
                        half = k % 2
                        last = pe.matmul(bt[D * half:D * half + D, 0:S], w(down, k * D, (k + 1) * D), t2[c][:, half, :],
                                         start=(k < 2), stop=(k >= tiles - 2 and bias is None),
                                         tile_position=(0, D * half), skip_group_check=True)
                    if i < tiles:
                        if gated:
                            yield
                            wait("t1")
                            gates_wide(i, bs[:, 0:S])
                        yield
                if bias is not None:
                    for k in range(3):
                        last = pe.matmul(bt[0:D, 0:S], bias[:, k, :], gT[c][:], start=False, stop=(k == 2), skip_group_check=True)
                last.then_inc(sig["moe"][c], 1)
                yield
                wait("oT")
                for t in range(TILES):
                    last = pe.transpose(bs[:, t * P:(t + 1) * P], oT[c][:, 0, t * P:(t + 1) * P], eye)
                last.then_inc(sig["o_turned"][c], 1)

            yield from mixture("moe_router", ("moe_w1", "moe_w3"), "moe_w2", HID_TILES, 0)
            yield

            yield
            wait("xn", TILES)
            turn(xn[c], bs)
            wait("hT")
            for k, name in enumerate(("one_wq", "one_wk")):
                last = pe.matmul(bt[0:D, k * S:(k + 1) * S], w(name), hT[c][:], start=True, stop=True)
            last.then_inc(sig["row_side"][c], 1)
            natural(bs, hT[c], w("one_wv"), "v_side")
            yield
            wait("rT")
            wait("vb")
            wait("kT")
            for t in range(TILES):
                pe.matmul(by_turns[t][:, 0:S], rT[c][0:D, 0, t * P:(t + 1) * P], hT[c][0:D, :], start=True, stop=True
                          ).then_inc(sig["scores"][c], 1)
            wait("max", TILES)
            pe.transpose(bt[0:TILES, 0:P], nm[c][:, 0:TILES], eye).then_inc(sig["turned"][c], 1)
            yield
            wait("max_row", 16)
            for t in range(TILES):
                pe.matmul(by_turns[t][:, 0:S], hT[c][:, t * P:(t + 1) * P], rT[c][:, 0, :], start=True, stop=True
                          ).then_inc(sig["scores"][c], 1)
            yield
            wait("exp", TILES)
            for t in range(TILES):
                for k in range(TILES):
                    last = pe.matmul(bs[:, t * VS:(t + 1) * VS], pr[c][:, k, t * P:(t + 1) * P], vb[c][:, k, 0, :],
                                     start=(k == 0), stop=(k == 1))
            last.then_inc(sig["values"][c], 1)
            yield

            yield
            yield
            yield from mixture("gelu_router", ("gelu_w1",), "gelu_w2", EXPERTS, HID_TILES * P, bias=b2_b)
            yield

        def act_chain(eng, c):
            cnt = Counts()
            bs, bt = bank[c]
            by_turns = (bt, bs)

            def wait(name, k=1):
                eng.wait_ge(sig[name][c], cnt(name, k))

            def copy_turned(src, dst, name):
                wait("turned")
                eng.copy(dst[c][0:D, :], src[0:D, 0:S]).then_inc(sig[name][c], 1)

            for l in range(TOK_LAYERS):
                copy_turned(bs, hT, "hT")
                yield
                if l == 0:
                    wait("clear_a", 3)
                wait("qkv")
                y = bt[:, 0:TILES * 3 * D].rearrange("p (t n) -> p t n", t=TILES)
                for a, dst, sl in ((1, kn, slice(1, 6, 2)), (0, qn, slice(0, 3))):
                    for t in range(TILES):
                        slots = dst[c][:, t * TOK_HEADS:(t + 1) * TOK_HEADS, 0:SPLIT_ROWS].rearrange("p h (i k) -> p h i k", k=TOK_HD)
                        eng.copy(slots[:, :, sl], y[:, t, a * D:(a + 1) * D].rearrange("p (h o k) -> p h o k", o=1, k=TOK_HD)
                                 .to_broadcast([P, TOK_HEADS, 3, TOK_HD])).then_inc(sig["part1"][c], 1)
                eng.copy(v8[c][:, :, :, 0:TOK_HD], y[:, :, 2 * D:3 * D].rearrange("p t (h k) -> p t h k", k=TOK_HD)
                         ).then_inc(sig["v8"][c], 1)
                yield
                yield
                yield
                yield
                if l == 0:
                    wait("clear_k")
                wait("k_turned")
                for a in range(2):
                    eng.copy(kT[c][SLOT * a:SLOT * (a + 1), :, a, :],
                             bs[:].bitcast(BF16)[SLOT * a:SLOT * (a + 1), :].rearrange("p (q s) -> p q s", q=PAIRS)
                             ).then_inc(sig["kT"][c], 1)
                yield
                for n in range(TOK_HEADS):
                    yield
                for part in range(4):
                    yield
                wait("q_turned", 2)
                for half in range(2):
                    eng.copy(qTb[c][:, 2 * half:2 * half + 2, :].rearrange("p q s -> p (q s)"),
                             bs[:].bitcast(BF16)[:, half * 2 * S:(half + 1) * 2 * S]).then_inc(sig["qTb"][c], 1)
                yield
                cnt("scores", TOK_HEADS)
                for n in range(TOK_HEADS):
                    wait("scores")
                    eng.activation(pr[c][:, n, :], by_turns[n % 2][:], ACT.Exp, scale=TOK_HD ** -0.5).then_inc(sig["exp"][c], 1)
                    yield
                for half in range(2):
                    wait("values")
                    eng.copy(oT[c][:, half, :], by_turns[half][:, 0:S]).then_inc(sig["oT"][c], 1)
                yield
                yield
                yield
                copy_turned(bs, hT, "hT")
                yield
                yield
                for part in range(NORM_STEPS):
                    yield
                copy_turned(bs, hT, "hT")
                yield
                wait("ffn")
                eng.activation(hid[c].rearrange("p a b -> p (a b)"), bt[:], ACT.Relu).then_inc(sig["hid"][c], 1)
                yield
                yield
                for part in range(NORM_STEPS):
                    yield

            yield
            yield
            copy_turned(bs, hT, "hT")
            wait("clear_b", CLEAR_B)
            for i in range(4):
                wait("row_side")
                eng.copy(rT[c][0:D, 2 * i:2 * i + 2, :].rearrange("p a s -> p (a s)"), (bs if i == 3 else bt)[0:D, :]
                         ).then_inc(sig["rT"][c], 1)
            yield
            for n in range(ATT_HEADS):
                yield
            wait("turned")
            eng.copy(nmT[c][:], bt[0:TILES * ATT_HEADS, 0:P]).then_inc(sig["nmT"][c], 1)
            yield
            cnt("scores", ATT_HEADS)
            for n in range(ATT_HEADS):
                wait("scores")
                eng.activation(pr[c][:, n, 0:CAUSAL], by_turns[n % 2][:, 0:CAUSAL], ACT.Exp).then_inc(sig["exp"][c], 1)
                yield
            yield
            yield

            yield
            yield
            yield
            copy_turned(bs, hT, "hT")
            wait("qkv")
            eng.copy(v4[c][:, :, :, 0:GQA_HD],
                     bt[:, 0:S].rearrange("p (t n) -> p t n", t=TILES)[:, :, 96:128].rearrange("p t (a k) -> p t a k", k=GQA_HD)
                     ).then_inc(sig["v8"][c], 1)
            yield
            yield
            wait("clear_c")
            wait("k_turned")
            for n in range(GQA_HEADS):
                eng.copy(k4T[c][32 * n:32 * n + 32, n, :], bs[32 * n:32 * n + 32, 0:S]).then_inc(sig["kT"][c], 1)
            yield
            for n in range(GQA_HEADS):
                yield
            wait("q_turned", 2)
            eng.copy(q4T[c][:], bt[:, 0:S]).then_inc(sig["qTb"][c], 1)
            yield
            cnt("scores", GQA_HEADS)
            for n in range(GQA_HEADS):
                wait("scores")
                eng.activation(pr[c][:, n, 0:CAUSAL], (bs, bt)[n % 2][:, 0:CAUSAL], ACT.Exp, scale=GQA_HD ** -0.5
                               ).then_inc(sig["exp"][c], 1)
                yield
            cnt("values", 2)
            wait("values")
            eng.copy(oT[c][:, 0, :], bs[:, 0:S]).then_inc(sig["oT"][c], 1)
            yield
            yield
            copy_turned(bs, hT, "hT")
            yield
            yield

            def mixture(func, name, tiles, steps):
                yield
                copy_turned(bs, hT, "hT")
                yield
                for i in range(ROUTE_STEPS):
                    if i == 2:
                        wait("lg", 2)
                        eng.activation(ex[c][:], lg[c][:], ACT.Exp).then_inc(sig["ex"][c], 1)
                    yield
                wait("turned")
                eng.copy(gT[c][0:GATE_ROWS, :], bs[:].bitcast(BF16)[0:GATE_ROWS, 0:S]).then_inc(sig["gT"][c], 1)
                yield
                for i in range(tiles):
                    wait("up")
                    if steps == 1:
                        wait("wide")
                    eng.activation(act[c][:, i % 2, :], bs[:, 0:S], func).then_inc(sig[name][c], 1)
                    for step in range(steps):
                        yield
                wait("moe")
                eng.copy(oT[c][:, 0, :], bt[:, 0:S]).then_inc(sig["oT"][c], 1)
                yield

            yield from mixture(ACT.Silu, "silu", HID_TILES, 2)
            yield

            yield
            copy_turned(bs, hT, "hT")
            wait("row_side")
            eng.copy(rT[c][0:D, 0, :], bt[0:D, 0:S]).then_inc(sig["rT"][c], 1)
            cnt("v_side", TILES)
            wait("v_side")
            eng.copy(hT[c][0:D, :], bt[0:D, S:2 * S]).then_inc(sig["kT"][c], 1)
            eng.copy(vb[c][:, :, 0, 0:D], bs[:, 0:TILES * D].rearrange("p (t d) -> p t d", t=TILES)).then_inc(sig["vb"][c], 1)
            yield
            wait("turned")
            eng.copy(nmT[c][0:TILES, :], bt[0:TILES, 0:P]).then_inc(sig["nmT"][c], 1)
            yield
            cnt("scores", TILES)
            for t in range(TILES):
                wait("scores")
                eng.activation(pr[c][:, t, 0:S], by_turns[t][:, 0:S], ACT.Exp, scale=D ** -0.5).then_inc(sig["exp"][c], 1)
            yield
            yield

            yield
            yield
            cnt("wide", HID_TILES)
            yield from mixture(ACT.Gelu, "gelu", EXPERTS, 1)
            yield

        def dve_chain(dve, c, g):
            cnt = Counts()
            bs, bt = bank[c]
            by_turns = (bt, bs)

            def wait(name, k=1):
                dve.wait_ge(sig[name][c], cnt(name, k))

            def link(ins):
                ins.then_inc(sig["dve"][c], 1)
                dve.wait_ge(sig["dve"][c], cnt("dve"))

            def step(ins, name="dve"):
                ins.then_inc(sig[name][c], 1)
                value = cnt(name)
                yield
                dve.wait_ge(sig[name][c], value)

            def show(ins, name):
                ins.then_inc(sig[name][c], 1)
                dve.wait_ge(sig[name][c], cnt(name))

            def moments(src):
                for t in range(TILES):
                    dve.bn_stats(stats[c][:, t, :], src[:, t, :]).then_inc(sig["dve"][c], 1)
                dve.wait_ge(sig["dve"][c], cnt("dve", TILES))
                for t in range(TILES):
                    dve.bn_aggr(mv[c][:, t, :], stats[c][:, t, :]).then_inc(sig["mv"][c], 1)
                wait("mv", TILES)

            def normalise(src, dst, name):
                wait("rstd")
                for t in range(TILES):
                    dve.tensor_scalar(dst[:, t, :], src[:, t, :], mv[c][:, t, 0:1], rstd[c][:, t:t + 1], ALU.subtract, ALU.mult
                                      ).then_inc(sig[name][c], 1)
                wait(name, TILES)

            def moments_stepwise(src, dst, gamma, a, b):
                for t in range(TILES):
                    dve.bn_stats(stats[c][:, t, :], src[:, t, :]).then_inc(sig["dve"][c], 1)
                value = cnt("dve", TILES)
                yield
                dve.wait_ge(sig["dve"][c], value)
                for t in range(TILES):
                    dve.bn_aggr(mv[c][:, t, :], stats[c][:, t, :]).then_inc(sig["mv"][c], 1)
                value = cnt("mv", TILES)
                yield
                dve.wait_ge(sig["mv"][c], value)
                for t in range(TILES):
                    dve.scalar_tensor_tensor(dst[:, t, :], src[:, t, :], mv[c][:, t, 0:1], w(gamma, a, b), ALU.subtract, ALU.mult
                                             ).then_inc(sig["dve"][c], 1)
                cnt("dve", TILES)

            def moments_scaled(src, dst, gamma, a, b):
                moments(src)
                for t in range(TILES):
                    dve.scalar_tensor_tensor(dst[:, t, :], src[:, t, :], mv[c][:, t, 0:1], w(gamma, a, b), ALU.subtract, ALU.mult
                                             ).then_inc(sig["dve"][c], 1)
                cnt("dve", TILES)

            def normalise_scaled(src, dst, beta, a, b, name):
                dve.wait_ge(sig["dve"][c], cnt.now("dve"))
                wait("rstd")
                for t in range(TILES):
                    dve.scalar_tensor_tensor(dst[:, t, :], src[:, t, :], rstd[c][:, t:t + 1], w(beta, a, b), ALU.mult, ALU.add
                                             ).then_inc(sig[name][c], 1)
                wait(name, TILES)

            def squares(src):
                for t in range(TILES):
                    dve.tensor_tensor_reduce(s_[c][:, t, :], src[:, t, :], src[:, t, :], 1.0, 0.0, ALU.mult, ALU.add,
                                             ss[c][:, t:t + 1]).then_inc(sig["ss"][c], 1)
                wait("ss", TILES)

            def rms_scaled(src, name):
                wait("rstd")
                for t in range(TILES):
                    dve.scalar_tensor_tensor(hc[c][:, t, :], src[:, t, :], rstd[c][:, t:t + 1], w(name), ALU.mult, ALU.mult
                                             ).then_inc(sig["hc"][c], 1)
                wait("hc", TILES)

            for t in range(TILES):
                dve.tensor_tensor(h[c][:, t:t + 1, :], tokens[:, bass.ds(g * (CHAINS * TILES) + (c * TILES + t), 1), :],
                                  w("enc", t * D, (t + 1) * D).rearrange("p (t d) -> p t d", t=1), ALU.add
                                  ).then_inc(sig["h"][c], 1)
            dve.memset(kT[c], 0.0).then_inc(sig["clear_k"][c], 1)
            wait("h", TILES)

            n_heads = TILES * TOK_HEADS
            for l in range(TOK_LAYERS):
                yield
                yield
                y = bt[:, 0:TILES * 3 * D].rearrange("p (t n) -> p t n", t=TILES)
                wait("part1", 2 * TILES)
                wait("v8")
                q_slots = qn[c][:, :, 0:SPLIT_ROWS].rearrange("p h (i k) -> p h i k", k=TOK_HD)
                heads = lambda ap, o=1: ap.rearrange("p (h o k) -> p h o k", o=o, k=TOK_HD)
                for a, src, at in ((1, kn, 1), (0, qn, 0)):
                    for t in range(TILES):
                        dve.tensor_tensor(rest[c][:, a, t * D:(t + 1) * D].rearrange("p (h k) -> p h k", k=TOK_HD),
                                          y[:, t, a * D:(a + 1) * D].rearrange("p (h k) -> p h k", k=TOK_HD),
                                          src[c][:, t * TOK_HEADS:(t + 1) * TOK_HEADS, at * TOK_HD:(at + 1) * TOK_HD],
                                          ALU.subtract).then_inc(sig[("rest_q", "rest_k")[a]][c], 1)
                wait("rest_q", TILES)
                yield
                yield from step(dve.tensor_copy(q_slots[:, :, 3:5], heads(rest[c][:, 0]).to_broadcast([P, n_heads, 2, TOK_HD])))
                show(dve.tensor_tensor(q_slots[:, :, 5], rest[c][:, 0].rearrange("p (h k) -> p h k", k=TOK_HD), q_slots[:, :, 3],
                                       ALU.subtract), "q_parts")
                yield
                wait("q_turned")
                dve.tensor_copy(qTa[c][:].rearrange("p q s -> p (q s)"), bt[:].bitcast(BF16)).then_inc(sig["qTa"][c], 1)
                yield
                for n in range(TOK_HEADS):
                    wait("scores")
                    dve.tensor_reduce(nm[c][:].rearrange("p (t h) -> p t h", t=TILES)[:, :, n],
                                      by_turns[n % 2][:].rearrange("p (t s) -> p t s", t=TILES), X_AXIS, ALU.max, negate=True
                                      ).then_inc(sig["max"][c], 1)
                    yield
                wait("max", TOK_HEADS)
                yield from step(dve.tensor_copy(qn[c][:, :, SPLIT_ROWS], nm[c][:]))
                yield from step(dve.tensor_tensor(nr[c][:], nm[c][:], qn[c][:, :, SPLIT_ROWS], ALU.subtract))
                yield from step(dve.tensor_copy(qn[c][:, :, SPLIT_ROWS + 1], nr[c][:]))
                show(dve.tensor_tensor(qn[c][:, :, SPLIT_ROWS + 2], nr[c][:], qn[c][:, :, SPLIT_ROWS + 1], ALU.subtract), "max_split")
                cnt("q_turned")
                yield
                yield
                cnt("scores", TOK_HEADS)
                for n in range(TOK_HEADS):
                    yield
                yield
                wait("o_turned")
                o = bt[:].rearrange("p (n k) -> p n k", k=32)
                yield from step(dve.reciprocal(rden[c][:], o[:, :, TOK_HD]))
                show(dve.tensor_tensor(att[c][:].rearrange("p t (n k) -> p (t n) k", k=TOK_HD), o[:, :, 0:TOK_HD],
                                       rden[c][:].rearrange("p (n o) -> p n o", o=1).to_broadcast([P, n_heads, TOK_HD]),
                                       ALU.mult), "att")
                yield
                yield
                yield
                lay = (l * D, (l + 1) * D)
                wait("proj")
                yield from step(dve.tensor_tensor(s_[c][:], bt[:, 0:TILES * D].rearrange("p (t d) -> p t d", t=TILES), h[c][:], ALU.add))
                yield from moments_stepwise(s_[c], xn[c], "tok_gamma", *lay)
                yield
                normalise_scaled(xn[c], h[c], "tok_beta", *lay, "h")
                yield
                yield
                yield
                yield
                wait("proj")
                wait("hb")
                yield from step(dve.tensor_tensor(s_[c][:], bs[:, 0:TILES * D].rearrange("p (t d) -> p t d", t=TILES), s_[c][:], ALU.add))
                yield from moments_stepwise(s_[c], xn[c], "tok_gamma", *lay)
                yield
                normalise_scaled(xn[c], h[c], "tok_beta", *lay, "h")
                yield

            moments(h[c])
            yield
            normalise(h[c], xn[c], "xn")
            yield
            for t in range(TILES):
                wait("v_side")
                dve.tensor_copy(vb[c][:, t, :, 0:D], bs[:].rearrange("p (n e) -> p n e", e=D)).then_inc(sig["vb"][c], 1)
            yield
            for n in range(ATT_HEADS):
                wait("scores")
                b = by_turns[n % 2]
                dve.tensor_reduce(nm[c][:, 2 * n:2 * n + 1], b[:, 0:P], X_AXIS, ALU.max, negate=True).then_inc(sig["dve"][c], 1)
                cnt("dve")
                dve.tensor_reduce(nm[c][:, 2 * n + 1:2 * n + 2], b[:, P:P + S], X_AXIS, ALU.max, negate=True
                                  ).then_inc(sig["max"][c], 1)
                yield
            cnt("max", ATT_HEADS)
            yield

            def take(half):
                wait("values")
                for t, b in enumerate((bt, bs)):
                    o = b[:, 0:4 * VS].rearrange("p (n e) -> p n e", e=VS)
                    rd = rden[c][:, 4 * t:4 * t + 4]
                    link(dve.reciprocal(rd, o[:, :, D]))
                    dve.tensor_tensor(ob[c][:, t, 4 * half:4 * half + 4, :], o[:, :, 0:D],
                                      rd.rearrange("p (n o) -> p n o", o=1).to_broadcast([P, 4, D]), ALU.mult
                                      ).then_inc(sig["ob"][c], 1)
                cnt("ob", 2)

            cnt("scores", ATT_HEADS)
            cnt("values", 2 * TOK_LAYERS)
            for n in range(ATT_HEADS):
                yield
            take(0)
            yield
            dve.wait_ge(sig["ob"][c], cnt.now("ob"))
            take(1)
            dve.wait_ge(sig["ob"][c], cnt.now("ob"))
            link(dve.tensor_reduce(s_[c][:], ob[c][:].rearrange("p t n d -> p t d n"), X_AXIS, ALU.add))
            link(dve.tensor_tensor(h[c][:], h[c][:], s_[c][:], ALU.add))
            yield

            moments(h[c])
            yield
            normalise(h[c], xn[c], "dve")
            squares(xn[c])
            yield
            rms_scaled(xn[c], "gqa_ln1")
            yield
            yield
            wait("v8")
            y = bt[:, 0:S].rearrange("p (t n) -> p t n", t=TILES)[:, :, 0:96].rearrange("p t (n k) -> p t n k", k=GQA_HD)
            H = GQA_HD // 2
            tab = lambda name, a, b: w(name).rearrange("p (t o k) -> p t o k", t=TILES, o=1)[:, :, :, a:b].to_broadcast([P, TILES, 6, b - a])
            dve.tensor_tensor(ra[c][:], y, tab("cos", 0, GQA_HD), ALU.mult).then_inc(sig["dve"][c], 1)
            dve.tensor_tensor(rb[c][:, :, :, 0:H], y[:, :, :, H:2 * H], tab("sin", 0, H), ALU.mult).then_inc(sig["dve"][c], 1)
            dve.tensor_tensor(rb[c][:, :, :, H:2 * H], y[:, :, :, 0:H], tab("sin", H, 2 * H), ALU.mult).then_inc(sig["dve"][c], 1)
            dve.wait_ge(sig["dve"][c], cnt("dve", 3))
            dve.tensor_tensor(q4[c][:, :, :, 0:GQA_HD], ra[c][:, :, 0:4], rb[c][:, :, 0:4], ALU.add).then_inc(sig["dve"][c], 1)
            for t in range(TILES):
                src = lambda r: r[c][:, t, 4:6].rearrange("p a (o k) -> p a o k", o=1).to_broadcast([P, GQA_KV, 2, GQA_HD])
                ins = dve.tensor_tensor(k4[c][:, t, :, 0:GQA_HD].rearrange("p (a o) k -> p a o k", o=2), src(ra), src(rb), ALU.add)
                if t < TILES - 1:
                    ins.then_inc(sig["dve"][c], 1)
            dve.wait_ge(sig["dve"][c], cnt("dve", TILES))
            show(ins, "parts")
            yield
            wait("q_turned")
            show(dve.tensor_copy(q4T[c][:], bt[:, 0:S]), "qTa")
            yield
            for n in range(GQA_HEADS):
                wait("scores")
                b = by_turns[n % 2]
                dve.tensor_reduce(q4[c][:, 0, n, GQA_HD:GQA_HD + 1], b[:, 0:P], X_AXIS, ALU.max, negate=True).then_inc(sig["dve"][c], 1)
                dve.tensor_reduce(q4[c][:, 1, n, GQA_HD:GQA_HD + 1], b[:, P:P + S], X_AXIS, ALU.max, negate=True
                                  ).then_inc(sig["max"][c], 1)
                cnt("dve")
                yield
            cnt("q_turned")
            yield
            for n in range(GQA_HEADS):
                yield
            yield
            wait("o_turned")
            cnt("values")
            o = bt[:, 0:S].rearrange("p (n k) -> p n k", k=32)
            n_heads = TILES * GQA_HEADS
            link(dve.reciprocal(rden[c][:, 0:n_heads], o[:, :, GQA_HD]))
            show(dve.tensor_tensor(att[c][:].rearrange("p t (n k) -> p (t n) k", k=GQA_HD), o[:, :, 0:GQA_HD],
                                   rden[c][:, 0:n_heads].rearrange("p (n o) -> p n o", o=1).to_broadcast([P, n_heads, GQA_HD]),
                                   ALU.mult), "att")
            yield
            yield
            wait("proj")
            link(dve.tensor_tensor(xn[c][:], xn[c][:], bt[:, 0:TILES * D].rearrange("p (t d) -> p t d", t=TILES), ALU.add))
            squares(xn[c])
            yield

            def mixture(eps, tiles, gated):
                yield
                yield
                wait("logits")
                lo = bt[:, 0:TILES * EXPERTS].rearrange("p (t e) -> p t e", t=TILES)
                for t in range(TILES):
                    dve.max(top[c][:, t, :], lo[:, t, :]).then_inc(sig["dve"][c], 1)
                value = cnt("dve", TILES)
                yield
                dve.wait_ge(sig["dve"][c], value)
                first = top[c][:, :, 0:1]
                dve.tensor_tensor(lg[c][:, :, 0:EXPERTS], lo, first.to_broadcast([P, TILES, EXPERTS]), ALU.subtract
                                  ).then_inc(sig["lg"][c], 1)
                dve.tensor_tensor(lg[c][:, :, EXPERTS:EXPERTS + 2], top[c][:, :, 0:2], first.to_broadcast([P, TILES, 2]),
                                  ALU.subtract).then_inc(sig["lg"][c], 1)
                for t in range(TILES):
                    dve.max_index(idx[c][:, t, :], top[c][:, t, :], lo[:, t, :]).then_inc(sig["dve"][c], 1)
                value = cnt("dve", TILES)
                yield
                dve.wait_ge(sig["dve"][c], value)
                yield from step(dve.tensor_copy(idf[c][:], idx[c][:]))
                over = [P, TILES, 2, EXPERTS]
                yield from step(dve.tensor_tensor(
                    pick[c][:], w("iota").rearrange("p (a b e) -> p a b e", a=1, b=1).to_broadcast(over),
                    idf[c][:, :, 0:2].rearrange("p t (k e) -> p t k e", e=1).to_broadcast(over), ALU.is_equal))
                wait("ex")
                dve.tensor_reduce(sw[c][:, :, 1:2], ex[c][:, :, EXPERTS:EXPERTS + 2], X_AXIS, ALU.add).then_inc(sig["dve"][c], 1)
                if eps:
                    dve.tensor_reduce(sw[c][:, :, 0:1], ex[c][:, :, 0:EXPERTS], X_AXIS, ALU.add).then_inc(sig["dve"][c], 1)
                cnt("dve", 2 if eps else 1)
                yield from step(dve.tensor_tensor(
                    pick[c][:], pick[c][:],
                    ex[c][:, :, EXPERTS:EXPERTS + 2].rearrange("p t (k e) -> p t k e", e=1).to_broadcast(over), ALU.mult))
                if eps:
                    dve.scalar_tensor_tensor(sw[c][:, :, 2:3], sw[c][:, :, 0:1], eps, sw[c][:, :, 1:2], ALU.mult, ALU.add
                                             ).then_inc(sig["dve"][c], 1)
                    cnt("dve")
                yield from step(dve.tensor_tensor(gates[c][:], pick[c][:, :, 0, :], pick[c][:, :, 1, :], ALU.add))
                k = 2 if eps else 1
                yield from step(dve.reciprocal(sw[c][:, :, 3:4], sw[c][:, :, k:k + 1]))
                dve.tensor_tensor(gates[c][:], gates[c][:], sw[c][:, :, 3:4].to_broadcast([P, TILES, EXPERTS]), ALU.mult
                                  ).then_inc(sig["weights"][c], 1)
                yield
                yield
                yield
                for i in range(tiles):
                    if gated:
                        wait("silu")
                        dve.tensor_tensor(t1[c][:, i % 2, :], act[c][:, i % 2, :], bs[:, S:2 * S], ALU.mult
                                          ).then_inc(sig["t1"][c], 1)
                        yield
                    wait("t1" if gated else "gelu")
                    wait("wide")
                    dve.tensor_tensor(t2[c][:, i % 2, :], (t1 if gated else act)[c][:, i % 2, :],
                                      bs[:, 0:S] if gated else bs[:, S:2 * S], ALU.mult).then_inc(sig["t2"][c], 1)
                    yield
                yield
                wait("o_turned")
                o = bs[:, 0:TILES * P].rearrange("p (t n) -> p t n", t=TILES)
                link(dve.tensor_tensor(h[c][:], h[c][:], o[:, :, 0:D], ALU.add))
                show(dve.tensor_tensor(h[c][:], h[c][:], o[:, :, D:2 * D], ALU.add), "stream")

            rms_scaled(xn[c], "gqa_ln2")
            link(dve.tensor_tensor(h[c][:], h[c][:], xn[c][:], ALU.add))
            yield from mixture(1e-9, HID_TILES, gated=True)
            moments(h[c])
            yield

            normalise(h[c], xn[c], "xn")
            yield
            yield
            cnt("scores", GQA_HEADS)
            for t in range(TILES):
                wait("scores")
                dve.tensor_reduce(nm[c][:, t:t + 1], by_turns[t][:, 0:S], X_AXIS, ALU.max, negate=True).then_inc(sig["max"][c], 1)
            yield
            yield
            wait("values")
            o = bs[:, 0:TILES * VS].rearrange("p (t e) -> p t e", e=VS)
            link(dve.reciprocal(rden[c][:, 0:TILES], o[:, :, D]))
            for t in range(TILES):
                dve.scalar_tensor_tensor(h[c][:, t, :], o[:, t, 0:D], rden[c][:, t:t + 1], h[c][:, t, :], ALU.mult, ALU.add
                                         ).then_inc(sig["dve"][c], 1)
            dve.wait_ge(sig["dve"][c], cnt("dve", TILES))
            moments(h[c])
            yield

            normalise(h[c], xn[c], "dve")
            moments_scaled(xn[c], s_[c], "gelu_gamma", 0, D)
            yield
            normalise_scaled(s_[c], hc[c], "gelu_beta", 0, D, "hc")
            yield
            yield from mixture(0.0, EXPERTS, gated=False)
            yield

        def pool_chain(pool, c):
            cnt = Counts()

            def wait(name, k=1):
                pool.wait_ge(sig[name][c], cnt(name, k))

            def link(ins):
                ins.then_inc(sig["pool"][c], 1)
                pool.wait_ge(sig["pool"][c], cnt("pool"))

            def inv_sqrt(src, scale, eps):
                link(pool.tensor_scalar(var[c][:], src, scale, eps, ALU.mult, ALU.add))
                pool.tensor_tensor(rstd[c][:], var[c][:], minus_half[:], ALU.pow).then_inc(sig["rstd"][c], 1)

            def norm(eps):
                wait("mv", TILES)
                inv_sqrt(mv[c][:, :, 1], 1.0, eps)

            def rms():
                wait("ss", TILES)
                inv_sqrt(ss[c][:], 1.0 / D, 1e-6)

            n_heads = TILES * TOK_HEADS
            cnt("h", TILES)
            pool.memset(qn[c], 0.0).then_inc(sig["clear_a"][c], 1)
            pool.memset(kn[c][:, :, ROWS:SLOT], 0.0).then_inc(sig["clear_a"][c], 1)
            pool.memset(kn[c][:, :, SPLIT_ROWS:ROWS], 1.0).then_inc(sig["clear_a"][c], 1)
            for l in range(TOK_LAYERS):
                yield
                yield
                wait("rest_k", TILES)
                k_slots = kn[c][:, :, 0:SPLIT_ROWS].rearrange("p h (i k) -> p h i k", k=TOK_HD)
                rest_k = rest[c][:, 1].rearrange("p (h o k) -> p h o k", o=1, k=TOK_HD)
                pool.tensor_copy(k_slots[:, :, 2:5:2], rest_k.to_broadcast([P, n_heads, 2, TOK_HD])).then_inc(sig["k_parts"][c], 1)
                wait("k_parts")
                pool.tensor_tensor(k_slots[:, :, 0], rest_k[:, :, 0], k_slots[:, :, 2], ALU.subtract).then_inc(sig["k_parts"][c], 1)
                cnt("k_parts")
                yield
                yield
                yield
                yield
                for n in range(TOK_HEADS + 5 + TOK_HEADS):
                    yield
                yield
                yield
                yield
                if l < TOK_LAYERS - 1:
                    wait("q_turned", 2)
                    pool.memset(qn[c][:, :, SPLIT_ROWS:ROWS], 0.0).then_inc(sig["max_clear"][c], 1)
                else:
                    pool.wait_ge(sig["values"][c], 2 * TOK_LAYERS)
                    pool.memset(rT[c][:], 0.0).then_inc(sig["clear_b"][c], 1)
                    for dst, value in ((vb[c][:, :, :, D:VS], 1.0), (q4[c][:], 0.0),
                                       (k4[c][:, :, :, GQA_HD + 1:32], 0.0), (k4[c][:, :, :, GQA_HD:GQA_HD + 1], 1.0),
                                       (v4[c][:, :, :, GQA_HD + 1:32], 0.0), (v4[c][:, :, :, GQA_HD:GQA_HD + 1], 1.0)):
                        pool.memset(dst, value).then_inc(sig["clear_b"][c], 1)
                yield
                yield
                yield
                yield
                yield
                norm(1e-3)
                yield
                wait("h", TILES)
                v = w("tok_b2", l * D, (l + 1) * D).rearrange("p (o d) -> p o d", o=1).to_broadcast([P, TILES, D])
                pool.tensor_tensor(s_[c][:], h[c][:], v, ALU.add).then_inc(sig["hb"][c], 1)
                cnt("h", TILES)
                yield
                yield
                yield
                yield
                yield
                yield
                yield
                norm(1e-3)
                yield
                yield
            norm(1e-5)
            yield
            yield
            yield
            for n in range(ATT_HEADS):
                yield
            yield
            for n in range(ATT_HEADS):
                yield
            yield
            yield
            pool.wait_ge(sig["values"][c], 2 * TOK_LAYERS + 2)
            pool.memset(k4T[c], 0.0).then_inc(sig["clear_c"][c], 1)
            norm(1e-5)
            yield
            rms()
            yield
            yield
            yield
            yield
            yield
            for n in range(2 * GQA_HEADS + 1):
                yield
            yield
            yield
            yield
            rms()
            yield
            def mixture(steps):
                yield
                yield
                for i in range(ROUTE_STEPS - 1):
                    yield
                wait("weights")
                part = [gp[c][:, :, k * EXPERTS:(k + 1) * EXPERTS] for k in range(3)]
                link(pool.tensor_copy(part[0], gates[c][:]))
                link(pool.tensor_tensor(gates[c][:], gates[c][:], part[0], ALU.subtract))
                link(pool.tensor_copy(part[1], gates[c][:]))
                pool.tensor_tensor(part[2], gates[c][:], part[1], ALU.subtract).then_inc(sig["gates"][c], 1)
                yield
                for i in range(steps):
                    yield

            yield from mixture(1 + 2 * HID_TILES + 1)
            norm(1e-5)
            yield
            for i in range(4):
                yield
            norm(1e-5)
            yield
            norm(1e-5)
            yield
            yield
            yield from mixture(1 + EXPERTS + 1)
            yield

        def sp_chain(sp, c, g):
            before = len(STEPS) - len(GELU_STEPS) - len(ONE_STEPS)
            row_at = {TOK_LAYERS * len(TOK_STEPS) + 3 + ATT_HEADS: ATT_HEADS, before + 2: 1}
            for i in range(len(STEPS)):
                if i in row_at:
                    sp.wait_ge(sig["nmT"][c], FIRST["nmT"] + 1 + (i == before + 2))
                    sp.dma_start(rT[c][D:VS, 0:row_at[i], :].rearrange("o n (t p) -> o (n t) p", p=P),
                                 nmT[c][0:row_at[i] * TILES, :]).then_inc(sig["max_row"][c], 16)
                yield
            sp.wait_ge(sig["stream"][c], FIRST["stream"] + 2)
            sp.dma_start(out_v[:, bass.ds(g * (CHAINS * TILES) + c * TILES, TILES), :], h[c][:]).then_inc(sig["stored"][c], 16)

        with nc.Fori(0, BATCH // CHAINS) as g:
            with nc.Block() as block:
                @block.tensor
                def _(pe):
                    in_turns([pe_chain(pe, c) for c in range(CHAINS)], LAG, STEPS)

                @block.scalar
                def _(eng):
                    in_turns([act_chain(eng, c) for c in range(CHAINS)], LAG, STEPS)

                @block.vector
                def _(dve):
                    in_turns([dve_chain(dve, c, g) for c in range(CHAINS)], LAG, STEPS)

                @block.gpsimd
                def _(pool):
                    in_turns([pool_chain(pool, c) for c in range(CHAINS)], LAG, STEPS)

                @block.sync
                def _(sp):
                    in_turns([sp_chain(sp, c, g) for c in range(CHAINS)], LAG, STEPS)
                    for c in range(CHAINS):
                        sp.wait_ge(sig["stored"][c], FIRST["stored"] + 16)

            with nc.Block() as block:
                @block.sync
                def _(sp):
                    sp.sem_clear(sig.numbers())


def kernel(**inputs):
    import concourse.bacc as _bacc
    from concourse.bass_utils import run_bass_kernel_spmd as _run

    nc = _bacc.Bacc("TRN2", target_bir_lowering=False, num_devices=1)
    laid = {k: np.ascontiguousarray(v) for k, v in pack(inputs).items()}
    shapes = {k: v.shape for k, v in laid.items()}
    arrays, packed = {}, {}
    for parts in sorted({p for p, _ in shapes.values()}):
        a = np.concatenate([v for v in laid.values() if v.shape[0] == parts], axis=1)
        arrays[f"packed{parts}"] = a
        packed[parts] = nc.dram_tensor(f"packed{parts}", a.shape, F32, kind="ExternalInput").ap()
    arrays["x"] = np.ascontiguousarray(np.asarray(inputs["x"]).reshape(BATCH * TILES, P).T)
    arrays["table"] = np.ascontiguousarray(inputs["L0_tok_emb"])
    x = nc.dram_tensor("x", arrays["x"].shape, I32, kind="ExternalInput").ap()
    table = nc.dram_tensor("table", arrays["table"].shape, F32, kind="ExternalInput").ap()
    out = nc.dram_tensor("out", (BATCH, S, D), F32, kind="ExternalOutput").ap()
    tower(nc, x, table, packed, shapes, out)
    r = _run(nc, [arrays], core_ids=[0])
    return r.results[0]["out"]
```
